# Optimizing a Trainium2 kernel written in Bass

```python
import numpy as np
import jax
import jax.numpy as jnp

def _softmax(x, axis=-1):
    return jax.nn.softmax(x, axis=axis)

def _gelu(x):
    return jax.nn.gelu(x, approximate=True)

def _silu(x):
    return jax.nn.silu(x)

def _sigmoid(x):
    return jax.nn.sigmoid(x)

def _layernorm(x, axis=-1, eps=1e-05):
    m = jnp.mean(x, axis=axis, keepdims=True)
    v = jnp.var(x, axis=axis, keepdims=True)
    return (x - m) / jnp.sqrt(v + eps)

def _scatter_add(tgt, idx, src, axis=0):
    return tgt.at[idx].add(src)

def _segment_sum(src, seg, n):
    return jax.ops.segment_sum(src, seg, n)
kernel_name = 'mk_gnn_ffn_d2_gnn_r8_3aae04'

def setup_inputs(seed: int=0):
    np.random.seed(seed)
    _w = jnp.asarray

    def _rec_inputs():
        import jax
        import jax.numpy as jnp
        _gk = jax.random.key(seed)
        x = -8.776e-05 + 1 * jax.random.normal(jax.random.fold_in(_gk, 1), (2500, 256), jnp.float32)
        src = jax.random.randint(jax.random.fold_in(_gk, 2), (40000,), 0, 2500, jnp.int32)
        dst = jax.random.randint(jax.random.fold_in(_gk, 3), (40000,), 0, 2500, jnp.int32)
        _o = jnp.argsort(dst, stable=True)
        src = src[_o]
        dst = dst[_o]
        edge_type_8 = jax.random.randint(jax.random.fold_in(_gk, 12), (40000,), 0, 8, jnp.int32)
        return (x, src, dst, edge_type_8)
    x, src, dst, edge_type_8 = _rec_inputs()

    def _L0_gnn_setup():
        import jax, jax.numpy as jnp
        import numpy as np
        N_NODES = 2500
        N_EDGES = 40000
        D = 256
        R = 8

        def _xavier(key, shape):
            fan_in, fan_out = (shape[-2], shape[-1])
            bound = float(np.sqrt(6.0 / (fan_in + fan_out)))
            return jax.random.uniform(key, shape, jnp.float32, -bound, bound)

        def _rgcn_layer(x, W, self_w, b, src, dst, edge_type, num_nodes):
            xW = jnp.einsum('ni,rio->rno', x, W)
            msg = xW[edge_type, src]
            agg = jax.ops.segment_sum(msg, dst, num_segments=num_nodes)
            return agg + x @ self_w + b
        key = jax.random.key(seed)
        ks = jax.random.split(key, 10)
        x = jax.random.normal(ks[0], (N_NODES, D), jnp.float32)
        edge_index = jax.random.randint(ks[1], (2, N_EDGES), 0, N_NODES)
        edge_type = jax.random.randint(ks[2], (N_EDGES,), 0, R)
        W1 = _xavier(ks[3], (R, D, D))
        self_w1 = _xavier(ks[4], (D, D))
        b1 = jnp.zeros((D,), jnp.float32)
        W2 = _xavier(ks[5], (R, D, D))
        self_w2 = _xavier(ks[6], (D, D))
        b2 = jnp.zeros((D,), jnp.float32)
        return {'x': x, 'W1': W1, 'self_w1': self_w1, 'b1': b1, 'W2': W2, 'self_w2': self_w2, 'b2': b2, 'edge_index': edge_index, 'edge_type': edge_type}
    _L0_gnn_all = _L0_gnn_setup()
    _L0_gnn_in = {k: v for k, v in _L0_gnn_all.items() if k in ('W1', 'self_w1', 'b1', 'W2', 'self_w2', 'b2')}
    del _L0_gnn_all

    def _L0_ffn_setup():
        import jax, jax.numpy as jnp
        import numpy as np
        B, S, D, H, E, K = (8, 1024, 256, 1024, 8, 2)
        key = jax.random.key(seed)
        ks = jax.random.split(key, 7)
        s_in = 1.0 / np.sqrt(D)
        s_hid = 1.0 / np.sqrt(H)
        return {'x': jax.random.normal(ks[0], (B, S, D), dtype=jnp.float32), 'Wg': jax.random.uniform(ks[1], (E, D), jnp.float32, -s_in, s_in), 'bg': jax.random.uniform(ks[2], (E,), jnp.float32, -s_in, s_in), 'W1': jax.random.uniform(ks[3], (E, H, D), jnp.float32, -s_in, s_in), 'b1': jax.random.uniform(ks[4], (E, H), jnp.float32, -s_in, s_in), 'W2': jax.random.uniform(ks[5], (E, D, H), jnp.float32, -s_hid, s_hid), 'b2': jax.random.uniform(ks[6], (E, D), jnp.float32, -s_hid, s_hid)}
    _L0_ffn_all = _L0_ffn_setup()
    _L0_ffn_in = {k: v for k, v in _L0_ffn_all.items() if k in ('Wg', 'bg', 'W1', 'b1', 'W2', 'b2')}
    del _L0_ffn_all

    def _L1_gnn_setup():
        import jax, jax.numpy as jnp
        import numpy as np
        N_NODES = 12500
        N_EDGES = 200000
        D_IN = 256
        HID = 256

        def _gcn_layer(h_in, W, b, src, dst, norm, deg_inv, n):
            h = h_in @ W
            msg = h[src] * norm[:, None]
            agg = jax.ops.segment_sum(msg, dst, num_segments=n)
            return agg + h * deg_inv[:, None] + b
        key = jax.random.key(seed)
        ks = jax.random.split(key, 12)
        x = jax.random.normal(ks[0], (N_NODES, D_IN), dtype=jnp.float32)
        edge_index = jax.random.randint(ks[1], (2, N_EDGES), 0, N_NODES, dtype=jnp.int32)

        def lin(k, fan_in, fan_out):
            s = 1.0 / np.sqrt(fan_in)
            kw, kb = jax.random.split(k)
            W = jax.random.uniform(kw, (fan_in, fan_out), jnp.float32, -s, s)
            b = jax.random.uniform(kb, (fan_out,), jnp.float32, -s, s)
            return (W, b)
        W1, b1 = lin(ks[2], D_IN, HID)
        W2, b2 = lin(ks[3], HID, HID)
        W3, b3 = lin(ks[4], HID, HID // 2)
        Wp, bp = lin(ks[5], HID // 2, D_IN)
        return {'x': x, 'edge_index': edge_index, 'W1': W1, 'b1': b1, 'W2': W2, 'b2': b2, 'W3': W3, 'b3': b3, 'Wp': Wp, 'bp': bp}
    _L1_gnn_all = _L1_gnn_setup()
    _L1_gnn_in = {k: v for k, v in _L1_gnn_all.items() if k in ('W1', 'b1', 'W2', 'b2', 'W3', 'b3', 'Wp', 'bp')}
    del _L1_gnn_all

    def _L1_ffn_setup():
        import jax, jax.numpy as jnp
        import numpy as np
        TOP_K = 2
        LN_EPS = 1e-05
        key = jax.random.key(seed)
        ks = jax.random.split(key, 8)
        B, S, D, E, H = (16, 1024, 256, 8, 1024)
        x = jax.random.normal(ks[0], (B, S, D), dtype=jnp.float32)
        Wr = jax.random.normal(ks[1], (D, E), dtype=jnp.float32) * 0.1
        br = jnp.zeros((E,), dtype=jnp.float32)
        ln_g = jnp.ones((E, D), dtype=jnp.float32)
        ln_b = jnp.zeros((E, D), dtype=jnp.float32)
        W1 = jax.random.normal(ks[2], (E, D, H), dtype=jnp.float32) * (1.0 / np.sqrt(D))
        b1 = jnp.zeros((E, H), dtype=jnp.float32)
        W2 = jax.random.normal(ks[3], (E, H, D), dtype=jnp.float32) * (1.0 / np.sqrt(H))
        b2 = jnp.zeros((E, D), dtype=jnp.float32)
        return {'x': x, 'Wr': Wr, 'br': br, 'ln_g': ln_g, 'ln_b': ln_b, 'W1': W1, 'b1': b1, 'W2': W2, 'b2': b2}
    _L1_ffn_all = _L1_ffn_setup()
    _L1_ffn_in = {k: v for k, v in _L1_ffn_all.items() if k in ('Wr', 'br', 'ln_g', 'ln_b', 'W1', 'b1', 'W2', 'b2')}
    del _L1_ffn_all
    return {'x': x, 'src': src, 'dst': dst, 'edge_type_8': edge_type_8, 'L0_gnn_W1': _L0_gnn_in['W1'], 'L0_gnn_self_w1': _L0_gnn_in['self_w1'], 'L0_gnn_b1': _L0_gnn_in['b1'], 'L0_gnn_W2': _L0_gnn_in['W2'], 'L0_gnn_self_w2': _L0_gnn_in['self_w2'], 'L0_gnn_b2': _L0_gnn_in['b2'], 'L0_ffn_Wg': _L0_ffn_in['Wg'], 'L0_ffn_bg': _L0_ffn_in['bg'], 'L0_ffn_W1': _L0_ffn_in['W1'], 'L0_ffn_b1': _L0_ffn_in['b1'], 'L0_ffn_W2': _L0_ffn_in['W2'], 'L0_ffn_b2': _L0_ffn_in['b2'], 'L1_gnn_W1': _L1_gnn_in['W1'], 'L1_gnn_b1': _L1_gnn_in['b1'], 'L1_gnn_W2': _L1_gnn_in['W2'], 'L1_gnn_b2': _L1_gnn_in['b2'], 'L1_gnn_W3': _L1_gnn_in['W3'], 'L1_gnn_b3': _L1_gnn_in['b3'], 'L1_gnn_Wp': _L1_gnn_in['Wp'], 'L1_gnn_bp': _L1_gnn_in['bp'], 'L1_ffn_Wr': _L1_ffn_in['Wr'], 'L1_ffn_br': _L1_ffn_in['br'], 'L1_ffn_ln_g': _L1_ffn_in['ln_g'], 'L1_ffn_ln_b': _L1_ffn_in['ln_b'], 'L1_ffn_W1': _L1_ffn_in['W1'], 'L1_ffn_b1': _L1_ffn_in['b1'], 'L1_ffn_W2': _L1_ffn_in['W2'], 'L1_ffn_b2': _L1_ffn_in['b2']}

def reference(x, src, dst, edge_type_8, L0_gnn_W1, L0_gnn_self_w1, L0_gnn_b1, L0_gnn_W2, L0_gnn_self_w2, L0_gnn_b2, L0_ffn_Wg, L0_ffn_bg, L0_ffn_W1, L0_ffn_b1, L0_ffn_W2, L0_ffn_b2, L1_gnn_W1, L1_gnn_b1, L1_gnn_W2, L1_gnn_b2, L1_gnn_W3, L1_gnn_b3, L1_gnn_Wp, L1_gnn_bp, L1_ffn_Wr, L1_ffn_br, L1_ffn_ln_g, L1_ffn_ln_b, L1_ffn_W1, L1_ffn_b1, L1_ffn_W2, L1_ffn_b2):
    import jax
    import jax.numpy as jnp

    def _L0_gnn_ref(x, W1, self_w1, b1, W2, self_w2, b2, edge_index, edge_type):
        import jax, jax.numpy as jnp
        import numpy as np
        N_NODES = 2500
        N_EDGES = 40000
        D = 256
        R = 8

        def _xavier(key, shape):
            fan_in, fan_out = (shape[-2], shape[-1])
            bound = float(np.sqrt(6.0 / (fan_in + fan_out)))
            return jax.random.uniform(key, shape, jnp.float32, -bound, bound)

        def _rgcn_layer(x, W, self_w, b, src, dst, edge_type, num_nodes):
            xW = jnp.einsum('ni,rio->rno', x, W)
            msg = xW[edge_type, src]
            agg = jax.ops.segment_sum(msg, dst, num_segments=num_nodes)
            return agg + x @ self_w + b
        src, dst = (edge_index[0], edge_index[1])
        h = _rgcn_layer(x, W1, self_w1, b1, src, dst, edge_type, N_NODES)
        h = jax.nn.relu(h)
        out = _rgcn_layer(h, W2, self_w2, b2, src, dst, edge_type, N_NODES)
        return out

    def _L0_ffn_ref(x, Wg, bg, W1, b1, W2, b2):
        import jax, jax.numpy as jnp
        import numpy as np
        B, S, D, H, E, K = (8, 1024, 256, 1024, 8, 2)
        gate_scores = jnp.einsum('bsd,ed->bse', x, Wg) + bg
        topk_scores, topk_idx = jax.lax.top_k(gate_scores, K)
        topk_probs = jax.nn.softmax(topk_scores, axis=-1)
        combine = jnp.sum(topk_probs[..., None] * jax.nn.one_hot(topk_idx, E, dtype=x.dtype), axis=-2)
        out = jnp.zeros_like(x)
        for e in range(E):
            h = jax.nn.relu(jnp.einsum('bsd,hd->bsh', x, W1[e]) + b1[e])
            y = jnp.einsum('bsh,dh->bsd', h, W2[e]) + b2[e]
            out = out + combine[..., e:e + 1] * y
        return out

    def _L1_gnn_ref(x, edge_index, W1, b1, W2, b2, W3, b3, Wp, bp):
        import jax, jax.numpy as jnp
        import numpy as np
        N_NODES = 12500
        N_EDGES = 200000
        D_IN = 256
        HID = 256

        def _gcn_layer(h_in, W, b, src, dst, norm, deg_inv, n):
            h = h_in @ W
            msg = h[src] * norm[:, None]
            agg = jax.ops.segment_sum(msg, dst, num_segments=n)
            return agg + h * deg_inv[:, None] + b
        n = x.shape[0]
        src, dst = (edge_index[0], edge_index[1])
        deg = jax.ops.segment_sum(jnp.ones(src.shape[0], x.dtype), dst, num_segments=n) + 1.0
        dinv_sqrt = jax.lax.rsqrt(deg)
        norm = dinv_sqrt[src] * dinv_sqrt[dst]
        deg_inv = 1.0 / deg
        h = jax.nn.relu(_gcn_layer(x, W1, b1, src, dst, norm, deg_inv, n))
        h = jax.nn.relu(_gcn_layer(h, W2, b2, src, dst, norm, deg_inv, n))
        h = jax.nn.relu(_gcn_layer(h, W3, b3, src, dst, norm, deg_inv, n))
        return h @ Wp + bp

    def _L1_ffn_ref(x, Wr, br, ln_g, ln_b, W1, b1, W2, b2):
        import jax, jax.numpy as jnp
        import numpy as np
        TOP_K = 2
        LN_EPS = 1e-05
        B, S, D = x.shape
        N = B * S
        xt = x.reshape(N, D)
        logits = xt @ Wr + br
        probs = jax.nn.softmax(logits, axis=-1)
        top_p, top_idx = jax.lax.top_k(probs, TOP_K)
        weights = top_p / top_p.sum(axis=-1, keepdims=True)
        mu = xt.mean(axis=-1, keepdims=True)
        var = ((xt - mu) ** 2).mean(axis=-1, keepdims=True)
        xn = (xt - mu) * jax.lax.rsqrt(var + LN_EPS)
        xe = xn[None, :, :] * ln_g[:, None, :] + ln_b[:, None, :]
        h = jax.nn.gelu(jnp.einsum('end,edh->enh', xe, W1) + b1[:, None, :], approximate=False)
        y = jnp.einsum('enh,ehd->end', h, W2) + b2[:, None, :]
        y_tok = jnp.transpose(y, (1, 0, 2))
        sel = jnp.take_along_axis(y_tok, top_idx[:, :, None], axis=1)
        out = (weights[:, :, None] * sel).sum(axis=1)
        return out.reshape(B, S, D)
    edge_index = jnp.stack([src, dst])
    x = x + _L0_gnn_ref(_layernorm(x, axis=-1), L0_gnn_W1, L0_gnn_self_w1, L0_gnn_b1, L0_gnn_W2, L0_gnn_self_w2, L0_gnn_b2, edge_index, edge_type_8)
    x = x + _L0_ffn_ref(_layernorm(x, axis=-1)[None], L0_ffn_Wg, L0_ffn_bg, L0_ffn_W1, L0_ffn_b1, L0_ffn_W2, L0_ffn_b2)[0]
    x = x + _L1_gnn_ref(_layernorm(x, axis=-1), edge_index, L1_gnn_W1, L1_gnn_b1, L1_gnn_W2, L1_gnn_b2, L1_gnn_W3, L1_gnn_b3, L1_gnn_Wp, L1_gnn_bp)
    x = x + _L1_ffn_ref(_layernorm(x, axis=-1)[None], L1_ffn_Wr, L1_ffn_br, L1_ffn_ln_g, L1_ffn_ln_b, L1_ffn_W1, L1_ffn_b1, L1_ffn_W2, L1_ffn_b2)[0]
    return x

_drawn_inputs = setup_inputs


def setup_inputs(seed=0):
    import zlib

    import numpy as np

    out = dict(_drawn_inputs(seed))
    spreads = {'L0_gnn_b1': (0.0, 0.285),
     'L0_gnn_b2': (0.0, 0.8),
     'L1_ffn_br': (0.0, 2.0),
     'L1_ffn_ln_g': (1.0, 0.6),
     'L1_ffn_ln_b': (0.0, 2.0),
     'L1_ffn_b1': (0.0, 2.0),
     'L1_ffn_b2': (0.0, 2.0)}
    factors = {'L0_ffn_Wg': 5.254,
     'L0_ffn_bg': 8.0,
     'L0_ffn_W1': 6.145,
     'L0_ffn_b1': 23.971,
     'L0_ffn_W2': 4.933,
     'L0_ffn_b2': 60.059,
     'L1_gnn_W1': 8.0,
     'L1_gnn_b1': 8.0,
     'L1_gnn_W2': 8.0,
     'L1_gnn_b2': 8.0,
     'L1_gnn_W3': 8.0,
     'L1_gnn_b3': 56.63,
     'L1_gnn_Wp': 8.0,
     'L1_gnn_bp': 64.0,
     'L1_ffn_Wr': 6.467,
     'L1_ffn_W1': 8.0,
     'L1_ffn_W2': 8.0}
    for name, (base, spread) in spreads.items():
        noise = np.random.default_rng([zlib.crc32(name.encode()), seed]).standard_normal(out[name].shape)
        drawn = base * np.exp(spread * noise) if base else spread * noise
        out[name] = jnp.asarray(drawn.astype(out[name].dtype))
    for name, factor in factors.items():
        out[name] = (out[name] * factor).astype(out[name].dtype)
    return out
```

```python
from contextlib import ExitStack, contextmanager

import concourse.bass as bass
from concourse import mybir

F32 = mybir.dt.float32
U32 = mybir.dt.uint32
I32 = mybir.dt.int32
ALU = mybir.AluOpType
ACT = mybir.ActivationFunctionType
AX = mybir.AxisListType

P = 128
NODES = 2500
D = 256
KD = D // P
TILES = -(-NODES // P)
NPAD = TILES * P
LAST = NODES - (TILES - 1) * P
EDGES = 40000
ETILES = -(-EDGES // P)
EFULL = EDGES // P
EREST = EDGES - EFULL * P
ECH = -(-ETILES // P)
ELASTCH = ETILES - (ECH - 1) * P
REL = 8
GSLOTS = 8
PAIRS = -(-(ETILES + TILES - 1) // GSLOTS) * GSLOTS
ACCW = D + 1
E = 8
H = 1024
HC = H // P
HB = H // 512
TOPK = 2
MTILES = (NPAD * TOPK + E * (P - 1)) // P
MTILES += MTILES % 2
SLOTS = MTILES * P
W1E = KD * H
W2E = HC * D
EPS = 1e-5
NEG = -3.0e38
SET = 44


def later(i):
    return not (isinstance(i, int) and i == 0)


class Chain:

    def __init__(self, eng, sem, base=0):
        self.eng, self.sem, self.base, self.n = eng, sem, base, 0

    def __call__(self, ins):
        ins.then_inc(self.sem, 1)
        self.n += 1
        self.eng.wait_ge(self.sem, self.base + self.n)


class Count:

    def __init__(self, sem):
        self.sem, self.base = sem, 0


def build(nc, a, out):
    with ExitStack() as ctx:
        Program(nc, a, out, ctx).run()


class Program:
    def __init__(self, nc, a, out, ctx):
        self.nc, self.a, self.out = nc, a, out

        def sb(name, shape, dt=F32):
            return ctx.enter_context(nc.sbuf_tensor(name, shape, dt))

        self.x = sb("x_all", [P, TILES * D])
        self.acc = sb("acc", [P, TILES * ACCW])
        self.big = sb("big", [P, E * (W1E + W2E)])
        self.w1 = self.big[:, 0:E * W1E]
        self.w2 = self.big[:, E * W1E:E * (W1E + W2E)]
        self.wgnn = self.big[:, 0:KD * REL * D]
        self.wself = self.big[:, KD * REL * D:KD * (REL + 1) * D]
        at = KD * (REL + 1) * D
        self.stage = [self.big[:, at + s * REL * D:at + (s + 1) * REL * D] for s in range(2)]
        self.wsmall = sb("w_small", [P, KD * D])
        self.wgate = sb("w_gate", [P, KD * E])
        self.ident = sb("ident", [P, P])
        self.tri = sb("tri", [P, P])
        self.ones = sb("ones", [P, P])
        self.iota = sb("iota", [P, PAIRS])
        self.gidx = [sb("gidx_relation", [P, PAIRS]), sb("gidx_node", [P, PAIRS])]
        self.rel = sb("dst_in_bucket", [P, PAIRS])
        self.bucket = sb("bucket_of_pair", [1, PAIRS], I32)
        self.dinv = sb("dinv", [P, TILES])
        self.bias = sb("bias_row", [P, D])
        self.hn = [sb(f"hn{s}", [P, D]) for s in range(2)]
        self.hT = [sb(f"hT{s}", [P, D]) for s in range(2)]
        self.stats = sb("stats", [P, TILES * 6])
        self.mv = sb("mean_var", [P, TILES * 2])
        self.rstd = sb("rstd", [P, TILES])
        self.r2, self.r3 = sb("root_of", [P, TILES]), sb("root", [P, TILES])
        self.scratch = sb("scratch", [P, 2048])
        self.wcomb = sb("w_comb", [P, 2 * TILES])
        self.spos = sb("slot_pos", [P, 2 * TILES], U32)
        self.texp = sb("tile_expert", [1, MTILES], I32)
        self.slots = sb("slots", [P, max(GSLOTS * (ACCW + P) * 1, 2 * 2 * D + 2 * (H + D))])
        self.rowbuf = [self.slots[:, s * ACCW:(s + 1) * ACCW] for s in range(GSLOTS)]
        at = GSLOTS * ACCW
        self.onehots = self.slots[:, at:at + GSLOTS * P]
        self.idx = [sb(f"idx{s}", [P, 1], U32) for s in range(GSLOTS)]
        self.iota_e = sb("iota_e", [P, TILES * E])
        self.ps = [ctx.enter_context(nc.psum_tensor(f"ps{b}", [P, 512], F32)) for b in range(8)]

        self.gate = ctx.enter_context(nc.semaphore("gate"))
        self.experts_loaded = ctx.enter_context(nc.semaphore("experts_loaded"))
        self.gathered = [Count(ctx.enter_context(nc.semaphore(f"gathered{s}"))) for s in range(GSLOTS)]
        self.y_stored = [Count(ctx.enter_context(nc.semaphore(f"y_stored{s}"))) for s in range(2)]
        self.sent = Count(ctx.enter_context(nc.semaphore("sent")))
        self.sets = [[ctx.enter_context(nc.semaphore(f"set{k}_{n}")) for n in range(SET)] for k in range(2)]
        self.turn = 0

        def dram(name, shape):
            return nc.dram_tensor(name, shape, F32, kind="Internal").ap()

        self.tab_rel = dram("tab_rel", [NPAD * REL, D])
        self.tab_node = dram("tab_node", [NPAD, D])
        self.tab_half = dram("tab_half", [NPAD, D // 2])
        self.xd = dram("x_dispatched", [SLOTS, D])
        self.yd = dram("y_dispatched", [SLOTS, D])

    @contextmanager
    def stage_block(self):
        own, other = self.sets[self.turn], self.sets[1 - self.turn]
        self.turn = 1 - self.turn
        free = iter(own)
        with self.nc.Block() as block:
            @block.sync
            def _(sp):
                sp.sem_clear(range(other[0].num, other[-1].num + 1))

            yield block, lambda *names: [next(free) for _ in names] if len(names) != 1 else next(free)

    def acc_tile(self, i, width=D):
        return self.acc[:, bass.ds(i * ACCW, width)]

    def x_tile(self, i):
        return self.x[:, bass.ds(i * D, D)]

    def run(self):
        a = self.a
        self.constants()
        self.edge_pairs()
        self.load(self.wgnn.rearrange("p (k r o) -> p k r o", k=KD, r=REL), a["L0_gnn_W1"].rearrange("r (k p) o -> p k r o", p=P), self.wself, a["L0_gnn_self_w1"])
        self.statistics()
        self.transform(self.prep_norm, self.relation_groups(), self.tab_rel)
        self.aggregate(self.tab_rel, self.gidx[0], D, count=True)
        self.degrees()
        self.load(self.wgnn.rearrange("p (k r o) -> p k r o", k=KD, r=REL), a["L0_gnn_W2"].rearrange("r (k p) o -> p k r o", p=P), self.wself, a["L0_gnn_self_w2"], bias=a["L0_gnn_b1"])
        self.transform(self.prep_sum, self.relation_groups(), self.tab_rel, relu=True)
        self.load_experts(0)
        self.aggregate(self.tab_rel, self.gidx[0], D)
        self.load_gate(a["L0_ffn_WgT"], a["L0_gnn_b2"])
        self.statistics(residual=True)
        self.transform(self.prep_kept, self.gate_groups(), None)
        self.moe(0)
        self.load(None, None, self.wsmall, a["L1_gnn_W1"])
        self.statistics()
        self.transform(self.prep_norm, self.node_groups(D), self.tab_node)
        self.aggregate(self.tab_node, self.gidx[1], D)
        self.load(None, None, self.wsmall, a["L1_gnn_W2"], bias=a["L1_gnn_b1"])
        self.transform(self.prep_scaled, self.node_groups(D), self.tab_node, relu=True)
        self.aggregate(self.tab_node, self.gidx[1], D)
        self.load(None, None, self.wsmall[:, 0:D], a["L1_gnn_W3"], bias=a["L1_gnn_b2"])
        self.transform(self.prep_scaled, self.node_groups(D // 2), self.tab_half, relu=True)
        self.load_experts(1)
        self.aggregate(self.tab_half, self.gidx[1], D // 2)
        self.load(None, None, self.wsmall[:, 0:D], a["L1_gnn_Wp"], bias=a["L1_gnn_b3"], rows=1)
        self.transform(self.prep_half, self.project_groups(), None, relu=True, chunks=1)
        self.load_gate(a["L1_ffn_Wr"], a["L1_gnn_bp"])
        self.statistics(residual=True)
        self.transform(self.prep_kept, self.gate_groups(), None)
        self.moe(1)
        self.store_out()

    def constants(self):
        nc = self.nc
        with self.stage_block() as (block, sem):
            base, loaded, zeroed, masked = sem("base", "loaded", "zeroed", "masked")

            @block.gpsimd
            def _(pool):
                nc.gpsimd.memset(self.x[:, (TILES - 1) * D:TILES * D], 0.0).then_inc(base, 1)
                nc.gpsimd.memset(self.scratch[:, 0:D], 0.0).then_inc(base, 1)
                nc.gpsimd.memset(self.acc[:, :].rearrange("p (t w) -> p t w", w=ACCW)[:, :, D:ACCW], 0.0)
                for s in range(GSLOTS):
                    nc.gpsimd.memset(self.rowbuf[s][:, D:ACCW], 1.0)
                nc.gpsimd.iota(self.iota_e[:, :], [[0, TILES], [1, E]], base=-E, channel_multiplier=0,
                               allow_small_or_imprecise_dtypes=True)
                nc.gpsimd.memset(self.ident[:, :], 0.0).then_inc(masked, 1)
                nc.gpsimd.memset(self.tri[:, :], 1.0).then_inc(masked, 1)
                nc.gpsimd.memset(self.ones[:, :], 1.0)
                nc.gpsimd.iota(self.iota[:, :], [[1, PAIRS]], base=0, channel_multiplier=0,
                               allow_small_or_imprecise_dtypes=True)
                pool.wait_ge(masked, 2)
                nc.gpsimd.affine_select(out=self.ident[:, :], in_=self.ident[:, :], compare_op=ALU.not_equal,
                                        fill=1.0, base=0, pattern=[[-1, P]], channel_multiplier=1)
                nc.gpsimd.affine_select(out=self.tri[:, :], in_=self.tri[:, :], compare_op=ALU.is_gt,
                                        fill=0.0, base=0, pattern=[[1, P]], channel_multiplier=-1)

            @block.sync
            def _(sp):
                x = self.a["x"]
                xv = self.x[:, 0:(TILES - 1) * D].rearrange("p (t d) -> p t d", d=D)
                sp.dma_start(xv, x[0:(TILES - 1) * P, :].rearrange("(t p) d -> p t d", p=P)).then_inc(loaded, 16)
                sp.wait_ge(base, 2)
                sp.dma_start(self.x[0:LAST, (TILES - 1) * D:TILES * D], x[(TILES - 1) * P:NODES, :]).then_inc(loaded, 16)
                for t in range(MTILES):
                    sp.dma_start(self.xd[t * P:(t + 1) * P, :], self.scratch[:, 0:D]).then_inc(zeroed, 16)
                sp.wait_ge(loaded, 32)
                sp.wait_ge(zeroed, 16 * MTILES)

    def edge_pairs(self):
        nc, a = self.nc, self.a
        W = ECH * P
        with ExitStack() as ctx:
            sb = lambda n, s, d=F32: ctx.enter_context(nc.sbuf_tensor(n, s, d))
            names = ("dst", "src", "edge_type_8")
            at = [self.big[:, k * W:(k + 1) * W].bitcast(I32) for k in range(4)]
            raw, bint = at[0:3], at[3]
            col = lambda k, n=W: self.big[:, k:k + n]
            dstf, srcf, typf, bf, g0, dp = (col((4 + k) * W) for k in range(6))
            S = col(10 * W, ECH * PAIRS)
            tmp = col(10 * W + ECH * PAIRS, PAIRS)
            bmin, bmax, n, start, bs, w, end = (sb(f"e_{k}", [P, ECH]) for k in ("bmin", "bmax", "n", "start", "bs", "w", "end"))
            ps = self.ps
            rows = [P] * (ECH - 1) + [ELASTCH]
            block, sem = ctx.enter_context(self.stage_block())
            padded, loaded, link, counted, started, chosen, done = sem(
                "padded", "loaded", "link", "counted", "started", "chosen", "done")

            @block.gpsimd
            def _(pool):
                for r, fill in zip(raw, (NPAD - 1, 0, 0)):
                    nc.gpsimd.memset(r[:, (ECH - 1) * P:ECH * P], fill).then_inc(padded, 1)

            @block.sync
            def _(sp):
                sp.wait_ge(padded, 3)
                for r, name in zip(raw, names):
                    full = a[name][0:EFULL * P].rearrange("(t e) -> t e", e=P)
                    for c in range(ECH):
                        k = min(P, EFULL - c * P)
                        sp.dma_start(r[0:k, c * P:(c + 1) * P], full[c * P:c * P + k, :]).then_inc(loaded, 16)
                    k = EFULL - (ECH - 1) * P
                    sp.dma_start(r[k:k + 1, (ECH - 1) * P:(ECH - 1) * P + EREST],
                                 a[name][EFULL * P:EDGES].rearrange("(t e) -> t e", t=1)).then_inc(loaded, 16)

            @block.vector
            def _(dve):
                link_ = Chain(dve, link)
                v = nc.vector
                dve.wait_ge(loaded, 16 * 3 * (ECH + 1))
                link_(v.tensor_single_scalar(bint, raw[0], 7, ALU.arith_shift_right))
                link_(v.tensor_copy(bf, bint))
                link_(v.tensor_copy(dstf, raw[0]))
                link_(v.tensor_copy(srcf, raw[1]))
                link_(v.tensor_copy(typf, raw[2]))
                b3 = bf.rearrange("p (c e) -> p c e", c=ECH)
                link_(v.tensor_reduce(bmin[:, :], b3, AX.X, ALU.min))
                link_(v.tensor_reduce(bmax[:, :], b3, AX.X, ALU.max))
                link_(v.scalar_tensor_tensor(out=n[:, :], in0=bmax[:, :], scalar=1.0, in1=bmin[:, :], op0=ALU.add, op1=ALU.subtract))
                v.scalar_tensor_tensor(out=g0, in0=srcf, scalar=float(REL), in1=typf, op0=ALU.mult, op1=ALU.add).then_inc(counted, 1)
                dve.wait_ge(started, 1)
                link_(v.tensor_copy(start[:, :], ps[0][:, 0:ECH]))
                link_(v.tensor_tensor(bs[:, :], bmin[:, :], start[:, :], ALU.subtract))
                link_(v.tensor_single_scalar(w[:, :], bs[:, :], float(P), ALU.mult))
                link_(v.tensor_tensor(end[:, :], start[:, :], n[:, :], ALU.add))
                for c in range(ECH):
                    link_(v.tensor_scalar(dp[:, c * P:(c + 1) * P], dstf[:, c * P:(c + 1) * P], w[:, c:c + 1], None, ALU.subtract))
                    link_(v.tensor_scalar(tmp, self.iota[:, :], start[:, c:c + 1], None, ALU.is_ge))
                    link_(v.scalar_tensor_tensor(out=S[:, c * PAIRS:(c + 1) * PAIRS], in0=self.iota[:, :], scalar=end[:, c:c + 1],
                                                 in1=tmp, op0=ALU.is_lt, op1=ALU.mult))
                v.tensor_copy(tmp, self.iota[:, :]).then_inc(chosen, 1)
                dve.wait_ge(done, 1)
                link_(v.tensor_copy(self.gidx[0][:, :], ps[1][:, 0:PAIRS]))
                link_(v.tensor_copy(self.gidx[1][:, :], ps[2][:, 0:PAIRS]))
                link_(v.scalar_tensor_tensor(out=self.rel[:, :], in0=self.iota[:, :], scalar=-float(P), in1=ps[3][:, 0:PAIRS],
                                             op0=ALU.mult, op1=ALU.add))
                link_(v.tensor_tensor(dstf[0:1, 0:PAIRS], self.iota[0:1, :], ps[5][0:1, 0:PAIRS], ALU.mult))
                link_(v.tensor_tensor(dstf[0:1, 0:PAIRS], dstf[0:1, 0:PAIRS], ps[4][0:1, 0:PAIRS], ALU.add))
                link_(v.tensor_single_scalar(dstf[0:1, 0:PAIRS], dstf[0:1, 0:PAIRS], float(ACCW), ALU.mult))
                link_(v.tensor_copy(self.bucket[:, :], dstf[0:1, 0:PAIRS]))

            @block.tensor
            def _(pe):
                t = nc.tensor
                pe.wait_ge(counted, 1)
                for c in range(ECH):
                    for d in range(c):
                        t.matmul(ps[0][:, c:c + 1], self.ones[:, :], n[:, d:d + 1], start=(d == 0), stop=False)
                    last = t.matmul(ps[0][:, c:c + 1], self.tri[0:rows[c], :], n[0:rows[c], c:c + 1], start=(c == 0), stop=True)
                last.then_inc(started, 1)
                pe.wait_ge(chosen, 1)
                for bank, m, lhs in ((1, P, g0), (2, P, srcf), (3, P, dp)):
                    for c in range(ECH):
                        k = rows[c]
                        t.matmul(ps[bank][:, 0:PAIRS], lhs[0:k, c * P:(c + 1) * P], S[0:k, c * PAIRS:(c + 1) * PAIRS],
                                 start=(c == 0), stop=(c == ECH - 1))
                for bank, lhs in ((4, bs), (5, None)):
                    for c in range(ECH):
                        k = rows[c]
                        left = self.ones[0:k, 0:1] if lhs is None else lhs[0:k, c:c + 1]
                        last = t.matmul(ps[bank][0:1, 0:PAIRS], left, S[0:k, c * PAIRS:(c + 1) * PAIRS],
                                        start=(c == 0), stop=(c == ECH - 1))
                last.then_inc(done, 1)

    def load(self, to, of, to2, of2, bias=None, rows=KD):
        nc = self.nc
        with self.stage_block() as (block, sem):
            loaded = sem("loaded")

            @block.sync
            def _(sp):
                n = 1
                if to is not None:
                    for k in range(KD):
                        sp.dma_start(to[:, k], of[:, k]).then_inc(loaded, 16)
                    n += KD
                v = to2.rearrange("p (k o) -> p k o", k=rows)
                sp.dma_start(v, of2.rearrange("(k p) o -> p k o", p=P)).then_inc(loaded, 16)
                if bias is not None:
                    sp.dma_start(self.bias[:, 0:bias.shape[0]], self.spread(bias)).then_inc(loaded, 16)
                    n += 1
                sp.wait_ge(loaded, 16 * n)

    def spread(self, row):
        return row.rearrange("(a n) -> a n", a=1).to_broadcast([P, row.shape[0]])

    def load_gate(self, w, bias):
        nc = self.nc
        with self.stage_block() as (block, sem):
            loaded = sem("loaded")

            @block.sync
            def _(sp):
                sp.dma_start(self.wgate[:, :].rearrange("p (k o) -> p k o", k=KD), w.rearrange("(k p) o -> p k o", p=P)).then_inc(loaded, 16)
                sp.dma_start(self.bias[:, :], self.spread(bias)).then_inc(loaded, 16)
                sp.wait_ge(loaded, 32)

    def statistics(self, residual=False):
        nc = self.nc
        x3 = self.x[:, :].rearrange("p (t d) -> p t d", d=D)
        with self.stage_block() as (block, sem):
            link, variance, rooted = sem("link", "variance", "rooted")

            @block.vector
            def _(dve):
                v = nc.vector
                step = Chain(dve, link)
                if residual:
                    bias = self.bias[:, :].rearrange("p (t d) -> p t d", t=1).broadcast_to([P, TILES, D])
                    step(v.tensor_tensor(x3, x3, bias, ALU.add))
                    step(v.tensor_tensor(x3, x3, self.acc[:, :].rearrange("p (t w) -> p t w", w=ACCW)[:, :, 0:D], ALU.add))
                for i in range(TILES):
                    last = v.bn_stats(self.stats[:, i * 6:(i + 1) * 6], self.x[:, i * D:(i + 1) * D])
                step(last)
                for i in range(TILES):
                    last = v.bn_aggr(self.mv[:, 2 * i:2 * i + 2], self.stats[:, i * 6:(i + 1) * 6])
                step(last)
                var = self.mv[:, :].rearrange("p (t w) -> p t w", w=2)[:, :, 1:2]
                self.inverse_root(dve, step, self.rstd, var, EPS, variance, rooted)

            @block.scalar
            def _(act):
                self.root(act, variance, rooted)

    def root(self, act, ready, rooted):
        act.wait_ge(ready, 1)
        self.nc.scalar.activation(self.r3[:, :], self.r2[:, :], ACT.Sqrt).then_inc(rooted, 1)

    def inverse_root(self, dve, step, to, of, plus, ready, rooted):
        v = self.nc.vector
        t = lambda r: r[:, :].rearrange("p (t w) -> p t w", w=1)
        v.tensor_single_scalar(t(self.r2), of, plus, ALU.add).then_inc(ready, 1)
        dve.wait_ge(rooted, 1)
        step(v.reciprocal(to[:, :], self.r3[:, :]))
        step(v.tensor_tensor(self.r3[:, :], to[:, :], to[:, :], ALU.mult))
        step(v.tensor_tensor(self.r3[:, :], self.r3[:, :], self.r2[:, :], ALU.mult))
        step(v.tensor_scalar(self.r3[:, :], self.r3[:, :], -0.5, 1.5, ALU.mult, ALU.add))
        step(v.tensor_tensor(to[:, :], to[:, :], self.r3[:, :], ALU.mult))

    def normed(self, to, i):
        return self.nc.vector.tensor_scalar(to, self.x_tile(i), self.mv[:, bass.ds(i * 2, 1)], self.rstd[:, bass.ds(i, 1)],
                                            ALU.subtract, ALU.mult)

    def prep_norm(self, i, s):
        return self.normed(self.hn[s][:, :], i)

    def prep_kept(self, i, s):
        self.normed(self.acc_tile(i), i)
        return self.normed(self.hn[s][:, :], i)

    def prep_sum(self, i, s):
        return self.nc.vector.tensor_tensor(self.hn[s][:, :], self.acc_tile(i), self.bias[:, :], ALU.add)

    def prep_scaled(self, i, s, width=D):
        return self.nc.vector.scalar_tensor_tensor(out=self.hn[s][:, 0:width], in0=self.acc_tile(i, width), scalar=self.dinv[:, bass.ds(i, 1)],
                                                   in1=self.bias[:, 0:width], op0=ALU.mult, op1=ALU.add)

    def prep_half(self, i, s):
        return self.prep_scaled(i, s, D // 2)

    def relation_groups(self):
        def self_term(ps, i, s):
            return self.nc.scalar.activation(self.acc_tile(i), ps, ACT.Copy)

        def relations(g):
            def put(ps, i, s):
                return self.nc.scalar.activation(self.stage[s][:, g * 512:(g + 1) * 512], ps, ACT.Copy)
            return put

        groups = [([self.wself[:, k * D:(k + 1) * D] for k in range(KD)], D, self_term)]
        for g in range(REL * D // 512):
            groups.append(([self.wgnn[:, k * REL * D + g * 512:k * REL * D + (g + 1) * 512] for k in range(KD)], 512, relations(g)))
        return groups

    def node_groups(self, width):
        def put(ps, i, s):
            return self.nc.scalar.activation(self.acc_tile(i, width), ps, ACT.Identity, scale=self.dinv[:, bass.ds(i, 1)])
        return [([self.wsmall[:, k * width:(k + 1) * width] for k in range(KD)], width, put)]

    def project_groups(self):
        def put(ps, i, s):
            return self.nc.scalar.activation(self.acc_tile(i), ps, ACT.Copy)
        return [([self.wsmall[:, 0:D]], D, put)]

    def gate_groups(self):
        def put(ps, i, s):
            return self.nc.scalar.activation(self.scratch[:, bass.ds(i * E, E)], ps, ACT.Copy)
        return [([self.wgate[:, k * E:(k + 1) * E] for k in range(KD)], E, put)]

    def transform(self, prep, groups, table, relu=False, chunks=KD):
        nc = self.nc
        ng = len(groups)
        width = groups[-1][1]
        staged = table is self.tab_rel
        psT, psM = self.ps[0:2], self.ps[2:2 + ng]
        with self.stage_block() as (block, sem):
            rows_ready, turned, hT_ready, stored = (
                [sem(f"{n}{s}") for s in range(2)] for n in ("rows_ready", "turned", "hT_ready", "stored"))
            bank_full, bank_free = ([sem(f"{n}{g}") for g in range(ng)] for n in ("bank_full", "bank_free"))

            @block.vector
            def _(dve):
                def tile(i, j, s):
                    prep(i, s).then_inc(rows_ready[s], 1)
                    dve.wait_ge(turned[s], j + 1)
                    if later(j):
                        dve.sem_inc(self.gate, 1)
                        dve.wait_ge(bank_full[ng - 1], i - 1)
                    o, p = self.hT[s][:, 0:chunks * P], psT[s][:, 0:chunks * P]
                    if relu:
                        nc.vector.tensor_single_scalar(o, p, 0.0, ALU.max).then_inc(hT_ready[s], 1)
                    else:
                        nc.vector.tensor_copy(o, p).then_inc(hT_ready[s], 1)

                for s in range(2):
                    tile(s, 0, s)
                with dve.Fori(1, TILES // 2) as j:
                    for s in range(2):
                        tile(j * 2 + s, j, s)

            @block.tensor
            def _(pe):
                def turn(j, s):
                    pe.wait_ge(rows_ready[s], j + 1)
                    for k in range(chunks):
                        last = nc.tensor.transpose(psT[s][:, k * P:(k + 1) * P], self.hn[s][:, k * P:(k + 1) * P], self.ident[:, :])
                    last.then_inc(turned[s], 1)

                def multiply(i, j, s):
                    pe.wait_ge(hT_ready[s], j + 1)
                    for g, (w, n, _) in enumerate(groups):
                        if later(i):
                            pe.wait_ge(bank_free[g], i)
                        for k in range(chunks):
                            last = nc.tensor.matmul(psM[g][:, 0:n], self.hT[s][:, k * P:(k + 1) * P], w[k],
                                                    start=(k == 0), stop=(k == chunks - 1))
                        last.then_inc(bank_full[g], 1)

                def pair(j):
                    turn(j, 1)
                    multiply(j * 2, j, 0)
                    turn(j + 1, 0)
                    multiply(j * 2 + 1, j, 1)

                turn(0, 0)
                pair(0)
                with pe.Fori(1, TILES // 2 - 1) as j:
                    pair(j)
                turn(TILES // 2 - 1, 1)
                multiply(TILES - 2, TILES // 2 - 1, 0)
                multiply(TILES - 1, TILES // 2 - 1, 1)

            @block.scalar
            def _(act):
                def pair(j):
                    for s in range(2):
                        i = j * 2 + s
                        for g, (_, n, put) in enumerate(groups):
                            if staged and g == 1 and later(j):
                                act.wait_ge(stored[s], j * 16)
                                act.sem_inc(self.gate, 1)
                            act.wait_ge(bank_full[g], i + 1)
                            act.sem_inc(self.gate, 1)
                            put(psM[g][:, 0:n], i, s).then_inc(bank_free[g], 1)

                pair(0)
                with act.Fori(1, TILES // 2) as j:
                    pair(j)

            @block.sync
            def _(sp):
                if table is None:
                    return
                with sp.Fori(0, TILES // 2) as j:
                    for s in range(2):
                        i = j * 2 + s
                        for g in range(ng):
                            sp.wait_ge(bank_free[g], i + 1)
                            sp.sem_inc(self.gate, 1)
                        if staged:
                            rows = table[bass.ds(i * (P * REL), P * REL), :].rearrange("(p r) d -> p (r d)", r=REL)
                            sp.dma_start(rows, self.stage[s]).then_inc(stored[s], 16)
                        else:
                            sp.dma_start(table[bass.ds(i * P, P), :], self.acc_tile(i, width)).then_inc(stored[s], 16)
                for s in range(2):
                    sp.wait_ge(stored[s], TILES // 2 * 16)

    def aggregate(self, table, gidx, width, count=False):
        nc = self.nc
        wide = width + 1 if count else width
        rounds = PAIRS // GSLOTS
        with self.stage_block() as (block, sem):
            idx_ready, onehot_ready, summed, added = (
                [sem(f"{n}{s}") for s in range(GSLOTS)] for n in ("idx_ready", "onehot_ready", "summed", "added"))
            gathered, before = [g.sem for g in self.gathered], [g.base for g in self.gathered]
            for g in self.gathered:
                g.base += 16 * rounds

            @block.scalar
            def _(act):
                def round_(i):
                    for s in range(GSLOTS):
                        if later(i):
                            act.wait_ge(gathered[s], i * 16 + before[s])
                            act.sem_inc(self.gate, 1)
                        nc.scalar.activation(self.idx[s][:, :], gidx[:, bass.ds(i * GSLOTS + s, 1)], ACT.Copy).then_inc(idx_ready[s], 1)

                round_(0)
                with act.Fori(1, rounds) as i:
                    round_(i)

            @block.gpsimd
            def _(pool):
                def round_(i):
                    for s in range(GSLOTS):
                        if later(i):
                            pool.wait_ge(summed[s], i)
                            pool.sem_inc(self.gate, 1)
                        pool.wait_ge(idx_ready[s], i + 1)
                        pool.sem_inc(self.gate, 1)
                        nc.gpsimd.indirect_dma_start(self.rowbuf[s][:, 0:width], None, table,
                                                     bass.IndirectOffsetOnAxis(ap=self.idx[s][:, :], axis=0)).then_inc(gathered[s], 16)

                round_(0)
                with pool.Fori(1, rounds) as i:
                    round_(i)

            @block.vector
            def _(dve):
                half = GSLOTS // 2
                cols = self.iota[:, 0:P].rearrange("p (s c) -> p s c", s=1).broadcast_to([P, half, P])

                def onehots(at, k):
                    to = self.onehots[:, k * half * P:(k + 1) * half * P].rearrange("p (s c) -> p s c", s=half)
                    dst = self.rel[:, bass.ds(at + k * half, half)].rearrange("p (s c) -> p s c", c=1).broadcast_to([P, half, P])
                    nc.vector.tensor_tensor(to, cols, dst, ALU.is_equal).then_inc(onehot_ready[k], 1)

                def add(at, n, s, first=False):
                    to = self.acc[:, bass.ds(dve.value_load(self.bucket[0:1, bass.ds(at + s, 1)]), wide)]
                    dve.wait_ge(summed[s], n)
                    if not first:
                        dve.wait_ge(added[s - 1], n if s else n - 1)
                    nc.vector.tensor_tensor(to, to, self.ps[s][:, 0:wide], ALU.add).then_inc(added[s], 1)

                def round_(at, n, first=False):
                    for k in range(2):
                        onehots(at, k)
                        for s in range(half):
                            if k:
                                add(at, n, s, first and s == 0)
                            elif not first:
                                add(at - GSLOTS, n - 1, half + s)

                round_(0, 1, first=True)
                with dve.Fori(2, rounds + 1) as n:
                    round_(dve.snap(n * GSLOTS - GSLOTS), n)
                for s in range(half, GSLOTS):
                    add(PAIRS - GSLOTS, rounds, s)

            @block.tensor
            def _(pe):
                def round_(i):
                    for s in range(GSLOTS):
                        if s % (GSLOTS // 2) == 0:
                            pe.wait_ge(onehot_ready[s // (GSLOTS // 2)], i + 1)
                            pe.sem_inc(self.gate, 1)
                        if later(i):
                            pe.wait_ge(added[s], i)
                            pe.sem_inc(self.gate, 1)
                        pe.wait_ge(gathered[s], i * 16 + (before[s] + 16))
                        nc.tensor.matmul(self.ps[s][:, 0:wide], self.onehots[:, s * P:(s + 1) * P], self.rowbuf[s][:, 0:wide],
                                         start=True, stop=True).then_inc(summed[s], 1)

                round_(0)
                with pe.Fori(1, rounds) as i:
                    round_(i)

    def degrees(self):
        nc = self.nc
        with self.stage_block() as (block, sem):
            link, degree, rooted = sem("link", "degree", "rooted")

            @block.vector
            def _(dve):
                counts = self.acc[:, :].rearrange("p (t w) -> p t w", w=ACCW)[:, :, D:ACCW]
                self.inverse_root(dve, Chain(dve, link), self.dinv, counts, 1.0, degree, rooted)

            @block.scalar
            def _(act):
                self.root(act, degree, rooted)

    def load_experts(self, m):
        a, pre = self.a, f"L{m}_ffn_"
        with self.stage_block() as (block, _):
            @block.scalar
            def _(act):
                for e in range(E):
                    act.dma_start(self.w1[:, e * W1E:(e + 1) * W1E].rearrange("p (k h) -> p k h", k=KD),
                                  a[pre + "W1t"][e].rearrange("(k p) h -> p k h", p=P)).then_inc(self.experts_loaded, 16)
                    act.dma_start(self.w2[:, e * W2E:(e + 1) * W2E].rearrange("p (c d) -> p c d", c=HC),
                                  a[pre + "W2t"][e].rearrange("(c p) d -> p c d", p=P)).then_inc(self.experts_loaded, 16)

    def route(self, m):
        nc, n = self.nc, TILES * E
        sc = self.scratch
        names = ("eq", "oh1", "oh2", "m2nd", "both", "tot", "sa", "sb", "excl", "pos")
        eq, oh1, oh2, rest, both, tot, sa, sb_, excl, pos = (sc[:, (k + 1) * n:(k + 2) * n] for k in range(len(names)))
        L = sc[:, 0:n]
        at = (len(names) + 1) * n
        m1, m2, i1, i2, t1, t2 = (sc[:, at + k * TILES:at + (k + 1) * TILES] for k in range(6))
        at += 6 * TILES
        nt, ea, eb, ts, gb = (sc[:, at + k * E:at + (k + 1) * E] for k in range(5))
        at += 5 * E
        ni = sc[:, at:at + E].bitcast(I32)
        row = [sc[0:1, at + E + k * MTILES:at + E + (k + 1) * MTILES] for k in range(2)]
        g3 = lambda t: t.rearrange("p (t e) -> p t e", e=E)
        over = lambda t: t.rearrange("p (t o) -> p t o", o=1).broadcast_to([P, TILES, E])
        per = lambda t: t.rearrange("p (o e) -> p o e", o=1).broadcast_to([P, TILES, E])
        with self.stage_block() as (block, sem):
            link, loaded, to_exp, exp_done, masked, ranked = sem("link", "loaded", "to_exp", "exp_done", "masked", "ranked")

            @block.sync
            def _(sp):
                sp.dma_start(gb, self.spread(self.a[("L0_ffn_bg", "L1_ffn_br")[m]])).then_inc(loaded, 16)

            @block.scalar
            def _(act):
                act.wait_ge(to_exp, 1)
                if m == 0:
                    nc.scalar.activation(t1, t1, ACT.Exp).then_inc(exp_done, 1)
                else:
                    nc.scalar.activation(L, L, ACT.Exp).then_inc(exp_done, 1)

            @block.vector
            def _(dve):
                v = nc.vector
                step = Chain(dve, link)

                def best(of, value, place, onehot):
                    step(v.tensor_reduce(value, g3(of), AX.X, ALU.max))
                    step(v.tensor_tensor(g3(eq), g3(of), over(value), ALU.is_equal))
                    step(v.tensor_tensor(eq, eq, self.iota_e[:, :], ALU.mult))
                    step(v.tensor_reduce(place, g3(eq), AX.X, ALU.min))
                    step(v.tensor_tensor(g3(onehot), g3(self.iota_e[:, :]), over(place), ALU.is_equal))

                dve.wait_ge(loaded, 16)
                step(v.tensor_tensor(g3(L), g3(L), per(gb), ALU.add))
                if m == 1:
                    step(v.tensor_reduce(m1, g3(L), AX.X, ALU.max))
                    v.tensor_tensor(g3(L), g3(L), over(m1), ALU.subtract).then_inc(to_exp, 1)
                    dve.wait_ge(exp_done, 1)
                    step(v.tensor_reduce(t1, g3(L), AX.X, ALU.add))
                    step(v.reciprocal(t2, t1))
                    step(v.tensor_tensor(g3(L), g3(L), over(t2), ALU.mult))
                best(L, m1, i1, oh1)
                step(v.scalar_tensor_tensor(out=rest, in0=oh1, scalar=NEG, in1=L, op0=ALU.mult, op1=ALU.add))
                best(rest, m2, i2, oh2)
                v.tensor_tensor(both, oh1, oh2, ALU.add).then_inc(masked, 1)
                w1, w2 = self.wcomb[:, 0:TILES], self.wcomb[:, TILES:2 * TILES]
                if m == 0:
                    v.tensor_tensor(t1, m2, m1, ALU.subtract).then_inc(to_exp, 1)
                    dve.wait_ge(exp_done, 1)
                    step(v.tensor_single_scalar(t2, t1, 1.0, ALU.add))
                    step(v.reciprocal(w1, t2))
                    step(v.tensor_tensor(w2, w1, t1, ALU.mult))
                else:
                    step(v.tensor_tensor(t1, m1, m2, ALU.add))
                    step(v.reciprocal(t2, t1))
                    step(v.tensor_tensor(w1, m1, t2, ALU.mult))
                    step(v.tensor_tensor(w2, m2, t2, ALU.mult))
                dve.wait_ge(ranked, 1)
                step(v.tensor_copy(tot, self.ps[1][:, 0:n]))
                a, b, d = tot, sa, 1
                while d < TILES:
                    step(v.tensor_copy(b[:, 0:d * E], a[:, 0:d * E]))
                    step(v.tensor_tensor(b[:, d * E:n], a[:, d * E:n], a[:, 0:n - d * E], ALU.add))
                    a, b, d = b, (sb_ if b is sa else sa), 2 * d
                step(v.tensor_tensor(excl, a, tot, ALU.subtract))
                step(v.tensor_single_scalar(ni, a[:, n - E:n], float(P - 1), ALU.add))
                step(v.tensor_single_scalar(ni, ni, 7, ALU.arith_shift_right))
                step(v.tensor_copy(nt, ni))
                a, b, d = nt, ea, 1
                while d < E:
                    step(v.tensor_copy(b[:, 0:d], a[:, 0:d]))
                    step(v.tensor_tensor(b[:, d:E], a[:, d:E], a[:, 0:E - d], ALU.add))
                    a, b, d = b, (eb if b is ea else ea), 2 * d
                step(v.tensor_tensor(ts, a, nt, ALU.subtract))
                step(v.tensor_single_scalar(ts, ts, float(P), ALU.mult))
                step(v.tensor_tensor(pos, excl, self.ps[0][:, 0:n], ALU.add))
                step(v.tensor_tensor(g3(pos), g3(pos), per(ts), ALU.add))
                for k, oh in enumerate((oh1, oh2)):
                    step(v.tensor_tensor(eq, oh, pos, ALU.mult))
                    step(v.tensor_reduce(t1, g3(eq), AX.X, ALU.add))
                    step(v.tensor_copy(self.spos[:, k * TILES:(k + 1) * TILES], t1))
                step(v.tensor_scalar(row[0], self.iota[0:1, 0:MTILES], a[0:1, 0:1], None, ALU.is_ge))
                for e in range(1, E - 1):
                    step(v.scalar_tensor_tensor(out=row[e % 2], in0=self.iota[0:1, 0:MTILES], scalar=a[0:1, e:e + 1],
                                                in1=row[(e - 1) % 2], op0=ALU.is_ge, op1=ALU.add))
                step(v.tensor_copy(self.texp[:, :], row[(E - 2) % 2]))

            @block.tensor
            def _(pe):
                pe.wait_ge(masked, 1)
                nc.tensor.matmul(self.ps[0][:, 0:n], self.tri[:, :], both, start=True, stop=True)
                nc.tensor.matmul(self.ps[1][:, 0:n], self.ones[:, :], both, start=True, stop=True).then_inc(ranked, 1)

    def dispatch(self):
        nc = self.nc
        with self.stage_block() as (block, _):
            sent = self.sent.sem
            self.sent.base += 16 * TOPK * TILES

            @block.gpsimd
            def _(pool):
                for k in range(TOPK):
                    for t in range(TILES):
                        c = k * TILES + t
                        nc.gpsimd.indirect_dma_start(self.xd, bass.IndirectOffsetOnAxis(ap=self.spos[:, c:c + 1], axis=0),
                                                     self.acc[:, t * ACCW:t * ACCW + D], None).then_inc(sent, 16)
                pool.wait_ge(sent, self.sent.base)

    def experts(self, m):
        nc, a = self.nc, self.a
        affine = m == 1
        func = (ACT.Relu, ACT.Gelu)[m]
        psH, psX, psG, psY = self.ps[0:2], self.ps[2], self.ps[3:5], self.ps[5:7]
        with self.stage_block() as (block, sem):
            brow = [self.slots[:, s * (H + D):(s + 1) * (H + D)] for s in range(2)]
            rows = [self.slots[:, 2 * (H + D) + s * D:2 * (H + D) + (s + 1) * D] for s in range(4)]
            xin, yout = rows[0:2], rows[2:4]
            h, hT, xT = self.scratch[:, 0:H], self.scratch[:, H:2 * H], self.hT[0][:, :]
            lng, lnb = (self.hn[0][:, k * E * KD:(k + 1) * E * KD] for k in range(2))
            x_in, bias_in, y_ready = ([sem(f"{k}{s}") for s in range(2)] for k in ("x_in", "bias_in", "y_ready"))
            y_stored, before = [y.sem for y in self.y_stored], self.y_stored[0].base
            for y in self.y_stored:
                y.base += MTILES // 2 * 16
            x_turned, xT_ready, h_full, h_ready, h_turned, hT_ready, y_full, ln_loaded = (
                sem(k) for k in ("x_turned", "xT_ready", "h_full", "h_ready", "h_turned", "hT_ready", "y_full", "ln_loaded"))

            def expert(eng, i):
                return eng.value_load(self.texp[0:1, bass.ds(i, 1)], min_val=0, max_val=E - 1)

            @block.sync
            def _(sp):
                if affine:
                    sp.dma_start(lng, a["L1_ffn_lngT"]).then_inc(ln_loaded, 16)
                    sp.dma_start(lnb, a["L1_ffn_lnbT"]).then_inc(ln_loaded, 16)

                def fetch(i, j, s):
                    e = expert(sp, i)
                    if later(j):
                        sp.wait_ge(x_turned, i - 1)
                        sp.sem_inc(self.gate, 1)
                    sp.dma_start(xin[s][:, 0:D], self.xd[bass.ds(i * P, P), :]).then_inc(x_in[s], 16)
                    if later(j):
                        sp.wait_ge(y_ready[s], j)
                        sp.sem_inc(self.gate, 1)
                    sp.dma_start(brow[s][:, :], a[f"L{m}_ffn_b12"][bass.ds(e, 1), :].to_broadcast([P, H + D])).then_inc(bias_in[s], 16)

                for s in range(2):
                    fetch(s, 0, s)
                with sp.Fori(1, MTILES // 2) as j:
                    for s in range(2):
                        fetch(j * 2 + s, j, s)

            @block.gpsimd
            def _(pool):
                with pool.Fori(0, MTILES // 2) as j:
                    for s in range(2):
                        pool.wait_ge(y_ready[s], j + 1)
                        pool.sem_inc(self.gate, 1)
                        pool.dma_start(self.yd[bass.ds((j * 2 + s) * P, P), :], yout[s][:, 0:D]).then_inc(y_stored[s], 16)
                for s in range(2):
                    pool.wait_ge(y_stored[s], self.y_stored[s].base)

            @block.tensor
            def _(pe):
                def turn_x(j, s):
                    pe.wait_ge(x_in[s], j * 16 + 16)
                    for k in range(KD):
                        last = nc.tensor.transpose(psX[:, k * P:(k + 1) * P], xin[s][:, k * P:(k + 1) * P], self.ident[:, :])
                    last.then_inc(x_turned, 1)

                def up(i):
                    e = expert(pe, i)
                    pe.wait_ge(xT_ready, i + 1)
                    pe.sem_inc(self.gate, 1)
                    for b in range(HB):
                        for k in range(KD):
                            last = nc.tensor.matmul(psH[b][:, :], xT[:, k * P:(k + 1) * P],
                                                    self.w1[:, bass.ds(e * W1E + (k * H + b * 512), 512)],
                                                    start=(k == 0), stop=(k == KD - 1))
                    last.then_inc(h_full, 1)

                def turn_h(i):
                    pe.wait_ge(h_ready, i + 1)
                    for c in range(HC):
                        last = nc.tensor.transpose(psG[c // 4][:, (c % 4) * P:(c % 4 + 1) * P], h[:, c * P:(c + 1) * P], self.ident[:, :])
                    last.then_inc(h_turned, 1)

                def down(i, s):
                    e = expert(pe, i)
                    pe.wait_ge(hT_ready, i * 2 + 2)
                    pe.sem_inc(self.gate, 1)
                    for c in range(HC):
                        last = nc.tensor.matmul(psY[s][:, 0:D], hT[:, c * P:(c + 1) * P], self.w2[:, bass.ds(e * W2E + c * D, D)],
                                                start=(c == 0), stop=(c == HC - 1))
                    last.then_inc(y_full, 1)

                pe.wait_ge(self.experts_loaded, 16 * 2 * E * (m + 1))
                turn_x(0, 0)
                up(0)
                turn_x(0, 1)
                turn_h(0)
                with pe.Fori(0, MTILES // 2 - 1) as j:
                    i = j * 2
                    up(i + 1)
                    turn_x(j + 1, 0)
                    down(i, 0)
                    turn_h(i + 1)
                    up(i + 2)
                    turn_x(j + 1, 1)
                    down(i + 1, 1)
                    turn_h(i + 2)
                up(MTILES - 1)
                down(MTILES - 2, 0)
                turn_h(MTILES - 1)
                down(MTILES - 1, 1)

            @block.vector
            def _(dve):
                def take_x(i):
                    e = expert(dve, i) if affine else None
                    dve.wait_ge(x_turned, i + 1)
                    if affine:
                        dve.sem_inc(self.gate, 1)
                    for k in range(KD):
                        o, p = xT[:, k * P:(k + 1) * P], psX[:, k * P:(k + 1) * P]
                        if affine:
                            last = nc.vector.tensor_scalar(o, p, lng[:, bass.ds(e * KD + k, 1)], lnb[:, bass.ds(e * KD + k, 1)], ALU.mult, ALU.add)
                        else:
                            last = nc.vector.tensor_copy(o, p)
                    last.then_inc(xT_ready, 1)

                def take_h(i, j, s):
                    dve.wait_ge(bias_in[s], j * 16 + 16)
                    dve.sem_inc(self.gate, 1)
                    dve.wait_ge(h_full, i + 1)
                    for b in range(HB):
                        last = nc.vector.tensor_tensor(h[:, b * 512:(b + 1) * 512], psH[b][:, :], brow[s][:, b * 512:(b + 1) * 512], ALU.add)
                    last.then_inc(h_ready, 1)

                def take_y(i, j, s):
                    if later(j):
                        dve.wait_ge(y_stored[s], j * 16 + before)
                        dve.sem_inc(self.gate, 1)
                    dve.wait_ge(y_full, i + 1)
                    nc.vector.tensor_tensor(yout[s][:, 0:D], psY[s][:, 0:D], brow[s][:, H:H + D], ALU.add).then_inc(y_ready[s], 1)

                def pair(j):
                    i = j * 2
                    take_h(i + 1, j, 1)
                    take_x(i + 2)
                    take_y(i, j, 0)
                    take_h(i + 2, j + 1, 0)
                    take_x(i + 3)
                    take_y(i + 1, j, 1)

                if affine:
                    dve.wait_ge(ln_loaded, 32)
                take_x(0)
                take_h(0, 0, 0)
                take_x(1)
                pair(0)
                with dve.Fori(1, MTILES // 2 - 1) as j:
                    pair(j)
                take_h(MTILES - 1, MTILES // 2 - 1, 1)
                take_y(MTILES - 2, MTILES // 2 - 1, 0)
                take_y(MTILES - 1, MTILES // 2 - 1, 1)

            @block.scalar
            def _(act):
                def take_g(i, first=False):
                    act.wait_ge(h_turned, i + 1)
                    for b in range(2):
                        if not first and b == 0:
                            act.sem_inc(self.gate, 1)
                            act.wait_ge(y_full, i)
                        nc.scalar.activation(hT[:, b * 512:(b + 1) * 512], psG[b][:, :], func).then_inc(hT_ready, 1)

                take_g(0, True)
                with act.Fori(1, MTILES) as i:
                    take_g(i)

    def combine(self):
        nc = self.nc
        with self.stage_block() as (block, sem):
            added = sem("added")
            fetched, before = [g.sem for g in self.gathered], [g.base for g in self.gathered]
            for g in self.gathered:
                g.base += 16 * TOPK * TILES // GSLOTS

            @block.gpsimd
            def _(pool):
                for c in range(TOPK * TILES):
                    s = c % GSLOTS
                    if c >= GSLOTS:
                        pool.wait_ge(added, c - GSLOTS + 1)
                    nc.gpsimd.indirect_dma_start(self.rowbuf[s][:, 0:D], None, self.yd,
                                                 bass.IndirectOffsetOnAxis(ap=self.spos[:, c:c + 1], axis=0)).then_inc(fetched[s], 16)

            @block.vector
            def _(dve):
                for c in range(TOPK * TILES):
                    s, t = c % GSLOTS, c % TILES
                    dve.wait_ge(fetched[s], before[s] + 16 * (c // GSLOTS + 1))
                    if c >= TILES:
                        dve.wait_ge(added, c - TILES + 1)
                    x = self.x[:, t * D:(t + 1) * D]
                    nc.vector.scalar_tensor_tensor(out=x, in0=self.rowbuf[s][:, 0:D], scalar=self.wcomb[:, c:c + 1], in1=x,
                                                   op0=ALU.mult, op1=ALU.add).then_inc(added, 1)

    def moe(self, m):
        self.route(m)
        self.dispatch()
        self.experts(m)
        self.combine()

    def store_out(self):
        nc = self.nc
        with self.stage_block() as (block, sem):
            stored = sem("stored")

            @block.sync
            def _(sp):
                full = (TILES - 1) * P
                sp.dma_start(self.out[0:full, :].rearrange("(t p) d -> p t d", p=P),
                             self.x[:, 0:(TILES - 1) * D].rearrange("p (t d) -> p t d", d=D)).then_inc(stored, 16)
                sp.dma_start(self.out[full:NODES, :], self.x[0:LAST, (TILES - 1) * D:TILES * D]).then_inc(stored, 16)
                sp.wait_ge(stored, 32)


def kernel(**inputs):
    import numpy as np
    import concourse.bacc as bacc
    from concourse.bass_utils import run_bass_kernel_spmd

    given = {k: np.asarray(v) for k, v in inputs.items()}
    arrays = {k: given[k] for k in (
        "x", "src", "dst", "edge_type_8", "L0_gnn_W1", "L0_gnn_self_w1", "L0_gnn_b1", "L0_gnn_W2", "L0_gnn_self_w2",
        "L0_gnn_b2", "L0_ffn_bg", "L1_gnn_W1", "L1_gnn_b1", "L1_gnn_W2", "L1_gnn_b2", "L1_gnn_W3", "L1_gnn_b3",
        "L1_gnn_Wp", "L1_gnn_bp", "L1_ffn_Wr", "L1_ffn_br")}
    arrays["L0_ffn_WgT"] = given["L0_ffn_Wg"].T
    arrays["L0_ffn_W1t"] = given["L0_ffn_W1"].transpose(0, 2, 1)
    arrays["L0_ffn_W2t"] = given["L0_ffn_W2"].transpose(0, 2, 1)
    arrays["L1_ffn_W1t"] = given["L1_ffn_W1"]
    arrays["L1_ffn_W2t"] = given["L1_ffn_W2"]
    for m in range(2):
        arrays[f"L{m}_ffn_b12"] = np.concatenate([given[f"L{m}_ffn_b1"], given[f"L{m}_ffn_b2"]], axis=1)
    for k, name in (("g", "L1_ffn_ln_g"), ("b", "L1_ffn_ln_b")):
        arrays[f"L1_ffn_ln{k}T"] = given[name].reshape(E, KD, P).transpose(2, 0, 1).reshape(P, E * KD)
    arrays = {k: np.ascontiguousarray(v) for k, v in arrays.items()}
    nc = bacc.Bacc("TRN2", target_bir_lowering=False, num_devices=1)
    a = {k: nc.dram_tensor(f"in_{k}", v.shape, mybir.dt.from_np(v.dtype), kind="ExternalInput").ap() for k, v in arrays.items()}
    out = nc.dram_tensor("out", (NODES, D), F32, kind="ExternalOutput").ap()
    build(nc, a, out)
    r = run_bass_kernel_spmd(nc, [{f"in_{k}": v for k, v in arrays.items()}], core_ids=[0])
    return r.results[0]["out"]
```

```python
from contextlib import ExitStack, contextmanager

import concourse.bass as bass
from concourse import mybir

F32 = mybir.dt.float32
U32 = mybir.dt.uint32
F16 = mybir.dt.float16
BF16 = mybir.dt.bfloat16
I32 = mybir.dt.int32
ALU = mybir.AluOpType
ACT = mybir.ActivationFunctionType
AX = mybir.AxisListType

P = 128
NODES = 2500
D = 256
KD = D // P
TILES = -(-NODES // P)
NPAD = TILES * P
LAST = NODES - (TILES - 1) * P
EDGES = 40000
ETILES = -(-EDGES // P)
EFULL = EDGES // P
EREST = EDGES - EFULL * P
ECH = -(-ETILES // P)
ELASTCH = ETILES - (ECH - 1) * P
REL = 8
GSLOTS = 8
PAIRS = -(-(ETILES + TILES - 1) // GSLOTS) * GSLOTS
WINDOW = 19
WINEDGES = WINDOW * P - (P - 1)
FULLCOUNT = 2048
HOTS = 5
PARTS = 3
MID = NPAD // 2
FAR = 1.0e5
ACCW = D + 1
E = 8
H = 1024
HC = H // P
HB = H // 512
TOPK = 2
MTILES = (NPAD * TOPK + E * (P - 1)) // P
MTILES += MTILES % 2
SLOTS = MTILES * P
W1E = KD * H
W2E = HC * D
EPS = 1e-5
NEG = -3.0e38
SET = 44


def later(i):
    return not (isinstance(i, int) and i == 0)


class Chain:

    def __init__(self, eng, sem, base=0):
        self.eng, self.sem, self.base, self.n = eng, sem, base, 0

    def __call__(self, ins):
        ins.then_inc(self.sem, 1)
        self.n += 1
        self.eng.wait_ge(self.sem, self.base + self.n)


class Count:

    def __init__(self, sem):
        self.sem, self.base = sem, 0


def build(nc, a, out):
    with ExitStack() as ctx:
        Program(nc, a, out, ctx).run()


class Program:
    def __init__(self, nc, a, out, ctx):
        self.nc, self.a, self.out = nc, a, out

        def sb(name, shape, dt=F32):
            return ctx.enter_context(nc.sbuf_tensor(name, shape, dt))

        self.x = sb("x_all", [P, TILES * D])
        self.acc = sb("acc", [P, TILES * ACCW])
        self.big = sb("big", [P, E * (W1E + W2E)])
        self.w1 = self.big[:, 0:E * W1E]
        self.w2 = self.big[:, E * W1E:E * (W1E + W2E)]
        self.counts = self.big[:, 0:TILES * NPAD // 2].bitcast(F16)
        self.free = self.big[:, TILES * NPAD // 2:]
        self.wgnn = self.big[:, 0:KD * REL * D]
        self.wself = self.big[:, KD * REL * D:KD * (REL + 1) * D]
        at = KD * (REL + 1) * D
        self.stage = [self.big[:, at + s * REL * D:at + (s + 1) * REL * D] for s in range(2)]
        self.wsmall = sb("w_small", [P, KD * D])
        self.wgate = sb("w_gate", [P, KD * E])
        self.ident = sb("ident", [P, P])
        self.tri = sb("tri", [P, P])
        self.ones = sb("ones", [P, P])
        self.iota = sb("iota", [P, PAIRS])
        self.gidx = [sb("gidx_relation", [P, PAIRS]), sb("gidx_node", [P, PAIRS])]
        self.rel = sb("dst_in_bucket", [P, PAIRS])
        self.bucket = sb("bucket_of_pair", [1, PAIRS], I32)
        self.dinv = sb("dinv", [P, TILES])
        self.bias = sb("bias_row", [P, D])
        self.hn = [sb(f"hn{s}", [P, D]) for s in range(2)]
        self.hT = [sb(f"hT{s}", [P, D]) for s in range(2)]
        self.stats = sb("stats", [P, TILES * 6])
        self.mv = sb("mean_var", [P, TILES * 2])
        self.rstd = sb("rstd", [P, TILES])
        self.r2, self.r3 = sb("root_of", [P, TILES]), sb("root", [P, TILES])
        self.scratch = sb("scratch", [P, 2048])
        self.wcomb = sb("w_comb", [P, 2 * TILES])
        self.spos = sb("slot_pos", [P, 2 * TILES], U32)
        self.texp = sb("tile_expert", [1, MTILES], I32)
        self.slots = sb("slots", [P, max(GSLOTS * (ACCW + P) * 1, 2 * 2 * D + 2 * (H + D))])
        self.rowbuf = [self.slots[:, s * ACCW:(s + 1) * ACCW] for s in range(GSLOTS)]
        at = GSLOTS * ACCW
        self.onehots = self.slots[:, at:at + GSLOTS * P]
        self.parts = [self.free[:, k * TILES * D // 2:(k + 1) * TILES * D // 2].bitcast(BF16) for k in range(2)]
        self.parts.append(self.slots[:, 0:TILES * D // 2].bitcast(BF16))
        self.window = sb("window", [1, TILES], I32)
        self.uncounted = sb("uncounted", [1, 1], I32)
        self.column = sb("column", [P, 4])
        self.idx = [sb(f"idx{s}", [P, 1], U32) for s in range(GSLOTS)]
        self.iota_e = sb("iota_e", [P, TILES * E])
        self.ps = [ctx.enter_context(nc.psum_tensor(f"ps{b}", [P, 512], F32)) for b in range(8)]

        self.gate = ctx.enter_context(nc.semaphore("gate"))
        self.experts_loaded = ctx.enter_context(nc.semaphore("experts_loaded"))
        self.gathered = [Count(ctx.enter_context(nc.semaphore(f"gathered{s}"))) for s in range(GSLOTS)]
        self.regathered = [Count(ctx.enter_context(nc.semaphore(f"regathered{s}"))) for s in range(GSLOTS)]
        self.y_stored = [Count(ctx.enter_context(nc.semaphore(f"y_stored{s}"))) for s in range(2)]
        self.sent = Count(ctx.enter_context(nc.semaphore("sent")))
        self.sets = [[ctx.enter_context(nc.semaphore(f"set{k}_{n}")) for n in range(SET)] for k in range(2)]
        self.turn = 0

        def dram(name, shape):
            return nc.dram_tensor(name, shape, F32, kind="Internal").ap()

        self.tab_rel = dram("tab_rel", [NPAD * REL, D])
        self.tab_node = dram("tab_node", [NPAD, D])
        self.tab_half = dram("tab_half", [NPAD, D // 2])
        self.xd = dram("x_dispatched", [SLOTS, D])
        self.yd = dram("y_dispatched", [SLOTS, D])

    @contextmanager
    def stage_block(self):
        own, other = self.sets[self.turn], self.sets[1 - self.turn]
        self.turn = 1 - self.turn
        free = iter(own)
        with self.nc.Block() as block:
            @block.sync
            def _(sp):
                sp.sem_clear(range(other[0].num, other[-1].num + 1))

            yield block, lambda *names: [next(free) for _ in names] if len(names) != 1 else next(free)

    def acc_tile(self, i, width=D):
        return self.acc[:, bass.ds(i * ACCW, width)]

    def x_tile(self, i):
        return self.x[:, bass.ds(i * D, D)]

    def run(self):
        a = self.a
        self.constants()
        self.edge_pairs()
        self.load(self.wgnn.rearrange("p (k r o) -> p k r o", k=KD, r=REL), a["L0_gnn_W1"].rearrange("r (k p) o -> p k r o", p=P), self.wself, a["L0_gnn_self_w1"])
        self.statistics()
        self.transform(self.prep_norm, self.relation_groups(), self.tab_rel)
        self.aggregate(self.tab_rel, self.gidx[0], D, count=True)
        self.degrees()
        self.load(self.wgnn.rearrange("p (k r o) -> p k r o", k=KD, r=REL), a["L0_gnn_W2"].rearrange("r (k p) o -> p k r o", p=P), self.wself, a["L0_gnn_self_w2"], bias=a["L0_gnn_b1"])
        self.transform(self.prep_sum, self.relation_groups(), self.tab_rel, relu=True)
        self.load_experts(0)
        self.aggregate(self.tab_rel, self.gidx[0], D)
        self.load_gate(a["L0_ffn_WgT"], a["L0_gnn_b2"])
        self.statistics(residual=True)
        self.transform(self.prep_kept, self.gate_groups(), None)
        self.moe(0)
        self.count_matrix()
        self.load(None, None, self.wsmall, a["L1_gnn_W1"])
        self.statistics()
        self.transform(self.prep_norm, self.node_groups(D), self.tab_node, split=True)
        self.aggregate(self.tab_node, self.gidx[1], D, counted=True)
        self.load(None, None, self.wsmall, a["L1_gnn_W2"], bias=a["L1_gnn_b1"])
        self.transform(self.prep_scaled, self.node_groups(D), self.tab_node, relu=True, split=True)
        self.aggregate(self.tab_node, self.gidx[1], D, counted=True)
        self.load(None, None, self.wsmall[:, 0:D], a["L1_gnn_W3"], bias=a["L1_gnn_b2"])
        self.transform(self.prep_scaled, self.node_groups(D // 2), self.tab_half, relu=True, split=True)
        self.aggregate(self.tab_half, self.gidx[1], D // 2, counted=True)
        self.load_experts(1)
        self.load(None, None, self.wsmall[:, 0:D], a["L1_gnn_Wp"], bias=a["L1_gnn_b3"], rows=1)
        self.transform(self.prep_half, self.project_groups(), None, relu=True, chunks=1)
        self.load_gate(a["L1_ffn_Wr"], a["L1_gnn_bp"])
        self.statistics(residual=True)
        self.transform(self.prep_kept, self.gate_groups(), None)
        self.moe(1)
        self.store_out()

    def constants(self):
        nc = self.nc
        with self.stage_block() as (block, sem):
            base, loaded, zeroed, masked = sem("base", "loaded", "zeroed", "masked")

            @block.gpsimd
            def _(pool):
                nc.gpsimd.memset(self.x[:, (TILES - 1) * D:TILES * D], 0.0).then_inc(base, 1)
                nc.gpsimd.memset(self.scratch[:, 0:D], 0.0).then_inc(base, 1)
                nc.gpsimd.memset(self.acc[:, :].rearrange("p (t w) -> p t w", w=ACCW)[:, :, D:ACCW], 0.0)
                for s in range(GSLOTS):
                    nc.gpsimd.memset(self.rowbuf[s][:, D:ACCW], 1.0)
                nc.gpsimd.iota(self.iota_e[:, :], [[0, TILES], [1, E]], base=-E, channel_multiplier=0,
                               allow_small_or_imprecise_dtypes=True)
                nc.gpsimd.memset(self.ident[:, :], 0.0).then_inc(masked, 1)
                nc.gpsimd.memset(self.tri[:, :], 1.0).then_inc(masked, 1)
                nc.gpsimd.memset(self.ones[:, :], 1.0)
                nc.gpsimd.iota(self.iota[:, :], [[1, PAIRS]], base=0, channel_multiplier=0,
                               allow_small_or_imprecise_dtypes=True)
                pool.wait_ge(masked, 2)
                nc.gpsimd.affine_select(out=self.ident[:, :], in_=self.ident[:, :], compare_op=ALU.not_equal,
                                        fill=1.0, base=0, pattern=[[-1, P]], channel_multiplier=1)
                nc.gpsimd.affine_select(out=self.tri[:, :], in_=self.tri[:, :], compare_op=ALU.is_gt,
                                        fill=0.0, base=0, pattern=[[1, P]], channel_multiplier=-1)

            @block.sync
            def _(sp):
                x = self.a["x"]
                xv = self.x[:, 0:(TILES - 1) * D].rearrange("p (t d) -> p t d", d=D)
                sp.dma_start(xv, x[0:(TILES - 1) * P, :].rearrange("(t p) d -> p t d", p=P)).then_inc(loaded, 16)
                sp.wait_ge(base, 2)
                sp.dma_start(self.x[0:LAST, (TILES - 1) * D:TILES * D], x[(TILES - 1) * P:NODES, :]).then_inc(loaded, 16)
                for t in range(MTILES):
                    sp.dma_start(self.xd[t * P:(t + 1) * P, :], self.scratch[:, 0:D]).then_inc(zeroed, 16)
                sp.wait_ge(loaded, 32)
                sp.wait_ge(zeroed, 16 * MTILES)

    def edge_pairs(self):
        nc, a = self.nc, self.a
        W = ECH * P
        with ExitStack() as ctx:
            names = ("dst", "src", "edge_type_8")
            at = [self.big[:, k * W:(k + 1) * W].bitcast(I32) for k in range(4)]
            raw, bint = at[0:3], at[3]
            col = lambda k, n=W: self.big[:, k:k + n]
            dstf, srcf, typf, bf, g0, dp = (col((4 + k) * W) for k in range(6))
            S = col(10 * W, ECH * PAIRS)
            tmp = col(10 * W + ECH * PAIRS, PAIRS)
            bmin, bmax, n, start, bs, w, end = (self.scratch[:, k * ECH:(k + 1) * ECH] for k in range(7))
            ps = self.ps
            rows = [P] * (ECH - 1) + [ELASTCH]
            block, sem = ctx.enter_context(self.stage_block())
            padded, loaded, link, counted, started, chosen, done = sem(
                "padded", "loaded", "link", "counted", "started", "chosen", "done")

            @block.gpsimd
            def _(pool):
                for r, fill in zip(raw, (NPAD - 1, 0, 0)):
                    nc.gpsimd.memset(r[:, (ECH - 1) * P:ECH * P], fill).then_inc(padded, 1)

            @block.sync
            def _(sp):
                sp.wait_ge(padded, 3)
                for r, name in zip(raw, names):
                    full = a[name][0:EFULL * P].rearrange("(t e) -> t e", e=P)
                    for c in range(ECH):
                        k = min(P, EFULL - c * P)
                        sp.dma_start(r[0:k, c * P:(c + 1) * P], full[c * P:c * P + k, :]).then_inc(loaded, 16)
                    k = EFULL - (ECH - 1) * P
                    sp.dma_start(r[k:k + 1, (ECH - 1) * P:(ECH - 1) * P + EREST],
                                 a[name][EFULL * P:EDGES].rearrange("(t e) -> t e", t=1)).then_inc(loaded, 16)

            @block.vector
            def _(dve):
                link_ = Chain(dve, link)
                v = nc.vector
                dve.wait_ge(loaded, 16 * 3 * (ECH + 1))
                link_(v.tensor_single_scalar(bint, raw[0], 7, ALU.arith_shift_right))
                link_(v.tensor_copy(bf, bint))
                link_(v.tensor_copy(dstf, raw[0]))
                link_(v.tensor_copy(srcf, raw[1]))
                link_(v.tensor_copy(typf, raw[2]))
                b3 = bf.rearrange("p (c e) -> p c e", c=ECH)
                link_(v.tensor_reduce(bmin[:, :], b3, AX.X, ALU.min))
                link_(v.tensor_reduce(bmax[:, :], b3, AX.X, ALU.max))
                link_(v.scalar_tensor_tensor(out=n[:, :], in0=bmax[:, :], scalar=1.0, in1=bmin[:, :], op0=ALU.add, op1=ALU.subtract))
                v.scalar_tensor_tensor(out=g0, in0=srcf, scalar=float(REL), in1=typf, op0=ALU.mult, op1=ALU.add).then_inc(counted, 1)
                dve.wait_ge(started, 1)
                link_(v.tensor_copy(start[:, :], ps[0][:, 0:ECH]))
                link_(v.tensor_tensor(bs[:, :], bmin[:, :], start[:, :], ALU.subtract))
                link_(v.tensor_single_scalar(w[:, :], bs[:, :], float(P), ALU.mult))
                link_(v.tensor_tensor(end[:, :], start[:, :], n[:, :], ALU.add))
                for c in range(ECH):
                    link_(v.tensor_scalar(dp[:, c * P:(c + 1) * P], dstf[:, c * P:(c + 1) * P], w[:, c:c + 1], None, ALU.subtract))
                    link_(v.tensor_scalar(tmp, self.iota[:, :], start[:, c:c + 1], None, ALU.is_ge))
                    link_(v.scalar_tensor_tensor(out=S[:, c * PAIRS:(c + 1) * PAIRS], in0=self.iota[:, :], scalar=end[:, c:c + 1],
                                                 in1=tmp, op0=ALU.is_lt, op1=ALU.mult))
                v.tensor_copy(tmp, self.iota[:, :]).then_inc(chosen, 1)
                dve.wait_ge(done, 1)
                link_(v.tensor_copy(self.gidx[0][:, :], ps[1][:, 0:PAIRS]))
                link_(v.tensor_copy(self.gidx[1][:, :], ps[2][:, 0:PAIRS]))
                link_(v.scalar_tensor_tensor(out=self.rel[:, :], in0=self.iota[:, :], scalar=-float(P), in1=ps[3][:, 0:PAIRS],
                                             op0=ALU.mult, op1=ALU.add))
                link_(v.tensor_tensor(dstf[0:1, 0:PAIRS], self.iota[0:1, :], ps[5][0:1, 0:PAIRS], ALU.mult))
                link_(v.tensor_tensor(dstf[0:1, 0:PAIRS], dstf[0:1, 0:PAIRS], ps[4][0:1, 0:PAIRS], ALU.add))
                link_(v.scalar_tensor_tensor(out=dstf[0:1, 0:PAIRS], in0=ps[5][0:1, 0:PAIRS], scalar=-float(TILES - 1),
                                             in1=dstf[0:1, 0:PAIRS], op0=ALU.mult, op1=ALU.add))
                link_(v.tensor_single_scalar(dstf[0:1, 0:PAIRS], dstf[0:1, 0:PAIRS], float(TILES - 1), ALU.add))
                link_(v.tensor_single_scalar(dstf[0:1, 0:PAIRS], dstf[0:1, 0:PAIRS], float(ACCW), ALU.mult))
                link_(v.tensor_copy(self.bucket[:, :], dstf[0:1, 0:PAIRS]))

            @block.tensor
            def _(pe):
                t = nc.tensor
                pe.wait_ge(counted, 1)
                for c in range(ECH):
                    for d in range(c):
                        t.matmul(ps[0][:, c:c + 1], self.ones[:, :], n[:, d:d + 1], start=(d == 0), stop=False)
                    last = t.matmul(ps[0][:, c:c + 1], self.tri[0:rows[c], :], n[0:rows[c], c:c + 1], start=(c == 0), stop=True)
                last.then_inc(started, 1)
                pe.wait_ge(chosen, 1)
                for bank, m, lhs in ((1, P, g0), (2, P, srcf), (3, P, dp)):
                    for c in range(ECH):
                        k = rows[c]
                        t.matmul(ps[bank][:, 0:PAIRS], lhs[0:k, c * P:(c + 1) * P], S[0:k, c * PAIRS:(c + 1) * PAIRS],
                                 start=(c == 0), stop=(c == ECH - 1))
                for bank, lhs in ((4, bs), (5, None)):
                    for c in range(ECH):
                        k = rows[c]
                        left = self.ones[0:k, 0:1] if lhs is None else lhs[0:k, c:c + 1]
                        last = t.matmul(ps[bank][0:1, 0:PAIRS], left, S[0:k, c * PAIRS:(c + 1) * PAIRS],
                                        start=(c == 0), stop=(c == ECH - 1))
                last.then_inc(done, 1)

    def load(self, to, of, to2, of2, bias=None, rows=KD):
        nc = self.nc
        with self.stage_block() as (block, sem):
            loaded = sem("loaded")

            @block.sync
            def _(sp):
                n = 1
                if to is not None:
                    for k in range(KD):
                        sp.dma_start(to[:, k], of[:, k]).then_inc(loaded, 16)
                    n += KD
                v = to2.rearrange("p (k o) -> p k o", k=rows)
                sp.dma_start(v, of2.rearrange("(k p) o -> p k o", p=P)).then_inc(loaded, 16)
                if bias is not None:
                    sp.dma_start(self.bias[:, 0:bias.shape[0]], self.spread(bias)).then_inc(loaded, 16)
                    n += 1
                sp.wait_ge(loaded, 16 * n)

    def spread(self, row):
        return row.rearrange("(a n) -> a n", a=1).to_broadcast([P, row.shape[0]])

    def load_gate(self, w, bias):
        nc = self.nc
        with self.stage_block() as (block, sem):
            loaded = sem("loaded")

            @block.sync
            def _(sp):
                sp.dma_start(self.wgate[:, :].rearrange("p (k o) -> p k o", k=KD), w.rearrange("(k p) o -> p k o", p=P)).then_inc(loaded, 16)
                sp.dma_start(self.bias[:, :], self.spread(bias)).then_inc(loaded, 16)
                sp.wait_ge(loaded, 32)

    def statistics(self, residual=False):
        nc = self.nc
        x3 = self.x[:, :].rearrange("p (t d) -> p t d", d=D)
        with self.stage_block() as (block, sem):
            link, variance, rooted = sem("link", "variance", "rooted")

            @block.vector
            def _(dve):
                v = nc.vector
                step = Chain(dve, link)
                if residual:
                    bias = self.bias[:, :].rearrange("p (t d) -> p t d", t=1).broadcast_to([P, TILES, D])
                    step(v.tensor_tensor(x3, x3, bias, ALU.add))
                    step(v.tensor_tensor(x3, x3, self.acc[:, :].rearrange("p (t w) -> p t w", w=ACCW)[:, :, 0:D], ALU.add))
                for i in range(TILES):
                    last = v.bn_stats(self.stats[:, i * 6:(i + 1) * 6], self.x[:, i * D:(i + 1) * D])
                step(last)
                for i in range(TILES):
                    last = v.bn_aggr(self.mv[:, 2 * i:2 * i + 2], self.stats[:, i * 6:(i + 1) * 6])
                step(last)
                var = self.mv[:, :].rearrange("p (t w) -> p t w", w=2)[:, :, 1:2]
                self.inverse_root(dve, step, self.rstd, var, EPS, variance, rooted)

            @block.scalar
            def _(act):
                self.root(act, variance, rooted)

    def root(self, act, ready, rooted):
        act.wait_ge(ready, 1)
        self.nc.scalar.activation(self.r3[:, :], self.r2[:, :], ACT.Sqrt).then_inc(rooted, 1)

    def inverse_root(self, dve, step, to, of, plus, ready, rooted):
        v = self.nc.vector
        t = lambda r: r[:, :].rearrange("p (t w) -> p t w", w=1)
        v.tensor_single_scalar(t(self.r2), of, plus, ALU.add).then_inc(ready, 1)
        dve.wait_ge(rooted, 1)
        step(v.reciprocal(to[:, :], self.r3[:, :]))
        step(v.tensor_tensor(self.r3[:, :], to[:, :], to[:, :], ALU.mult))
        step(v.tensor_tensor(self.r3[:, :], self.r3[:, :], self.r2[:, :], ALU.mult))
        step(v.tensor_scalar(self.r3[:, :], self.r3[:, :], -0.5, 1.5, ALU.mult, ALU.add))
        step(v.tensor_tensor(to[:, :], to[:, :], self.r3[:, :], ALU.mult))

    def normed(self, to, i):
        return self.nc.vector.tensor_scalar(to, self.x_tile(i), self.mv[:, bass.ds(i * 2, 1)], self.rstd[:, bass.ds(i, 1)],
                                            ALU.subtract, ALU.mult)

    def prep_norm(self, i, s):
        return self.normed(self.hn[s][:, :], i)

    def prep_kept(self, i, s):
        self.normed(self.acc_tile(i), i)
        return self.normed(self.hn[s][:, :], i)

    def prep_sum(self, i, s):
        return self.nc.vector.tensor_tensor(self.hn[s][:, :], self.acc_tile(i), self.bias[:, :], ALU.add)

    def prep_scaled(self, i, s, width=D):
        return self.nc.vector.scalar_tensor_tensor(out=self.hn[s][:, 0:width], in0=self.acc_tile(i, width), scalar=self.dinv[:, bass.ds(i, 1)],
                                                   in1=self.bias[:, 0:width], op0=ALU.mult, op1=ALU.add)

    def prep_half(self, i, s):
        return self.prep_scaled(i, s, D // 2)

    def relation_groups(self):
        def self_term(ps, i, s):
            return self.nc.scalar.activation(self.acc_tile(i), ps, ACT.Copy)

        def relations(g):
            def put(ps, i, s):
                return self.nc.scalar.activation(self.stage[s][:, g * 512:(g + 1) * 512], ps, ACT.Copy)
            return put

        groups = [([self.wself[:, k * D:(k + 1) * D] for k in range(KD)], D, self_term)]
        for g in range(REL * D // 512):
            groups.append(([self.wgnn[:, k * REL * D + g * 512:k * REL * D + (g + 1) * 512] for k in range(KD)], 512, relations(g)))
        return groups

    def node_groups(self, width):
        def put(ps, i, s):
            return self.nc.scalar.activation(self.acc_tile(i, width), ps, ACT.Identity, scale=self.dinv[:, bass.ds(i, 1)])
        return [([self.wsmall[:, k * width:(k + 1) * width] for k in range(KD)], width, put)]

    def project_groups(self):
        def put(ps, i, s):
            return self.nc.scalar.activation(self.acc_tile(i), ps, ACT.Copy)
        return [([self.wsmall[:, 0:D]], D, put)]

    def gate_groups(self):
        def put(ps, i, s):
            return self.nc.scalar.activation(self.scratch[:, bass.ds(i * E, E)], ps, ACT.Copy)
        return [([self.wgate[:, k * E:(k + 1) * E] for k in range(KD)], E, put)]

    def transform(self, prep, groups, table, relu=False, chunks=KD, split=False):
        nc = self.nc
        ng = len(groups)
        width = groups[-1][1]
        staged = table is self.tab_rel
        psT, psM = self.ps[0:2], self.ps[2:2 + ng]
        with self.stage_block() as (block, sem):
            rows_ready, turned, hT_ready, stored = (
                [sem(f"{n}{s}") for s in range(2)] for n in ("rows_ready", "turned", "hT_ready", "stored"))
            bank_full, bank_free = ([sem(f"{n}{g}") for g in range(ng)] for n in ("bank_full", "bank_free"))
            rest_ready, middle_ready = sem("rest_ready", "middle_ready")

            @block.vector
            def _(dve):
                def ready(i, s):
                    prep(i, s).then_inc(rows_ready[s], 1)

                def take(i, j, s):
                    dve.wait_ge(turned[s], j + 1)
                    if later(j):
                        dve.sem_inc(self.gate, 1)
                        dve.wait_ge(bank_full[ng - 1], i - 1)
                    o, p = self.hT[s][:, 0:chunks * P], psT[s][:, 0:chunks * P]
                    if relu:
                        nc.vector.tensor_single_scalar(o, p, 0.0, ALU.max).then_inc(hT_ready[s], 1)
                    else:
                        nc.vector.tensor_copy(o, p).then_inc(hT_ready[s], 1)

                def pair(j):
                    ready(j * 2 + 1, 1)
                    take(j * 2, j, 0)
                    ready(j * 2 + 2, 0)
                    take(j * 2 + 1, j, 1)

                ready(0, 0)
                pair(0)
                with dve.Fori(1, TILES // 2 - 1) as j:
                    pair(j)
                ready(TILES - 1, 1)
                take(TILES - 2, TILES // 2 - 1, 0)
                take(TILES - 1, TILES // 2 - 1, 1)

            @block.gpsimd
            def _(pool):
                if not split:
                    return
                with pool.Fori(0, TILES // 2) as j:
                    for s in range(2):
                        i = j * 2 + s
                        rest = self.scratch[:, s * D:s * D + width]
                        high, middle, low = (p[:, bass.ds(i * D, width)] for p in self.parts)
                        pool.wait_ge(bank_free[0], i + 1)
                        pool.sem_inc(self.gate, 1)
                        nc.gpsimd.tensor_tensor(rest, self.acc_tile(i, width), high, ALU.subtract).then_inc(rest_ready, 1)
                        pool.wait_ge(rest_ready, i + 1)
                        pool.sem_inc(self.gate, 1)
                        nc.gpsimd.tensor_copy(middle, rest).then_inc(middle_ready, 1)
                        pool.wait_ge(middle_ready, i + 1)
                        pool.sem_inc(self.gate, 1)
                        nc.gpsimd.tensor_tensor(low, rest, middle, ALU.subtract)

            @block.tensor
            def _(pe):
                def turn(j, s):
                    pe.wait_ge(rows_ready[s], j + 1)
                    for k in range(chunks):
                        last = nc.tensor.transpose(psT[s][:, k * P:(k + 1) * P], self.hn[s][:, k * P:(k + 1) * P], self.ident[:, :])
                    last.then_inc(turned[s], 1)

                def multiply(i, j, s):
                    pe.wait_ge(hT_ready[s], j + 1)
                    for g, (w, n, _) in enumerate(groups):
                        if later(i):
                            pe.wait_ge(bank_free[g], i)
                        for k in range(chunks):
                            last = nc.tensor.matmul(psM[g][:, 0:n], self.hT[s][:, k * P:(k + 1) * P], w[k],
                                                    start=(k == 0), stop=(k == chunks - 1))
                        last.then_inc(bank_full[g], 1)

                def pair(j):
                    turn(j, 1)
                    multiply(j * 2, j, 0)
                    turn(j + 1, 0)
                    multiply(j * 2 + 1, j, 1)

                turn(0, 0)
                pair(0)
                with pe.Fori(1, TILES // 2 - 1) as j:
                    pair(j)
                turn(TILES // 2 - 1, 1)
                multiply(TILES - 2, TILES // 2 - 1, 0)
                multiply(TILES - 1, TILES // 2 - 1, 1)

            @block.scalar
            def _(act):
                def pair(j):
                    for s in range(2):
                        i = j * 2 + s
                        for g, (_, n, put) in enumerate(groups):
                            if staged and g == 1 and later(j):
                                act.wait_ge(stored[s], j * 16)
                                act.sem_inc(self.gate, 1)
                            act.wait_ge(bank_full[g], i + 1)
                            act.sem_inc(self.gate, 1)
                            last = put(psM[g][:, 0:n], i, s)
                            if split:
                                last = nc.scalar.activation(self.parts[0][:, bass.ds(i * D, n)], psM[g][:, 0:n], ACT.Identity,
                                                            scale=self.dinv[:, bass.ds(i, 1)])
                            last.then_inc(bank_free[g], 1)

                pair(0)
                with act.Fori(1, TILES // 2) as j:
                    pair(j)

            @block.sync
            def _(sp):
                if table is None:
                    return
                with sp.Fori(0, TILES // 2) as j:
                    for s in range(2):
                        i = j * 2 + s
                        for g in range(ng):
                            sp.wait_ge(bank_free[g], i + 1)
                            sp.sem_inc(self.gate, 1)
                        if staged:
                            rows = table[bass.ds(i * (P * REL), P * REL), :].rearrange("(p r) d -> p (r d)", r=REL)
                            sp.dma_start(rows, self.stage[s]).then_inc(stored[s], 16)
                        else:
                            sp.dma_start(table[bass.ds(i * P, P), :], self.acc_tile(i, width)).then_inc(stored[s], 16)
                for s in range(2):
                    sp.wait_ge(stored[s], TILES // 2 * 16)

    def aggregate(self, table, gidx, width, count=False, counted=False):
        nc = self.nc
        wide = width + 1 if count else width
        rounds = PAIRS // GSLOTS
        with self.stage_block() as (block, sem):
            idx_ready, onehot_ready, summed, added = (
                [sem(f"{n}{s}") for s in range(GSLOTS)] for n in ("idx_ready", "onehot_ready", "summed", "added"))
            product_full, product_added = sem("product_full", "product_added")
            gathers = self.regathered if counted else self.gathered
            gathered, before = [g.sem for g in gathers], [g.base for g in gathers]
            for g in gathers:
                g.base += 16 * rounds

            @block.scalar
            def _(act):
                with self.exact_counts(act, counted, False):
                    def round_(i):
                        for s in range(GSLOTS):
                            if later(i):
                                act.wait_ge(gathered[s], i * 16 + before[s])
                                act.sem_inc(self.gate, 1)
                            nc.scalar.activation(self.idx[s][:, :], gidx[:, bass.ds(i * GSLOTS + s, 1)], ACT.Copy).then_inc(idx_ready[s], 1)

                    round_(0)
                    with act.Fori(1, rounds) as i:
                        round_(i)

            @block.gpsimd
            def _(pool):
                with self.exact_counts(pool, counted, False):
                    def round_(i):
                        for s in range(GSLOTS):
                            if later(i):
                                pool.wait_ge(summed[s], i)
                                pool.sem_inc(self.gate, 1)
                            pool.wait_ge(idx_ready[s], i + 1)
                            pool.sem_inc(self.gate, 1)
                            nc.gpsimd.indirect_dma_start(self.rowbuf[s][:, 0:width], None, table,
                                                         bass.IndirectOffsetOnAxis(ap=self.idx[s][:, :], axis=0)).then_inc(gathered[s], 16)

                    round_(0)
                    with pool.Fori(1, rounds) as i:
                        round_(i)

            @block.vector
            def _(dve):
                with self.exact_counts(dve, counted, False):
                    half = GSLOTS // 2
                    cols = self.iota[:, 0:P].rearrange("p (s c) -> p s c", s=1).broadcast_to([P, half, P])

                    def onehots(at, k):
                        to = self.onehots[:, k * half * P:(k + 1) * half * P].rearrange("p (s c) -> p s c", s=half)
                        dst = self.rel[:, bass.ds(at + k * half, half)].rearrange("p (s c) -> p s c", c=1).broadcast_to([P, half, P])
                        nc.vector.tensor_tensor(to, cols, dst, ALU.is_equal).then_inc(onehot_ready[k], 1)

                    def add(at, n, s, first=False):
                        to = self.acc[:, bass.ds(dve.value_load(self.bucket[0:1, bass.ds(at + s, 1)]), wide)]
                        dve.wait_ge(summed[s], n)
                        if not first:
                            dve.wait_ge(added[s - 1], n if s else n - 1)
                        nc.vector.tensor_tensor(to, to, self.ps[s][:, 0:wide], ALU.add).then_inc(added[s], 1)

                    def round_(at, n, first=False):
                        for k in range(2):
                            onehots(at, k)
                            for s in range(half):
                                if k:
                                    add(at, n, s, first and s == 0)
                                elif not first:
                                    add(at - GSLOTS, n - 1, half + s)

                    round_(0, 1, first=True)
                    with dve.Fori(2, rounds + 1) as n:
                        round_(dve.snap(n * GSLOTS - GSLOTS), n)
                    for s in range(half, GSLOTS):
                        add(PAIRS - GSLOTS, rounds, s)
                if counted:
                    with self.exact_counts(dve, counted, True):
                        with dve.Fori(0, TILES // 2) as j:
                            for s in range(2):
                                b = j * 2 + s
                                dve.wait_ge(product_full, b + 1)
                                dve.sem_inc(self.gate, 1)
                                nc.vector.tensor_tensor(self.acc_tile(b, width), self.acc_tile(b, width), self.ps[s][:, 0:width],
                                                        ALU.add).then_inc(product_added, 1)

            @block.tensor
            def _(pe):
                with self.exact_counts(pe, counted, False):
                    def round_(i):
                        for s in range(GSLOTS):
                            if s % (GSLOTS // 2) == 0:
                                pe.wait_ge(onehot_ready[s // (GSLOTS // 2)], i + 1)
                                pe.sem_inc(self.gate, 1)
                            if later(i):
                                pe.wait_ge(added[s], i)
                                pe.sem_inc(self.gate, 1)
                            pe.wait_ge(gathered[s], i * 16 + (before[s] + 16))
                            nc.tensor.matmul(self.ps[s][:, 0:wide], self.onehots[:, s * P:(s + 1) * P], self.rowbuf[s][:, 0:wide],
                                             start=True, stop=True).then_inc(summed[s], 1)

                    round_(0)
                    with pe.Fori(1, rounds) as i:
                        round_(i)
                if counted:
                    with self.exact_counts(pe, counted, True):
                        def product(b, s):
                            if later(b) and not (isinstance(b, int) and b < 2):
                                pe.wait_ge(product_added, b - 1)
                            for g in range(TILES):
                                counts = self.counts[:, bass.ds(b * NPAD + g * P, P)]
                                for k, part in enumerate(self.parts):
                                    last = nc.tensor.matmul(self.ps[s][:, 0:width], counts, part[:, g * D:g * D + width],
                                                            start=(g == 0 and k == 0), stop=(g == TILES - 1 and k == PARTS - 1))
                            last.then_inc(product_full, 1)

                        for s in range(2):
                            product(s, s)
                        with pe.Fori(1, TILES // 2) as j:
                            for s in range(2):
                                product(j * 2 + s, s)
    @contextmanager
    def exact_counts(self, eng, counted, exact):
        if not counted:
            yield
            return
        uncounted = eng.value_load(self.uncounted[0:1, 0:1], min_val=0, max_val=1)
        with eng.If(uncounted == (0 if exact else 1)):
            yield

    def count_matrix(self):
        nc = self.nc
        at = self.slots[:, :]
        src_hots = [at[:, s * WINDOW * P // 2:(s + 1) * WINDOW * P // 2].bitcast(F16) for s in range(2)]
        pair_hots = [self.free[:, s * NPAD // 2:(s + 1) * NPAD // 2].bitcast(F16) for s in range(HOTS)]
        bucket = self.free[:, HOTS * NPAD // 2:HOTS * NPAD // 2 + PAIRS]
        places = self.scratch[:, 0:NPAD // 2].bitcast(F16)
        src_low, key = (self.scratch[:, NPAD // 2 + k * PAIRS:NPAD // 2 + (k + 1) * PAIRS] for k in range(2))
        tmp, row = self.acc[:, 0:PAIRS], self.acc[0:1, PAIRS:2 * PAIRS]
        whole = self.acc[:, 2 * PAIRS:3 * PAIRS].bitcast(I32)
        edge_key = [self.acc[:, 3 * PAIRS + s * WINDOW:3 * PAIRS + (s + 1) * WINDOW] for s in range(2)]
        off = self.acc[:, 3 * PAIRS + 2 * WINDOW:3 * PAIRS + 3 * WINDOW]
        bucket_no = self.acc[:, 4 * PAIRS:4 * PAIRS + TILES]
        first = self.column[:, 2:3]
        part_no = self.column[:, 3:4]
        with self.stage_block() as (block, sem):
            link, places_ready, row_ready, spread, first_ready, turned, keyed, src_hot, pair_hot, summed, bank_full, bank_out = sem(
                "link", "places_ready", "row_ready", "spread", "first_ready", "turned", "keyed", "src_hot", "pair_hot", "summed",
                "bank_full", "bank_out")
            BANKS = NPAD // 512

            @block.gpsimd
            def _(pool):
                nc.gpsimd.iota(places, [[1, NPAD]], base=-MID, channel_multiplier=0,
                               allow_small_or_imprecise_dtypes=True).then_inc(places_ready, 1)
                nc.gpsimd.iota(bucket_no, [[ACCW, TILES]], base=0, channel_multiplier=0,
                               allow_small_or_imprecise_dtypes=True).then_inc(places_ready, 1)
                nc.gpsimd.iota(part_no, [[0, 1]], base=0, channel_multiplier=ACCW,
                               allow_small_or_imprecise_dtypes=True).then_inc(places_ready, 1)

            @block.vector
            def _(dve):
                v = nc.vector
                step = Chain(dve, link)
                v.tensor_copy(row, self.bucket[:, :]).then_inc(row_ready, 1)
                src = self.gidx[1][:, :]
                step(v.tensor_copy(whole, src))
                step(v.tensor_single_scalar(whole, whole, 7, ALU.arith_shift_right))
                step(v.tensor_copy(tmp, whole))
                step(v.scalar_tensor_tensor(out=src_low, in0=tmp, scalar=-float(P), in1=src, op0=ALU.mult, op1=ALU.add))
                step(v.scalar_tensor_tensor(out=key, in0=tmp, scalar=float(P), in1=self.rel[:, :], op0=ALU.mult, op1=ALU.add))
                step(v.tensor_single_scalar(key, key, -float(MID), ALU.add))
                step(v.tensor_scalar(tmp, self.rel[:, :], 0.0, FAR, ALU.is_lt, ALU.mult))
                step(v.tensor_tensor(key, key, tmp, ALU.add))
                step(v.tensor_scalar(tmp, self.rel[:, :], float(P), FAR, ALU.is_ge, ALU.mult))
                step(v.tensor_tensor(key, key, tmp, ALU.add))
                dve.wait_ge(places_ready, 3)
                dve.wait_ge(spread, 1)
                step(v.tensor_copy(bucket, self.ps[7][:, 0:PAIRS]))
                step(v.tensor_scalar(tmp, bucket, part_no, None, ALU.is_lt))
                step(v.tensor_reduce(first, tmp, AX.X, ALU.add))
                v.tensor_single_scalar(first, first, float(PAIRS - WINDOW), ALU.min).then_inc(first_ready, 1)
                dve.wait_ge(turned, 1)
                step(v.tensor_copy(self.window[:, :], self.ps[6][0:1, 0:TILES]))
                places_low = self.iota[:, 0:P].rearrange("p (s c) -> p s c", s=1).broadcast_to([P, WINDOW, P])

                def window(b, s):
                    at = dve.value_load(self.window[0:1, bass.ds(b, 1)], min_val=0, max_val=PAIRS - WINDOW)
                    low = src_low[:, bass.ds(at, WINDOW)].rearrange("p (s c) -> p s c", c=1).broadcast_to([P, WINDOW, P])
                    v.tensor_tensor(src_hots[s].rearrange("p (s c) -> p s c", s=WINDOW), places_low, low, ALU.is_equal).then_inc(src_hot, 1)
                    v.tensor_scalar(off, bucket[:, bass.ds(at, WINDOW)], bucket_no[:, bass.ds(b, 1)], FAR,
                                    ALU.not_equal, ALU.mult).then_inc(keyed, 1)
                    dve.wait_ge(keyed, b * 2 + 1)
                    dve.sem_inc(self.gate, 1)
                    v.tensor_tensor(edge_key[s], key[:, bass.ds(at, WINDOW)], off, ALU.add).then_inc(keyed, 1)
                    dve.wait_ge(keyed, b * 2 + 2)
                    for k in range(WINDOW):
                        before = k - HOTS if k >= HOTS else max(n for n in range(WINDOW) if n % HOTS == k) - WINDOW
                        if later(b) or before >= 0:
                            dve.wait_ge(summed, b * WINDOW + (before + 1))
                            dve.sem_inc(self.gate, 1)
                        v.tensor_scalar(pair_hots[k % HOTS], places, edge_key[s][:, k:k + 1], None, ALU.is_equal).then_inc(pair_hot, 1)

                for s in range(2):
                    window(s, s)
                with dve.Fori(1, TILES // 2) as j:
                    for s in range(2):
                        window(j * 2 + s, s)

            @block.tensor
            def _(pe):
                t = nc.tensor
                pe.wait_ge(row_ready, 1)
                t.matmul(self.ps[7][:, 0:PAIRS], self.ones[0:1, :], row, start=True, stop=True).then_inc(spread, 1)
                pe.wait_ge(first_ready, 1)
                t.matmul(self.ps[6][0:1, 0:P], first, self.ident[:, :], start=True, stop=True).then_inc(turned, 1)

                def bucket_sums(b, s):
                    pe.wait_ge(src_hot, b + 1)
                    for k in range(WINDOW):
                        pe.wait_ge(pair_hot, b * WINDOW + (k + 1))
                        pe.sem_inc(self.gate, 1)
                        for g in range(BANKS):
                            if k == 0 and later(b):
                                pe.wait_ge(bank_out, b * BANKS + (g + 1 - BANKS))
                                pe.sem_inc(self.gate, 1)
                            last = t.matmul(self.ps[g][:, :], src_hots[s][:, k * P:(k + 1) * P], pair_hots[k % HOTS][:, g * 512:(g + 1) * 512],
                                            start=(k == 0), stop=(k == WINDOW - 1))
                            if k == WINDOW - 1 and g < BANKS - 1:
                                last.then_inc(bank_full, 1)
                        last.then_inc(summed, 1)

                for s in range(2):
                    bucket_sums(s, s)
                with pe.Fori(1, TILES // 2) as j:
                    for s in range(2):
                        bucket_sums(j * 2 + s, s)

            @block.scalar
            def _(act):
                with act.Fori(0, TILES) as b:
                    for g in range(BANKS):
                        if g < BANKS - 1:
                            act.wait_ge(bank_full, b * (BANKS - 1) + (g + 1))
                        else:
                            act.wait_ge(summed, b * WINDOW + WINDOW)
                        act.sem_inc(self.gate, 1)
                        nc.scalar.activation(self.counts[:, bass.ds(b * NPAD + g * 512, 512)], self.ps[g][:, :], ACT.Copy).then_inc(bank_out, 1)

    def degrees(self):
        nc = self.nc
        most = [self.scratch[0:1, k:k + 1] for k in range(2)]
        with self.stage_block() as (block, sem):
            link, degree, rooted, copied, ranked = sem("link", "degree", "rooted", "copied", "ranked")

            @block.vector
            def _(dve):
                v = nc.vector
                step = Chain(dve, link)
                counts = self.acc[:, :].rearrange("p (t w) -> p t w", w=ACCW)[:, :, D:ACCW]
                self.inverse_root(dve, step, self.dinv, counts, 1.0, degree, rooted)
                step(v.tensor_copy(self.r3[:, :].rearrange("p (t w) -> p t w", w=1), counts))
                v.tensor_reduce(self.column[:, 0:1], self.r3[:, :], AX.X, ALU.max).then_inc(copied, 1)
                dve.wait_ge(ranked, 1)
                step(v.tensor_reduce(most[0], self.ps[0][0:1, 0:TILES], AX.X, ALU.max))
                step(v.tensor_reduce(most[1], self.ps[1][0:1, 0:P], AX.X, ALU.max))
                step(v.tensor_single_scalar(most[0], most[0], float(WINEDGES), ALU.is_gt))
                step(v.tensor_single_scalar(most[1], most[1], float(FULLCOUNT), ALU.is_gt))
                step(v.tensor_tensor(most[0], most[0], most[1], ALU.max))
                step(v.tensor_copy(self.uncounted[:, :], most[0]))

            @block.tensor
            def _(pe):
                pe.wait_ge(copied, 1)
                nc.tensor.matmul(self.ps[0][0:1, 0:TILES], self.ones[:, 0:1], self.r3[:, :], start=True, stop=True)
                nc.tensor.matmul(self.ps[1][0:1, 0:P], self.column[:, 0:1], self.ident[:, :], start=True, stop=True).then_inc(ranked, 1)

            @block.scalar
            def _(act):
                self.root(act, degree, rooted)

    def load_experts(self, m):
        a, pre = self.a, f"L{m}_ffn_"
        with self.stage_block() as (block, _):
            @block.scalar
            def _(act):
                for e in range(E):
                    act.dma_start(self.w1[:, e * W1E:(e + 1) * W1E].rearrange("p (k h) -> p k h", k=KD),
                                  a[pre + "W1t"][e].rearrange("(k p) h -> p k h", p=P)).then_inc(self.experts_loaded, 16)
                    act.dma_start(self.w2[:, e * W2E:(e + 1) * W2E].rearrange("p (c d) -> p c d", c=HC),
                                  a[pre + "W2t"][e].rearrange("(c p) d -> p c d", p=P)).then_inc(self.experts_loaded, 16)

    def route(self, m):
        nc, n = self.nc, TILES * E
        sc = self.scratch
        names = ("eq", "oh1", "oh2", "m2nd", "both", "tot", "sa", "sb", "excl", "pos")
        eq, oh1, oh2, rest, both, tot, sa, sb_, excl, pos = (sc[:, (k + 1) * n:(k + 2) * n] for k in range(len(names)))
        L = sc[:, 0:n]
        at = (len(names) + 1) * n
        m1, m2, i1, i2, t1, t2 = (sc[:, at + k * TILES:at + (k + 1) * TILES] for k in range(6))
        at += 6 * TILES
        nt, ea, eb, ts, gb = (sc[:, at + k * E:at + (k + 1) * E] for k in range(5))
        at += 5 * E
        ni = sc[:, at:at + E].bitcast(I32)
        row = [sc[0:1, at + E + k * MTILES:at + E + (k + 1) * MTILES] for k in range(2)]
        g3 = lambda t: t.rearrange("p (t e) -> p t e", e=E)
        over = lambda t: t.rearrange("p (t o) -> p t o", o=1).broadcast_to([P, TILES, E])
        per = lambda t: t.rearrange("p (o e) -> p o e", o=1).broadcast_to([P, TILES, E])
        with self.stage_block() as (block, sem):
            link, loaded, to_exp, exp_done, masked, ranked = sem("link", "loaded", "to_exp", "exp_done", "masked", "ranked")

            @block.sync
            def _(sp):
                sp.dma_start(gb, self.spread(self.a[("L0_ffn_bg", "L1_ffn_br")[m]])).then_inc(loaded, 16)

            @block.scalar
            def _(act):
                act.wait_ge(to_exp, 1)
                if m == 0:
                    nc.scalar.activation(t1, t1, ACT.Exp).then_inc(exp_done, 1)
                else:
                    nc.scalar.activation(L, L, ACT.Exp).then_inc(exp_done, 1)

            @block.vector
            def _(dve):
                v = nc.vector
                step = Chain(dve, link)

                def best(of, value, place, onehot):
                    step(v.tensor_reduce(value, g3(of), AX.X, ALU.max))
                    step(v.tensor_tensor(g3(eq), g3(of), over(value), ALU.is_equal))
                    step(v.tensor_tensor(eq, eq, self.iota_e[:, :], ALU.mult))
                    step(v.tensor_reduce(place, g3(eq), AX.X, ALU.min))
                    step(v.tensor_tensor(g3(onehot), g3(self.iota_e[:, :]), over(place), ALU.is_equal))

                dve.wait_ge(loaded, 16)
                step(v.tensor_tensor(g3(L), g3(L), per(gb), ALU.add))
                if m == 1:
                    step(v.tensor_reduce(m1, g3(L), AX.X, ALU.max))
                    v.tensor_tensor(g3(L), g3(L), over(m1), ALU.subtract).then_inc(to_exp, 1)
                    dve.wait_ge(exp_done, 1)
                    step(v.tensor_reduce(t1, g3(L), AX.X, ALU.add))
                    step(v.reciprocal(t2, t1))
                    step(v.tensor_tensor(g3(L), g3(L), over(t2), ALU.mult))
                best(L, m1, i1, oh1)
                step(v.scalar_tensor_tensor(out=rest, in0=oh1, scalar=NEG, in1=L, op0=ALU.mult, op1=ALU.add))
                best(rest, m2, i2, oh2)
                v.tensor_tensor(both, oh1, oh2, ALU.add).then_inc(masked, 1)
                w1, w2 = self.wcomb[:, 0:TILES], self.wcomb[:, TILES:2 * TILES]
                if m == 0:
                    v.tensor_tensor(t1, m2, m1, ALU.subtract).then_inc(to_exp, 1)
                    dve.wait_ge(exp_done, 1)
                    step(v.tensor_single_scalar(t2, t1, 1.0, ALU.add))
                    step(v.reciprocal(w1, t2))
                    step(v.tensor_tensor(w2, w1, t1, ALU.mult))
                else:
                    step(v.tensor_tensor(t1, m1, m2, ALU.add))
                    step(v.reciprocal(t2, t1))
                    step(v.tensor_tensor(w1, m1, t2, ALU.mult))
                    step(v.tensor_tensor(w2, m2, t2, ALU.mult))
                dve.wait_ge(ranked, 1)
                step(v.tensor_copy(tot, self.ps[1][:, 0:n]))
                a, b, d = tot, sa, 1
                while d < TILES:
                    step(v.tensor_copy(b[:, 0:d * E], a[:, 0:d * E]))
                    step(v.tensor_tensor(b[:, d * E:n], a[:, d * E:n], a[:, 0:n - d * E], ALU.add))
                    a, b, d = b, (sb_ if b is sa else sa), 2 * d
                step(v.tensor_tensor(excl, a, tot, ALU.subtract))
                step(v.tensor_single_scalar(ni, a[:, n - E:n], float(P - 1), ALU.add))
                step(v.tensor_single_scalar(ni, ni, 7, ALU.arith_shift_right))
                step(v.tensor_copy(nt, ni))
                a, b, d = nt, ea, 1
                while d < E:
                    step(v.tensor_copy(b[:, 0:d], a[:, 0:d]))
                    step(v.tensor_tensor(b[:, d:E], a[:, d:E], a[:, 0:E - d], ALU.add))
                    a, b, d = b, (eb if b is ea else ea), 2 * d
                step(v.tensor_tensor(ts, a, nt, ALU.subtract))
                step(v.tensor_single_scalar(ts, ts, float(P), ALU.mult))
                step(v.tensor_tensor(pos, excl, self.ps[0][:, 0:n], ALU.add))
                step(v.tensor_tensor(g3(pos), g3(pos), per(ts), ALU.add))
                for k, oh in enumerate((oh1, oh2)):
                    step(v.tensor_tensor(eq, oh, pos, ALU.mult))
                    step(v.tensor_reduce(t1, g3(eq), AX.X, ALU.add))
                    step(v.tensor_copy(self.spos[:, k * TILES:(k + 1) * TILES], t1))
                step(v.tensor_scalar(row[0], self.iota[0:1, 0:MTILES], a[0:1, 0:1], None, ALU.is_ge))
                for e in range(1, E - 1):
                    step(v.scalar_tensor_tensor(out=row[e % 2], in0=self.iota[0:1, 0:MTILES], scalar=a[0:1, e:e + 1],
                                                in1=row[(e - 1) % 2], op0=ALU.is_ge, op1=ALU.add))
                step(v.tensor_copy(self.texp[:, :], row[(E - 2) % 2]))

            @block.tensor
            def _(pe):
                pe.wait_ge(masked, 1)
                nc.tensor.matmul(self.ps[0][:, 0:n], self.tri[:, :], both, start=True, stop=True)
                nc.tensor.matmul(self.ps[1][:, 0:n], self.ones[:, :], both, start=True, stop=True).then_inc(ranked, 1)

    def dispatch(self):
        nc = self.nc
        with self.stage_block() as (block, _):
            sent = self.sent.sem
            self.sent.base += 16 * TOPK * TILES

            @block.gpsimd
            def _(pool):
                for k in range(TOPK):
                    for t in range(TILES):
                        c = k * TILES + t
                        nc.gpsimd.indirect_dma_start(self.xd, bass.IndirectOffsetOnAxis(ap=self.spos[:, c:c + 1], axis=0),
                                                     self.acc[:, t * ACCW:t * ACCW + D], None).then_inc(sent, 16)
                pool.wait_ge(sent, self.sent.base)

    def experts(self, m):
        nc, a = self.nc, self.a
        affine = m == 1
        func = (ACT.Relu, ACT.Gelu)[m]
        psH, psX, psG, psY = self.ps[0:2], self.ps[2], self.ps[3:5], self.ps[5:7]
        with self.stage_block() as (block, sem):
            brow = [self.slots[:, s * (H + D):(s + 1) * (H + D)] for s in range(2)]
            rows = [self.slots[:, 2 * (H + D) + s * D:2 * (H + D) + (s + 1) * D] for s in range(4)]
            xin, yout = rows[0:2], rows[2:4]
            h, hT, xT = self.scratch[:, 0:H], self.scratch[:, H:2 * H], self.hT[0][:, :]
            lng, lnb = (self.hn[0][:, k * E * KD:(k + 1) * E * KD] for k in range(2))
            x_in, bias_in, y_ready = ([sem(f"{k}{s}") for s in range(2)] for k in ("x_in", "bias_in", "y_ready"))
            y_stored, before = [y.sem for y in self.y_stored], self.y_stored[0].base
            for y in self.y_stored:
                y.base += MTILES // 2 * 16
            x_turned, xT_ready, h_full, h_ready, h_turned, hT_ready, y_full, ln_loaded = (
                sem(k) for k in ("x_turned", "xT_ready", "h_full", "h_ready", "h_turned", "hT_ready", "y_full", "ln_loaded"))

            def expert(eng, i):
                return eng.value_load(self.texp[0:1, bass.ds(i, 1)], min_val=0, max_val=E - 1)

            @block.sync
            def _(sp):
                if affine:
                    sp.dma_start(lng, a["L1_ffn_lngT"]).then_inc(ln_loaded, 16)
                    sp.dma_start(lnb, a["L1_ffn_lnbT"]).then_inc(ln_loaded, 16)

                def fetch(i, j, s):
                    e = expert(sp, i)
                    if later(j):
                        sp.wait_ge(x_turned, i - 1)
                        sp.sem_inc(self.gate, 1)
                    sp.dma_start(xin[s][:, 0:D], self.xd[bass.ds(i * P, P), :]).then_inc(x_in[s], 16)
                    if later(j):
                        sp.wait_ge(y_ready[s], j)
                        sp.sem_inc(self.gate, 1)
                    sp.dma_start(brow[s][:, :], a[f"L{m}_ffn_b12"][bass.ds(e, 1), :].to_broadcast([P, H + D])).then_inc(bias_in[s], 16)

                for s in range(2):
                    fetch(s, 0, s)
                with sp.Fori(1, MTILES // 2) as j:
                    for s in range(2):
                        fetch(j * 2 + s, j, s)

            @block.gpsimd
            def _(pool):
                with pool.Fori(0, MTILES // 2) as j:
                    for s in range(2):
                        pool.wait_ge(y_ready[s], j + 1)
                        pool.sem_inc(self.gate, 1)
                        pool.dma_start(self.yd[bass.ds((j * 2 + s) * P, P), :], yout[s][:, 0:D]).then_inc(y_stored[s], 16)
                for s in range(2):
                    pool.wait_ge(y_stored[s], self.y_stored[s].base)

            @block.tensor
            def _(pe):
                def turn_x(j, s):
                    pe.wait_ge(x_in[s], j * 16 + 16)
                    for k in range(KD):
                        last = nc.tensor.transpose(psX[:, k * P:(k + 1) * P], xin[s][:, k * P:(k + 1) * P], self.ident[:, :])
                    last.then_inc(x_turned, 1)

                def up(i):
                    e = expert(pe, i)
                    pe.wait_ge(xT_ready, i + 1)
                    pe.sem_inc(self.gate, 1)
                    for b in range(HB):
                        for k in range(KD):
                            last = nc.tensor.matmul(psH[b][:, :], xT[:, k * P:(k + 1) * P],
                                                    self.w1[:, bass.ds(e * W1E + (k * H + b * 512), 512)],
                                                    start=(k == 0), stop=(k == KD - 1))
                    last.then_inc(h_full, 1)

                def turn_h(i):
                    pe.wait_ge(h_ready, i + 1)
                    for c in range(HC):
                        last = nc.tensor.transpose(psG[c // 4][:, (c % 4) * P:(c % 4 + 1) * P], h[:, c * P:(c + 1) * P], self.ident[:, :])
                    last.then_inc(h_turned, 1)

                def down(i, s):
                    e = expert(pe, i)
                    pe.wait_ge(hT_ready, i * 2 + 2)
                    pe.sem_inc(self.gate, 1)
                    for c in range(HC):
                        last = nc.tensor.matmul(psY[s][:, 0:D], hT[:, c * P:(c + 1) * P], self.w2[:, bass.ds(e * W2E + c * D, D)],
                                                start=(c == 0), stop=(c == HC - 1))
                    last.then_inc(y_full, 1)

                pe.wait_ge(self.experts_loaded, 16 * 2 * E * (m + 1))
                turn_x(0, 0)
                up(0)
                turn_x(0, 1)
                turn_h(0)
                with pe.Fori(0, MTILES // 2 - 1) as j:
                    i = j * 2
                    up(i + 1)
                    turn_x(j + 1, 0)
                    down(i, 0)
                    turn_h(i + 1)
                    up(i + 2)
                    turn_x(j + 1, 1)
                    down(i + 1, 1)
                    turn_h(i + 2)
                up(MTILES - 1)
                down(MTILES - 2, 0)
                turn_h(MTILES - 1)
                down(MTILES - 1, 1)

            @block.vector
            def _(dve):
                def take_x(i):
                    e = expert(dve, i) if affine else None
                    dve.wait_ge(x_turned, i + 1)
                    if affine:
                        dve.sem_inc(self.gate, 1)
                    for k in range(KD):
                        o, p = xT[:, k * P:(k + 1) * P], psX[:, k * P:(k + 1) * P]
                        if affine:
                            last = nc.vector.tensor_scalar(o, p, lng[:, bass.ds(e * KD + k, 1)], lnb[:, bass.ds(e * KD + k, 1)], ALU.mult, ALU.add)
                        else:
                            last = nc.vector.tensor_copy(o, p)
                    last.then_inc(xT_ready, 1)

                def take_h(i, j, s):
                    dve.wait_ge(bias_in[s], j * 16 + 16)
                    dve.sem_inc(self.gate, 1)
                    dve.wait_ge(h_full, i + 1)
                    for b in range(HB):
                        last = nc.vector.tensor_tensor(h[:, b * 512:(b + 1) * 512], psH[b][:, :], brow[s][:, b * 512:(b + 1) * 512], ALU.add)
                    last.then_inc(h_ready, 1)

                def take_y(i, j, s):
                    if later(j):
                        dve.wait_ge(y_stored[s], j * 16 + before)
                        dve.sem_inc(self.gate, 1)
                    dve.wait_ge(y_full, i + 1)
                    nc.vector.tensor_tensor(yout[s][:, 0:D], psY[s][:, 0:D], brow[s][:, H:H + D], ALU.add).then_inc(y_ready[s], 1)

                def pair(j):
                    i = j * 2
                    take_h(i + 1, j, 1)
                    take_x(i + 2)
                    take_y(i, j, 0)
                    take_h(i + 2, j + 1, 0)
                    take_x(i + 3)
                    take_y(i + 1, j, 1)

                if affine:
                    dve.wait_ge(ln_loaded, 32)
                take_x(0)
                take_h(0, 0, 0)
                take_x(1)
                pair(0)
                with dve.Fori(1, MTILES // 2 - 1) as j:
                    pair(j)
                take_h(MTILES - 1, MTILES // 2 - 1, 1)
                take_y(MTILES - 2, MTILES // 2 - 1, 0)
                take_y(MTILES - 1, MTILES // 2 - 1, 1)

            @block.scalar
            def _(act):
                def take_g(i, first=False):
                    act.wait_ge(h_turned, i + 1)
                    for b in range(2):
                        if not first and b == 0:
                            act.sem_inc(self.gate, 1)
                            act.wait_ge(y_full, i)
                        nc.scalar.activation(hT[:, b * 512:(b + 1) * 512], psG[b][:, :], func).then_inc(hT_ready, 1)

                take_g(0, True)
                with act.Fori(1, MTILES) as i:
                    take_g(i)

    def combine(self):
        nc = self.nc
        with self.stage_block() as (block, sem):
            added = sem("added")
            fetched, before = [g.sem for g in self.gathered], [g.base for g in self.gathered]
            for g in self.gathered:
                g.base += 16 * TOPK * TILES // GSLOTS

            @block.gpsimd
            def _(pool):
                for c in range(TOPK * TILES):
                    s = c % GSLOTS
                    if c >= GSLOTS:
                        pool.wait_ge(added, c - GSLOTS + 1)
                    nc.gpsimd.indirect_dma_start(self.rowbuf[s][:, 0:D], None, self.yd,
                                                 bass.IndirectOffsetOnAxis(ap=self.spos[:, c:c + 1], axis=0)).then_inc(fetched[s], 16)

            @block.vector
            def _(dve):
                for c in range(TOPK * TILES):
                    s, t = c % GSLOTS, c % TILES
                    dve.wait_ge(fetched[s], before[s] + 16 * (c // GSLOTS + 1))
                    if c >= TILES:
                        dve.wait_ge(added, c - TILES + 1)
                    x = self.x[:, t * D:(t + 1) * D]
                    nc.vector.scalar_tensor_tensor(out=x, in0=self.rowbuf[s][:, 0:D], scalar=self.wcomb[:, c:c + 1], in1=x,
                                                   op0=ALU.mult, op1=ALU.add).then_inc(added, 1)

    def moe(self, m):
        self.route(m)
        self.dispatch()
        self.experts(m)
        self.combine()

    def store_out(self):
        nc = self.nc
        with self.stage_block() as (block, sem):
            stored = sem("stored")

            @block.sync
            def _(sp):
                full = (TILES - 1) * P
                sp.dma_start(self.out[0:full, :].rearrange("(t p) d -> p t d", p=P),
                             self.x[:, 0:(TILES - 1) * D].rearrange("p (t d) -> p t d", d=D)).then_inc(stored, 16)
                sp.dma_start(self.out[full:NODES, :], self.x[0:LAST, (TILES - 1) * D:TILES * D]).then_inc(stored, 16)
                sp.wait_ge(stored, 32)


def kernel(**inputs):
    import numpy as np
    import concourse.bacc as bacc
    from concourse.bass_utils import run_bass_kernel_spmd

    given = {k: np.asarray(v) for k, v in inputs.items()}
    arrays = {k: given[k] for k in (
        "x", "src", "dst", "edge_type_8", "L0_gnn_W1", "L0_gnn_self_w1", "L0_gnn_b1", "L0_gnn_W2", "L0_gnn_self_w2",
        "L0_gnn_b2", "L0_ffn_bg", "L1_gnn_W1", "L1_gnn_b1", "L1_gnn_W2", "L1_gnn_b2", "L1_gnn_W3", "L1_gnn_b3",
        "L1_gnn_Wp", "L1_gnn_bp", "L1_ffn_Wr", "L1_ffn_br")}
    arrays["L0_ffn_WgT"] = given["L0_ffn_Wg"].T
    arrays["L0_ffn_W1t"] = given["L0_ffn_W1"].transpose(0, 2, 1)
    arrays["L0_ffn_W2t"] = given["L0_ffn_W2"].transpose(0, 2, 1)
    arrays["L1_ffn_W1t"] = given["L1_ffn_W1"]
    arrays["L1_ffn_W2t"] = given["L1_ffn_W2"]
    for m in range(2):
        arrays[f"L{m}_ffn_b12"] = np.concatenate([given[f"L{m}_ffn_b1"], given[f"L{m}_ffn_b2"]], axis=1)
    for k, name in (("g", "L1_ffn_ln_g"), ("b", "L1_ffn_ln_b")):
        arrays[f"L1_ffn_ln{k}T"] = given[name].reshape(E, KD, P).transpose(2, 0, 1).reshape(P, E * KD)
    arrays = {k: np.ascontiguousarray(v) for k, v in arrays.items()}
    nc = bacc.Bacc("TRN2", target_bir_lowering=False, num_devices=1)
    a = {k: nc.dram_tensor(f"in_{k}", v.shape, mybir.dt.from_np(v.dtype), kind="ExternalInput").ap() for k, v in arrays.items()}
    out = nc.dram_tensor("out", (NODES, D), F32, kind="ExternalOutput").ap()
    build(nc, a, out)
    r = run_bass_kernel_spmd(nc, [{f"in_{k}": v for k, v in arrays.items()}], core_ids=[0])
    return r.results[0]["out"]
```

```python
from contextlib import ExitStack, contextmanager

import concourse.bass as bass
from concourse import mybir

F32 = mybir.dt.float32
U32 = mybir.dt.uint32
F16 = mybir.dt.float16
BF16 = mybir.dt.bfloat16
F32R = mybir.dt.float32r
I32 = mybir.dt.int32
ALU = mybir.AluOpType
ACT = mybir.ActivationFunctionType
AX = mybir.AxisListType

P = 128
NODES = 2500
D = 256
KD = D // P
TILES = -(-NODES // P)
NPAD = TILES * P
LAST = NODES - (TILES - 1) * P
EDGES = 40000
ETILES = -(-EDGES // P)
EFULL = EDGES // P
EREST = EDGES - EFULL * P
ECH = -(-ETILES // P)
ELASTCH = ETILES - (ECH - 1) * P
REL = 8
GSLOTS = 8
PAIRS = -(-(ETILES + TILES - 1) // GSLOTS) * GSLOTS
WINDOW = 18
WINEDGES = WINDOW * P - (P - 1)
FULLCOUNT = 2048
HOTS = 5
PARTS = 3
MID = NPAD // 2
FAR = 1.0e5
ACCW = D + 1
E = 8
H = 1024
HC = H // P
HB = H // 512
TOPK = 2
MTILES = (NPAD * TOPK + E * (P - 1)) // P
MTILES += MTILES % 2
SLOTS = MTILES * P
W1E = KD * H
W2E = HC * D
WE = W1E + W2E
RING = E // 2
EPS = 1e-5
NEG = -3.0e38
RELW = KD * (REL + 1) * D
SCRATCH = 4 * D + H
SLOTCOLS = max(GSLOTS * (ACCW + P), 2 * H + 2 * D)
PACE = 3
SET = 44


def later(i):
    return not (isinstance(i, int) and i == 0)


class Chain:

    def __init__(self, eng, sem, base=0):
        self.eng, self.sem, self.base, self.n = eng, sem, base, 0

    def __call__(self, ins):
        ins.then_inc(self.sem, 1)
        self.n += 1
        self.eng.wait_ge(self.sem, self.base + self.n)


class Count:

    def __init__(self, sem):
        self.sem, self.base = sem, 0


def build(nc, a, out):
    with ExitStack() as ctx:
        Program(nc, a, out, ctx).run()


class Program:
    def __init__(self, nc, a, out, ctx):
        self.nc, self.a, self.out = nc, a, out

        def sb(name, shape, dt=F32):
            return ctx.enter_context(nc.sbuf_tensor(name, shape, dt))

        self.x = sb("x_all", [P, TILES * D])
        self.acc = sb("acc", [P, TILES * ACCW])
        self.wsmall = sb("w_small", [P, KD * D])
        self.wgate = sb("w_gate", [P, KD * E])
        self.ident = sb("ident", [P, P])
        self.tri = sb("tri", [P, P])
        self.ones = sb("ones", [P, P])
        self.iota = sb("iota", [P, PAIRS])
        self.gidx = [sb("gidx_relation", [P, PAIRS]), sb("gidx_node", [P, PAIRS])]
        self.rel = sb("dst_in_bucket", [P, PAIRS])
        self.bucket = sb("bucket_of_pair", [1, PAIRS], I32)
        self.dinv = sb("dinv", [P, TILES])
        self.bias = sb("bias_row", [P, D])
        self.hn = [sb(f"hn{s}", [P, D]) for s in range(2)]
        self.hT = [sb(f"hT{s}", [P, D]) for s in range(2)]
        self.mv = sb("mean_var", [P, TILES * 2])
        self.rstd = sb("rstd", [P, TILES])
        self.r2, self.r3 = sb("root_of", [P, TILES]), sb("root", [P, TILES])
        self.wcomb = sb("w_comb", [P, 2 * TILES])
        self.spos = sb("slot_pos", [P, 2 * TILES], U32)
        self.texp = sb("tile_expert", [1, MTILES + E], I32)
        self.window = sb("window", [1, TILES], I32)
        self.uncounted = sb("uncounted", [1, 1], I32)
        self.column = sb("column", [P, 4])
        self.idx = [sb(f"idx{s}", [P, 1], U32) for s in range(GSLOTS)]
        self.iota_e = sb("iota_e", [P, TILES * E])
        self.ps = [ctx.enter_context(nc.psum_tensor(f"ps{b}", [P, 512], F32)) for b in range(8)]

        self.gate = ctx.enter_context(nc.semaphore("gate"))
        self.experts_loaded = ctx.enter_context(nc.semaphore("experts_loaded"))
        self.gathered = [Count(ctx.enter_context(nc.semaphore(f"gathered{s}"))) for s in range(GSLOTS)]
        self.regathered = [Count(ctx.enter_context(nc.semaphore(f"regathered{s}"))) for s in range(GSLOTS)]
        self.refilled = Count(ctx.enter_context(nc.semaphore("refilled")))
        self.sent = Count(ctx.enter_context(nc.semaphore("sent")))
        self.sets = [[ctx.enter_context(nc.semaphore(f"set{k}_{n}")) for n in range(SET)] for k in range(2)]
        self.turn = 0
        self.scopes = 0
        self.pace = lambda: None

        def dram(name, shape):
            return nc.dram_tensor(name, shape, F32, kind="Internal").ap()

        self.tab_rel = dram("tab_rel", [NPAD * REL, D])
        self.tab_node = dram("tab_node", [NPAD, D])
        self.tab_half = dram("tab_half", [NPAD, D // 2])
        self.xd = dram("x_dispatched", [SLOTS, D])
        self.yd = dram("y_dispatched", [SLOTS, D])

    @contextmanager
    def stage_block(self):
        own, other = self.sets[self.turn], self.sets[1 - self.turn]
        self.turn = 1 - self.turn
        free = iter(own)
        with self.nc.Block() as block:
            @block.sync
            def _(sp):
                sp.sem_clear(range(other[0].num, other[-1].num + 1))

            yield block, lambda *names: [next(free) for _ in names] if len(names) != 1 else next(free)

    def scoped(self, ctx, name, cols):
        self.scopes += 1
        return ctx.enter_context(self.nc.sbuf_tensor(f"{name}_{self.scopes}", [P, cols], F32))

    @contextmanager
    def relational_memory(self):
        with ExitStack() as ctx:
            halves = self.scoped(ctx, "relation_halves", 2 * RELW + 4 * D)
            self.relw = [halves[:, k * RELW:(k + 1) * RELW] for k in range(2)]
            self.row_halves = [[halves[:, 2 * RELW + (s * 2 + k) * D:2 * RELW + (s * 2 + k + 1) * D].bitcast(F32R) for k in range(2)]
                               for s in range(2)]
            rest = self.scoped(ctx, "relation_rest", RING * 2 * WE - 2 * RELW - 4 * D)
            self.stage = [rest[:, s * REL * D:(s + 1) * REL * D] for s in range(2)]
            self.raw = rest[:, 2 * REL * D:2 * REL * D + RELW]
            self.rest = rest[:, 2 * REL * D + RELW:]
            yield

    @contextmanager
    def ring_memory(self):
        with ExitStack() as ctx:
            self.big = self.scoped(ctx, "ring", RING * 2 * WE)
            yield

    @contextmanager
    def count_memory(self):
        with ExitStack() as ctx:
            big = self.scoped(ctx, "counts", RING * 2 * WE)
            self.counts = big[:, 0:TILES * NPAD // 2].bitcast(F16)
            self.free = big[:, TILES * NPAD // 2:]
            self.parts = [self.free[:, k * TILES * D // 2:(k + 1) * TILES * D // 2].bitcast(BF16) for k in range(2)]
            yield

    @contextmanager
    def working(self):
        with ExitStack() as ctx:
            self.scratch = self.scoped(ctx, "scratch", SCRATCH)
            self.stats = self.scratch[:, 0:TILES * 6]
            slots = self.slots = self.scoped(ctx, "slots", SLOTCOLS)
            self.rowbuf = [slots[:, s * ACCW:(s + 1) * ACCW] for s in range(GSLOTS)]
            self.onehots = slots[:, GSLOTS * ACCW:GSLOTS * (ACCW + P)]
            self.low_part = slots[:, 0:TILES * D // 2].bitcast(BF16)
            yield

    def acc_tile(self, i, width=D):
        return self.acc[:, bass.ds(i * ACCW, width)]

    def x_tile(self, i):
        return self.x[:, bass.ds(i * D, D)]

    def run(self):
        a = self.a
        with self.relational_memory(), self.working():
            self.constants()
            self.edge_pairs(self.relational(a["L0_gnn_W1"], a["L0_gnn_self_w1"]))
            self.statistics()
            self.transform(self.prep_norm, self.relation_groups(), self.tab_rel, halves=True)
            self.aggregate(self.tab_rel, self.gidx[0], D,
                           self.both(self.relational(a["L0_gnn_W2"], a["L0_gnn_self_w2"], bias=a["L0_gnn_b1"]), self.clear_dispatched,
                                     self.gate_weights(a["L0_ffn_WgT"], a["L0_gnn_b2"], self.wsmall[:, 0:D])),
                           count=True)
            self.degrees()
            self.transform(self.prep_sum, self.relation_groups(), self.tab_rel, relu=True, halves=True, x_bias=self.wsmall[:, 0:D])
        with self.ring_memory():
            with self.working():
                self.aggregate(self.tab_rel, self.gidx[0], D, self.first_experts(0))
                self.mixture(0)
            self.experts(0)
        with self.count_memory(), self.working():
            self.count_matrix(self.small(self.wsmall[:, :], a["L1_gnn_W1"]))
            self.statistics()
            self.transform(self.prep_norm, self.node_groups(D), self.tab_node, split=True)
            self.aggregate(self.tab_node, self.gidx[1], D, self.small(self.wsmall[:, :], a["L1_gnn_W2"], bias=a["L1_gnn_b1"]), counted=True)
            self.transform(self.prep_scaled, self.node_groups(D), self.tab_node, relu=True, split=True)
            self.aggregate(self.tab_node, self.gidx[1], D, self.small(self.wsmall[:, 0:D], a["L1_gnn_W3"], bias=a["L1_gnn_b2"]), counted=True)
            self.transform(self.prep_scaled, self.node_groups(D // 2), self.tab_half, relu=True, split=True)
            self.aggregate(self.tab_half, self.gidx[1], D // 2,
                           self.both(self.small(self.wsmall[:, 0:D], a["L1_gnn_Wp"], rows=1, bias=a["L1_gnn_b3"]),
                                     self.gate_weights(a["L1_ffn_Wr"], a["L1_gnn_bp"], self.wsmall[:, D:2 * D])),
                           counted=True)
        with self.ring_memory():
            with self.working():
                self.load_experts(1)
                self.transform(self.prep_half, self.project_groups(), None, relu=True, chunks=1, x_bias=self.wsmall[:, D:2 * D])
                self.mixture(1)
            self.experts(1)
            with self.working():
                self.combine_and_store()

    def mixture(self, m):
        self.statistics(residual=True)
        self.transform(self.prep_norm, self.gate_groups(), None, kept=True)
        self.route(m)
        self.dispatch(m)

    def constants(self):
        nc = self.nc
        with self.stage_block() as (block, sem):
            masked = sem("masked")

            @block.gpsimd
            def _(pool):
                nc.gpsimd.memset(self.x[:, (TILES - 1) * D:TILES * D], 0.0)
                nc.gpsimd.memset(self.zeros(), 0.0)
                nc.gpsimd.memset(self.acc[:, :].rearrange("p (t w) -> p t w", w=ACCW)[:, :, D:ACCW], 0.0)
                for s in range(GSLOTS):
                    nc.gpsimd.memset(self.rowbuf[s][:, D:ACCW], 1.0)
                nc.gpsimd.iota(self.iota_e[:, :], [[0, TILES], [1, E]], base=-E, channel_multiplier=0,
                               allow_small_or_imprecise_dtypes=True)
                nc.gpsimd.memset(self.ident[:, :], 0.0).then_inc(masked, 1)
                nc.gpsimd.memset(self.tri[:, :], 1.0).then_inc(masked, 1)
                nc.gpsimd.memset(self.ones[:, :], 1.0)
                nc.gpsimd.iota(self.iota[:, :], [[1, PAIRS]], base=0, channel_multiplier=0,
                               allow_small_or_imprecise_dtypes=True)
                pool.wait_ge(masked, 2)
                nc.gpsimd.affine_select(out=self.ident[:, :], in_=self.ident[:, :], compare_op=ALU.not_equal,
                                        fill=1.0, base=0, pattern=[[-1, P]], channel_multiplier=1)
                nc.gpsimd.affine_select(out=self.tri[:, :], in_=self.tri[:, :], compare_op=ALU.is_gt,
                                        fill=0.0, base=0, pattern=[[1, P]], channel_multiplier=-1)

    def zeros(self):
        return self.scratch[:, H:H + D]

    def fetch_x(self, sp, loaded):
        x = self.a["x"]
        xv = self.x[:, 0:(TILES - 1) * D].rearrange("p (t d) -> p t d", d=D)
        sp.dma_start(xv, x[0:(TILES - 1) * P, :].rearrange("(t p) d -> p t d", p=P)).then_inc(loaded, 16)
        sp.dma_start(self.x[0:LAST, (TILES - 1) * D:TILES * D], x[(TILES - 1) * P:NODES, :]).then_inc(loaded, 16)
        return 2

    def clear_dispatched(self, sp, stored):
        for t in range(MTILES):
            if t % 6 == 0:
                self.pace()
            sp.dma_start(self.xd[t * P:(t + 1) * P, :], self.zeros()).then_inc(stored, 16)
        return MTILES

    def both(self, *fetches):
        return lambda sp, loaded: sum(f(sp, loaded) for f in fetches)

    def edge_pairs(self, fetch):
        nc, a = self.nc, self.a
        W = ECH * P
        with ExitStack() as ctx:
            names = ("dst", "src", "edge_type_8")
            big = self.rest
            at = [big[:, k * W:(k + 1) * W].bitcast(I32) for k in range(4)]
            raw, bint = at[0:3], at[3]
            col = lambda k, n=W: big[:, k:k + n]
            dstf, srcf, typf, bf, g0, dp = (col((4 + k) * W) for k in range(6))
            S = col(10 * W, ECH * PAIRS)
            tmp = col(10 * W + ECH * PAIRS, PAIRS)
            bmin, bmax, n, start, bs, w, end = (self.scratch[:, k * ECH:(k + 1) * ECH] for k in range(7))
            ps = self.ps
            rows = [P] * (ECH - 1) + [ELASTCH]
            block, sem = ctx.enter_context(self.stage_block())
            fetched, high_ready, x_loaded, padded, loaded, link, counted, started, chosen, done = sem(
                "fetched", "high_ready", "x_loaded", "padded", "loaded", "link", "counted", "started", "chosen", "done")

            @block.gpsimd
            def _(pool):
                for r, fill in zip(raw, (NPAD - 1, 0, 0)):
                    nc.gpsimd.memset(r[:, (ECH - 1) * P:ECH * P], fill).then_inc(padded, 1)
                self.low_weights(pool, nc.gpsimd, high_ready)

            @block.scalar
            def _(act):
                act.wait_ge(fetched, 16 * (KD + 1))
                self.high_weights(act, high_ready)

            @block.sync
            def _(sp):
                sp.wait_ge(padded, 3)
                for r, name in zip(raw, names):
                    full = a[name][0:EFULL * P].rearrange("(t e) -> t e", e=P)
                    for c in range(ECH):
                        k = min(P, EFULL - c * P)
                        sp.dma_start(r[0:k, c * P:(c + 1) * P], full[c * P:c * P + k, :]).then_inc(loaded, 16)
                    k = EFULL - (ECH - 1) * P
                    sp.dma_start(r[k:k + 1, (ECH - 1) * P:(ECH - 1) * P + EREST],
                                 a[name][EFULL * P:EDGES].rearrange("(t e) -> t e", t=1)).then_inc(loaded, 16)
                n = fetch(sp, fetched)
                sp.wait_ge(x_loaded, 16 * self.fetch_x(sp, x_loaded))
                sp.wait_ge(fetched, 16 * n)

            @block.vector
            def _(dve):
                link_ = Chain(dve, link)
                v = nc.vector
                dve.wait_ge(loaded, 16 * 3 * (ECH + 1))
                link_(v.tensor_single_scalar(bint, raw[0], 7, ALU.arith_shift_right))
                link_(v.tensor_copy(bf, bint))
                link_(v.tensor_copy(dstf, raw[0]))
                link_(v.tensor_copy(srcf, raw[1]))
                link_(v.tensor_copy(typf, raw[2]))
                b3 = bf.rearrange("p (c e) -> p c e", c=ECH)
                link_(v.tensor_reduce(bmin[:, :], b3, AX.X, ALU.min))
                link_(v.tensor_reduce(bmax[:, :], b3, AX.X, ALU.max))
                link_(v.scalar_tensor_tensor(out=n[:, :], in0=bmax[:, :], scalar=1.0, in1=bmin[:, :], op0=ALU.add, op1=ALU.subtract))
                v.scalar_tensor_tensor(out=g0, in0=srcf, scalar=float(REL), in1=typf, op0=ALU.mult, op1=ALU.add).then_inc(counted, 1)
                dve.wait_ge(started, 1)
                link_(v.tensor_copy(start[:, :], ps[0][:, 0:ECH]))
                link_(v.tensor_tensor(bs[:, :], bmin[:, :], start[:, :], ALU.subtract))
                link_(v.tensor_single_scalar(w[:, :], bs[:, :], float(P), ALU.mult))
                link_(v.tensor_tensor(end[:, :], start[:, :], n[:, :], ALU.add))
                for c in range(ECH):
                    link_(v.tensor_scalar(dp[:, c * P:(c + 1) * P], dstf[:, c * P:(c + 1) * P], w[:, c:c + 1], None, ALU.subtract))
                    link_(v.tensor_scalar(tmp, self.iota[:, :], start[:, c:c + 1], None, ALU.is_ge))
                    link_(v.scalar_tensor_tensor(out=S[:, c * PAIRS:(c + 1) * PAIRS], in0=self.iota[:, :], scalar=end[:, c:c + 1],
                                                 in1=tmp, op0=ALU.is_lt, op1=ALU.mult))
                v.tensor_copy(tmp, self.iota[:, :]).then_inc(chosen, 1)
                dve.wait_ge(done, 1)
                link_(v.tensor_copy(self.gidx[0][:, :], ps[1][:, 0:PAIRS]))
                link_(v.tensor_copy(self.gidx[1][:, :], ps[2][:, 0:PAIRS]))
                link_(v.scalar_tensor_tensor(out=self.rel[:, :], in0=self.iota[:, :], scalar=-float(P), in1=ps[3][:, 0:PAIRS],
                                             op0=ALU.mult, op1=ALU.add))
                link_(v.tensor_tensor(dstf[0:1, 0:PAIRS], self.iota[0:1, :], ps[5][0:1, 0:PAIRS], ALU.mult))
                link_(v.tensor_tensor(dstf[0:1, 0:PAIRS], dstf[0:1, 0:PAIRS], ps[4][0:1, 0:PAIRS], ALU.add))
                link_(v.scalar_tensor_tensor(out=dstf[0:1, 0:PAIRS], in0=ps[5][0:1, 0:PAIRS], scalar=-float(TILES - 1),
                                             in1=dstf[0:1, 0:PAIRS], op0=ALU.mult, op1=ALU.add))
                link_(v.tensor_single_scalar(dstf[0:1, 0:PAIRS], dstf[0:1, 0:PAIRS], float(TILES - 1), ALU.add))
                link_(v.tensor_single_scalar(dstf[0:1, 0:PAIRS], dstf[0:1, 0:PAIRS], float(ACCW), ALU.mult))
                link_(v.tensor_copy(self.bucket[:, :], dstf[0:1, 0:PAIRS]))

            @block.tensor
            def _(pe):
                t = nc.tensor
                pe.wait_ge(counted, 1)
                for c in range(ECH):
                    for d in range(c):
                        t.matmul(ps[0][:, c:c + 1], self.ones[:, :], n[:, d:d + 1], start=(d == 0), stop=False)
                    last = t.matmul(ps[0][:, c:c + 1], self.tri[0:rows[c], :], n[0:rows[c], c:c + 1], start=(c == 0), stop=True)
                last.then_inc(started, 1)
                pe.wait_ge(chosen, 1)
                for bank, m, lhs in ((1, P, g0), (2, P, srcf), (3, P, dp)):
                    for c in range(ECH):
                        k = rows[c]
                        t.matmul(ps[bank][:, 0:PAIRS], lhs[0:k, c * P:(c + 1) * P], S[0:k, c * PAIRS:(c + 1) * PAIRS],
                                 start=(c == 0), stop=(c == ECH - 1))
                for bank, lhs in ((4, bs), (5, None)):
                    for c in range(ECH):
                        k = rows[c]
                        left = self.ones[0:k, 0:1] if lhs is None else lhs[0:k, c:c + 1]
                        last = t.matmul(ps[bank][0:1, 0:PAIRS], left, S[0:k, c * PAIRS:(c + 1) * PAIRS],
                                        start=(c == 0), stop=(c == ECH - 1))
                last.then_inc(done, 1)

    def small(self, to, of, rows=KD, bias=None, bias_to=None):
        def fetch(sp, loaded):
            sp.dma_start(to.rearrange("p (k o) -> p k o", k=rows), of.rearrange("(k p) o -> p k o", p=P)).then_inc(loaded, 16)
            if bias is not None:
                row = self.bias[:, 0:bias.shape[0]] if bias_to is None else bias_to
                sp.dma_start(row, self.spread(bias)).then_inc(loaded, 16)
            return 1 + (bias is not None)
        return fetch

    def relational(self, of, self_of, bias=None):
        to, own = self.raw[:, 0:KD * REL * D], self.raw[:, KD * REL * D:RELW]
        to, of = to.rearrange("p (k r o) -> p k r o", k=KD, r=REL), of.rearrange("r (k p) o -> p k r o", p=P)

        def fetch(sp, loaded):
            for k in range(KD):
                self.pace()
                sp.dma_start(to[:, k], of[:, k]).then_inc(loaded, 16)
            self.pace()
            return KD + self.small(own, self_of, bias=bias)(sp, loaded)
        return fetch

    def high_weights(self, act, ready):
        self.nc.scalar.activation(self.relw[0].bitcast(F32R), self.raw, ACT.Copy).then_inc(ready, 1)

    def low_weights(self, eng, engine, ready):
        eng.wait_ge(ready, 1)
        engine.tensor_tensor(self.relw[1].bitcast(F32R), self.raw, self.relw[0].bitcast(F32R), ALU.subtract)

    def gate_weights(self, w, bias, to):
        return self.small(self.wgate[:, :], w, bias=bias, bias_to=to)

    def spread(self, row):
        return row.rearrange("(a n) -> a n", a=1).to_broadcast([P, row.shape[0]])

    def statistics(self, residual=False):
        nc = self.nc
        x3 = self.x[:, :].rearrange("p (t d) -> p t d", d=D)
        with self.stage_block() as (block, sem):
            link, variance, rooted = sem("link", "variance", "rooted")

            @block.vector
            def _(dve):
                v = nc.vector
                step = Chain(dve, link)
                if residual:
                    step(v.tensor_tensor(x3, x3, self.acc[:, :].rearrange("p (t w) -> p t w", w=ACCW)[:, :, 0:D], ALU.add))
                for i in range(TILES):
                    last = v.bn_stats(self.stats[:, i * 6:(i + 1) * 6], self.x[:, i * D:(i + 1) * D])
                step(last)
                for i in range(TILES):
                    last = v.bn_aggr(self.mv[:, 2 * i:2 * i + 2], self.stats[:, i * 6:(i + 1) * 6])
                step(last)
                var = self.mv[:, :].rearrange("p (t w) -> p t w", w=2)[:, :, 1:2]
                self.inverse_root(dve, step, self.rstd, var, EPS, variance, rooted)

            @block.scalar
            def _(act):
                self.root(act, variance, rooted)

    def root(self, act, ready, rooted):
        act.wait_ge(ready, 1)
        self.nc.scalar.activation(self.r3[:, :], self.r2[:, :], ACT.Sqrt).then_inc(rooted, 1)

    def inverse_root(self, dve, step, to, of, plus, ready, rooted):
        v = self.nc.vector
        t = lambda r: r[:, :].rearrange("p (t w) -> p t w", w=1)
        v.tensor_single_scalar(t(self.r2), of, plus, ALU.add).then_inc(ready, 1)
        dve.wait_ge(rooted, 1)
        step(v.reciprocal(to[:, :], self.r3[:, :]))
        step(v.tensor_tensor(self.r3[:, :], to[:, :], to[:, :], ALU.mult))
        step(v.tensor_tensor(self.r3[:, :], self.r3[:, :], self.r2[:, :], ALU.mult))
        step(v.tensor_scalar(self.r3[:, :], self.r3[:, :], -0.5, 1.5, ALU.mult, ALU.add))
        step(v.tensor_tensor(to[:, :], to[:, :], self.r3[:, :], ALU.mult))

    def normed(self, to, i):
        return self.nc.vector.tensor_scalar(to, self.x_tile(i), self.mv[:, bass.ds(i * 2, 1)], self.rstd[:, bass.ds(i, 1)],
                                            ALU.subtract, ALU.mult)

    def prep_norm(self, i, s):
        return self.normed(self.hn[s][:, :], i)

    def prep_sum(self, i, s):
        return self.nc.vector.tensor_tensor(self.hn[s][:, :], self.acc_tile(i), self.bias[:, :], ALU.add)

    def prep_scaled(self, i, s, width=D):
        return self.nc.vector.scalar_tensor_tensor(out=self.hn[s][:, 0:width], in0=self.acc_tile(i, width), scalar=self.dinv[:, bass.ds(i, 1)],
                                                   in1=self.bias[:, 0:width], op0=ALU.mult, op1=ALU.add)

    def prep_half(self, i, s):
        return self.prep_scaled(i, s, D // 2)

    def relation_groups(self):
        def self_term(ps, i, s):
            return self.nc.scalar.activation(self.acc_tile(i), ps, ACT.Copy)

        def relations(g):
            def put(ps, i, s):
                return self.nc.scalar.activation(self.stage[s][:, g * 512:(g + 1) * 512], ps, ACT.Copy)
            return put

        def weights(at, n):
            return [w[:, at:at + n].bitcast(F32R) for w in self.relw]

        groups = [([weights((KD * REL + k) * D, D) for k in range(KD)], D, self_term)]
        for g in range(REL * D // 512):
            groups.append(([weights(k * REL * D + g * 512, 512) for k in range(KD)], 512, relations(g)))
        return groups

    def node_groups(self, width):
        def put(ps, i, s):
            return self.nc.scalar.activation(self.acc_tile(i, width), ps, ACT.Identity, scale=self.dinv[:, bass.ds(i, 1)])
        return [([self.wsmall[:, k * width:(k + 1) * width] for k in range(KD)], width, put)]

    def project_groups(self):
        def put(ps, i, s):
            return self.nc.scalar.activation(self.acc_tile(i), ps, ACT.Copy)
        return [([self.wsmall[:, 0:D]], D, put)]

    def gate_groups(self):
        def put(ps, i, s):
            return self.nc.scalar.activation(self.scratch[:, bass.ds(i * E, E)], ps, ACT.Copy)
        return [([self.wgate[:, k * E:(k + 1) * E] for k in range(KD)], E, put)]

    def transform(self, prep, groups, table, relu=False, chunks=KD, split=False, halves=False, x_bias=None, kept=False):
        nc = self.nc
        ng = len(groups)
        width = groups[-1][1]
        staged = table is self.tab_rel
        psT, psM = self.ps[0:2], self.ps[2:2 + ng]
        with self.stage_block() as (block, sem):
            rows_ready, turned, hT_ready, stored = (
                [sem(f"{n}{s}") for s in range(2)] for n in ("rows_ready", "turned", "hT_ready", "stored"))
            bank_full, bank_free = ([sem(f"{n}{g}") for g in range(ng)] for n in ("bank_full", "bank_free"))
            rest_ready, middle_ready, high_ready, rows_kept = sem("rest_ready", "middle_ready", "high_ready", "rows_kept")

            @block.vector
            def _(dve):
                def ready(i, s):
                    if kept and not (isinstance(i, int) and i < 2):
                        dve.wait_ge(rows_kept, i - 1)
                        dve.sem_inc(self.gate, 1)
                    prep(i, s).then_inc(rows_ready[s], 1)

                def take(i, j, s):
                    dve.wait_ge(turned[s], j + 1)
                    if later(j):
                        dve.sem_inc(self.gate, 1)
                        dve.wait_ge(bank_full[ng - 1], i - 1)
                    v, p = nc.vector, psT[s][:, 0:chunks * P]
                    if halves:
                        high, low = self.row_halves[s]
                        if relu:
                            v.tensor_single_scalar(high, p, 0.0, ALU.max).then_inc(high_ready, 1)
                        else:
                            v.tensor_copy(high, p).then_inc(high_ready, 1)
                        dve.wait_ge(high_ready, i + 1)
                        if relu:
                            dve.sem_inc(self.gate, 1)
                            v.scalar_tensor_tensor(out=low, in0=p, scalar=0.0, in1=high, op0=ALU.max, op1=ALU.subtract).then_inc(hT_ready[s], 1)
                        else:
                            v.tensor_tensor(low, p, high, ALU.subtract).then_inc(hT_ready[s], 1)
                    elif relu:
                        v.tensor_single_scalar(self.hT[s][:, 0:chunks * P], p, 0.0, ALU.max).then_inc(hT_ready[s], 1)
                    else:
                        v.tensor_copy(self.hT[s][:, 0:chunks * P], p).then_inc(hT_ready[s], 1)

                def pair(j):
                    ready(j * 2 + 1, 1)
                    take(j * 2, j, 0)
                    ready(j * 2 + 2, 0)
                    take(j * 2 + 1, j, 1)

                ready(0, 0)
                pair(0)
                with dve.Fori(1, TILES // 2 - 1) as j:
                    pair(j)
                ready(TILES - 1, 1)
                take(TILES - 2, TILES // 2 - 1, 0)
                take(TILES - 1, TILES // 2 - 1, 1)

            @block.gpsimd
            def _(pool):
                if x_bias is not None:
                    x3 = self.x[:, :].rearrange("p (t d) -> p t d", d=D)
                    nc.gpsimd.tensor_tensor(x3, x3, x_bias.rearrange("p (t d) -> p t d", t=1).broadcast_to([P, TILES, D]), ALU.add)
                if not split:
                    return
                with pool.Fori(0, TILES // 2) as j:
                    for s in range(2):
                        i = j * 2 + s
                        rest = self.scratch[:, s * D:s * D + width]
                        high, middle, low = (p[:, bass.ds(i * D, width)] for p in self.parts + [self.low_part])
                        pool.wait_ge(bank_free[0], i + 1)
                        pool.sem_inc(self.gate, 1)
                        nc.gpsimd.tensor_tensor(rest, self.acc_tile(i, width), high, ALU.subtract).then_inc(rest_ready, 1)
                        pool.wait_ge(rest_ready, i + 1)
                        pool.sem_inc(self.gate, 1)
                        nc.gpsimd.tensor_copy(middle, rest).then_inc(middle_ready, 1)
                        pool.wait_ge(middle_ready, i + 1)
                        pool.sem_inc(self.gate, 1)
                        nc.gpsimd.tensor_tensor(low, rest, middle, ALU.subtract)

            @block.tensor
            def _(pe):
                def turn(j, s):
                    pe.wait_ge(rows_ready[s], j + 1)
                    for k in range(chunks):
                        last = nc.tensor.transpose(psT[s][:, k * P:(k + 1) * P], self.hn[s][:, k * P:(k + 1) * P], self.ident[:, :])
                    last.then_inc(turned[s], 1)

                def multiply(i, j, s):
                    pe.wait_ge(hT_ready[s], j + 1)
                    for g, (w, n, _) in enumerate(groups):
                        if later(i):
                            pe.wait_ge(bank_free[g], i)
                        for k in range(chunks):
                            for left, right in ((0, 0), (0, 1), (1, 0)) if halves else ((0, 0),):
                                lhs = self.row_halves[s][left] if halves else self.hT[s]
                                last = nc.tensor.matmul(psM[g][:, 0:n], lhs[:, k * P:(k + 1) * P], w[k][right] if halves else w[k],
                                                        start=(k == 0 and left == right), stop=(k == chunks - 1 and (left == 1 or not halves)))
                        last.then_inc(bank_full[g], 1)

                def pair(j):
                    turn(j, 1)
                    multiply(j * 2, j, 0)
                    turn(j + 1, 0)
                    multiply(j * 2 + 1, j, 1)

                turn(0, 0)
                pair(0)
                with pe.Fori(1, TILES // 2 - 1) as j:
                    pair(j)
                turn(TILES // 2 - 1, 1)
                multiply(TILES - 2, TILES // 2 - 1, 0)
                multiply(TILES - 1, TILES // 2 - 1, 1)

            @block.scalar
            def _(act):
                def pair(j):
                    for s in range(2):
                        i = j * 2 + s
                        if kept:
                            act.wait_ge(rows_ready[s], j + 1)
                            act.sem_inc(self.gate, 1)
                            nc.scalar.activation(self.acc_tile(i), self.hn[s][:, :], ACT.Copy).then_inc(rows_kept, 1)
                        for g, (_, n, put) in enumerate(groups):
                            if staged and g == 1 and later(j):
                                act.wait_ge(stored[s], j * 16)
                                act.sem_inc(self.gate, 1)
                            act.wait_ge(bank_full[g], i + 1)
                            act.sem_inc(self.gate, 1)
                            last = put(psM[g][:, 0:n], i, s)
                            if split:
                                last = nc.scalar.activation(self.parts[0][:, bass.ds(i * D, n)], psM[g][:, 0:n], ACT.Identity,
                                                            scale=self.dinv[:, bass.ds(i, 1)])
                            last.then_inc(bank_free[g], 1)

                pair(0)
                with act.Fori(1, TILES // 2) as j:
                    pair(j)

            @block.sync
            def _(sp):
                if table is None:
                    return
                with sp.Fori(0, TILES // 2) as j:
                    for s in range(2):
                        i = j * 2 + s
                        for g in range(ng):
                            sp.wait_ge(bank_free[g], i + 1)
                            sp.sem_inc(self.gate, 1)
                        if staged:
                            rows = table[bass.ds(i * (P * REL), P * REL), :].rearrange("(p r) d -> p (r d)", r=REL)
                            sp.dma_start(rows, self.stage[s]).then_inc(stored[s], 16)
                        else:
                            sp.dma_start(table[bass.ds(i * P, P), :], self.acc_tile(i, width)).then_inc(stored[s], 16)
                for s in range(2):
                    sp.wait_ge(stored[s], TILES // 2 * 16)

    def aggregate(self, table, gidx, width, fetch, count=False, counted=False):
        nc = self.nc
        wide = width + 1 if count else width
        rounds = PAIRS // GSLOTS
        with self.stage_block() as (block, sem):
            idx_ready, onehot_ready, summed, added = (
                [sem(f"{n}{s}") for s in range(GSLOTS)] for n in ("idx_ready", "onehot_ready", "summed", "added"))
            product_full, product_added, fetched = sem("product_full", "product_added", "fetched")
            gathers = self.regathered if counted else self.gathered
            gathered, before = [g.sem for g in gathers], [g.base for g in gathers]
            for g in gathers:
                g.base += 16 * rounds

            @block.sync
            def _(sp):
                steps = iter(range(0, rounds, PACE))

                def pace():
                    n = next(steps)
                    if n > 0:
                        sp.wait_ge(summed[0], n)
                if not counted:
                    self.pace = pace
                n = fetch(sp, fetched)
                self.pace = lambda: None
                if n > 0:
                    sp.wait_ge(fetched, 16 * n)

            @block.scalar
            def _(act):
                with self.exact_counts(act, counted, False):
                    def round_(i):
                        for s in range(GSLOTS):
                            if later(i):
                                act.wait_ge(gathered[s], i * 16 + before[s])
                                act.sem_inc(self.gate, 1)
                            nc.scalar.activation(self.idx[s][:, :], gidx[:, bass.ds(i * GSLOTS + s, 1)], ACT.Copy).then_inc(idx_ready[s], 1)

                    round_(0)
                    with act.Fori(1, rounds) as i:
                        round_(i)

            @block.gpsimd
            def _(pool):
                with self.exact_counts(pool, counted, False):
                    def round_(i):
                        for s in range(GSLOTS):
                            if later(i):
                                pool.wait_ge(summed[s], i)
                                pool.sem_inc(self.gate, 1)
                            pool.wait_ge(idx_ready[s], i + 1)
                            pool.sem_inc(self.gate, 1)
                            nc.gpsimd.indirect_dma_start(self.rowbuf[s][:, 0:width], None, table,
                                                         bass.IndirectOffsetOnAxis(ap=self.idx[s][:, :], axis=0)).then_inc(gathered[s], 16)

                    round_(0)
                    with pool.Fori(1, rounds) as i:
                        round_(i)

            @block.vector
            def _(dve):
                with self.exact_counts(dve, counted, False):
                    half = GSLOTS // 2
                    cols = self.iota[:, 0:P].rearrange("p (s c) -> p s c", s=1).broadcast_to([P, half, P])

                    def onehots(at, k):
                        to = self.onehots[:, k * half * P:(k + 1) * half * P].rearrange("p (s c) -> p s c", s=half)
                        dst = self.rel[:, bass.ds(at + k * half, half)].rearrange("p (s c) -> p s c", c=1).broadcast_to([P, half, P])
                        nc.vector.tensor_tensor(to, cols, dst, ALU.is_equal).then_inc(onehot_ready[k], 1)

                    def add(at, n, s, first=False):
                        to = self.acc[:, bass.ds(dve.value_load(self.bucket[0:1, bass.ds(at + s, 1)], min_val=0, max_val=(TILES - 1) * ACCW), wide)]
                        dve.wait_ge(summed[s], n)
                        if not first:
                            dve.wait_ge(added[s - 1], n if s else n - 1)
                        nc.vector.tensor_tensor(to, to, self.ps[s][:, 0:wide], ALU.add).then_inc(added[s], 1)

                    def round_(at, n, first=False):
                        for k in range(2):
                            onehots(at, k)
                            for s in range(half):
                                if k:
                                    add(at, n, s, first and s == 0)
                                elif not first:
                                    add(at - GSLOTS, n - 1, half + s)

                    round_(0, 1, first=True)
                    with dve.Fori(2, rounds + 1) as n:
                        round_(dve.snap(n * GSLOTS - GSLOTS), n)
                    for s in range(half, GSLOTS):
                        add(PAIRS - GSLOTS, rounds, s)
                if counted:
                    with self.exact_counts(dve, counted, True):
                        with dve.Fori(0, TILES // 2) as j:
                            for s in range(2):
                                b = j * 2 + s
                                dve.wait_ge(product_full, b + 1)
                                dve.sem_inc(self.gate, 1)
                                nc.vector.tensor_tensor(self.acc_tile(b, width), self.acc_tile(b, width), self.ps[s][:, 0:width],
                                                        ALU.add).then_inc(product_added, 1)

            @block.tensor
            def _(pe):
                with self.exact_counts(pe, counted, False):
                    def round_(i):
                        for s in range(GSLOTS):
                            if s % (GSLOTS // 2) == 0:
                                pe.wait_ge(onehot_ready[s // (GSLOTS // 2)], i + 1)
                                pe.sem_inc(self.gate, 1)
                            if later(i):
                                pe.wait_ge(added[s], i)
                                pe.sem_inc(self.gate, 1)
                            pe.wait_ge(gathered[s], i * 16 + (before[s] + 16))
                            nc.tensor.matmul(self.ps[s][:, 0:wide], self.onehots[:, s * P:(s + 1) * P], self.rowbuf[s][:, 0:wide],
                                             start=True, stop=True).then_inc(summed[s], 1)

                    round_(0)
                    with pe.Fori(1, rounds) as i:
                        round_(i)
                if counted:
                    with self.exact_counts(pe, counted, True):
                        def product(b, s):
                            if later(b) and not (isinstance(b, int) and b < 2):
                                pe.wait_ge(product_added, b - 1)
                            for g in range(TILES):
                                counts = self.counts[:, bass.ds(b * NPAD + g * P, P)]
                                for k, part in enumerate(self.parts + [self.low_part]):
                                    last = nc.tensor.matmul(self.ps[s][:, 0:width], counts, part[:, g * D:g * D + width],
                                                            start=(g == 0 and k == 0), stop=(g == TILES - 1 and k == PARTS - 1))
                            last.then_inc(product_full, 1)

                        for s in range(2):
                            product(s, s)
                        with pe.Fori(1, TILES // 2) as j:
                            for s in range(2):
                                product(j * 2 + s, s)
    @contextmanager
    def exact_counts(self, eng, counted, exact):
        if not counted:
            yield
            return
        uncounted = eng.value_load(self.uncounted[0:1, 0:1], min_val=0, max_val=1)
        with eng.If(uncounted == (0 if exact else 1)):
            yield

    def count_matrix(self, fetch):
        nc = self.nc
        at = self.slots[:, :]
        src_hots = [at[:, s * WINDOW * P // 2:(s + 1) * WINDOW * P // 2].bitcast(F16) for s in range(2)]
        pair_hots = [self.free[:, s * NPAD // 2:(s + 1) * NPAD // 2].bitcast(F16) for s in range(HOTS)]
        bucket = self.free[:, HOTS * NPAD // 2:HOTS * NPAD // 2 + PAIRS]
        places = self.scratch[:, 0:NPAD // 2].bitcast(F16)
        src_low, key = (self.scratch[:, NPAD // 2 + k * PAIRS:NPAD // 2 + (k + 1) * PAIRS] for k in range(2))
        tmp, row = self.acc[:, 0:PAIRS], self.acc[0:1, PAIRS:2 * PAIRS]
        whole = self.acc[:, 2 * PAIRS:3 * PAIRS].bitcast(I32)
        edge_key = [self.acc[:, 3 * PAIRS + s * WINDOW:3 * PAIRS + (s + 1) * WINDOW] for s in range(2)]
        off = self.acc[:, 3 * PAIRS + 2 * WINDOW:3 * PAIRS + 3 * WINDOW]
        bucket_no = self.acc[:, 4 * PAIRS:4 * PAIRS + TILES]
        first = self.column[:, 2:3]
        part_no = self.column[:, 3:4]
        with self.stage_block() as (block, sem):
            link, places_ready, row_ready, spread, first_ready, turned, keyed, src_hot, pair_hot, summed, bank_full, bank_out = sem(
                "link", "places_ready", "row_ready", "spread", "first_ready", "turned", "keyed", "src_hot", "pair_hot", "summed",
                "bank_full", "bank_out")
            fetched, rows_added = sem("fetched", "rows_added")
            BANKS = NPAD // 512
            banks = [[self.ps[g] for g in (2, 3, 4, 0, 1)], [self.ps[g] for g in (5, 6, 7, 0, 1)]]
            last_order = (3, 4, 0, 1, 2)
            rows = [self.acc[:, 5 * PAIRS + n * D:5 * PAIRS + (n + 1) * D] for n in range(2 * TOPK)]
            row_in, rows_before = [g.sem for g in self.gathered[0:2 * TOPK]], [g.base for g in self.gathered[0:2 * TOPK]]
            for g in self.gathered[0:2 * TOPK]:
                g.base += 16 * TILES // 2

            @block.sync
            def _(sp):
                sp.wait_ge(fetched, 16 * fetch(sp, fetched))

            @block.gpsimd
            def _(pool):
                nc.gpsimd.iota(places, [[1, NPAD]], base=-MID, channel_multiplier=0,
                               allow_small_or_imprecise_dtypes=True).then_inc(places_ready, 1)
                nc.gpsimd.iota(bucket_no, [[ACCW, TILES]], base=0, channel_multiplier=0,
                               allow_small_or_imprecise_dtypes=True).then_inc(places_ready, 1)
                nc.gpsimd.iota(part_no, [[0, 1]], base=0, channel_multiplier=ACCW,
                               allow_small_or_imprecise_dtypes=True).then_inc(places_ready, 1)
                for n in range(TOPK * TILES):
                    t, k = n // TOPK, n % TOPK
                    if n >= 2 * TOPK:
                        pool.wait_ge(rows_added, n - 2 * TOPK + 1)
                    c = k * TILES + t
                    nc.gpsimd.indirect_dma_start(rows[n % (2 * TOPK)], None, self.yd,
                                                 bass.IndirectOffsetOnAxis(ap=self.spos[:, c:c + 1], axis=0)).then_inc(row_in[n % (2 * TOPK)], 16)

            @block.vector
            def _(dve):
                v = nc.vector
                step = Chain(dve, link)
                v.tensor_copy(row, self.bucket[:, :]).then_inc(row_ready, 1)
                src = self.gidx[1][:, :]
                step(v.tensor_copy(whole, src))
                step(v.tensor_single_scalar(whole, whole, 7, ALU.arith_shift_right))
                step(v.tensor_copy(tmp, whole))
                step(v.scalar_tensor_tensor(out=src_low, in0=tmp, scalar=-float(P), in1=src, op0=ALU.mult, op1=ALU.add))
                step(v.scalar_tensor_tensor(out=key, in0=tmp, scalar=float(P), in1=self.rel[:, :], op0=ALU.mult, op1=ALU.add))
                step(v.tensor_single_scalar(key, key, -float(MID), ALU.add))
                step(v.tensor_scalar(tmp, self.rel[:, :], 0.0, FAR, ALU.is_lt, ALU.mult))
                step(v.tensor_tensor(key, key, tmp, ALU.add))
                step(v.tensor_scalar(tmp, self.rel[:, :], float(P), FAR, ALU.is_ge, ALU.mult))
                step(v.tensor_tensor(key, key, tmp, ALU.add))
                dve.wait_ge(places_ready, 3)
                dve.wait_ge(spread, 1)
                step(v.tensor_copy(bucket, self.ps[7][:, 0:PAIRS]))
                step(v.tensor_scalar(tmp, bucket, part_no, None, ALU.is_lt))
                step(v.tensor_reduce(first, tmp, AX.X, ALU.add))
                v.tensor_single_scalar(first, first, float(PAIRS - WINDOW), ALU.min).then_inc(first_ready, 1)
                dve.wait_ge(turned, 1)
                step(v.tensor_copy(self.window[:, :], self.ps[6][0:1, 0:TILES]))
                places_low = self.iota[:, 0:P].rearrange("p (s c) -> p s c", s=1).broadcast_to([P, WINDOW, P])

                def combine(b, j, s):
                    for k in range(TOPK):
                        n = s * TOPK + k
                        dve.wait_ge(row_in[n], j * 16 + (rows_before[n] + 16))
                        dve.sem_inc(self.gate, 1)
                        if k or later(b):
                            dve.wait_ge(rows_added, b * TOPK + k)
                            dve.sem_inc(self.gate, 1)
                        v.scalar_tensor_tensor(out=self.x_tile(b), in0=rows[n], scalar=self.wcomb[:, bass.ds(b + k * TILES, 1)],
                                               in1=self.x_tile(b), op0=ALU.mult, op1=ALU.add).then_inc(rows_added, 1)

                def window(b, j, s):
                    at = dve.value_load(self.window[0:1, bass.ds(b, 1)], min_val=0, max_val=PAIRS - WINDOW)
                    low = src_low[:, bass.ds(at, WINDOW)].rearrange("p (s c) -> p s c", c=1).broadcast_to([P, WINDOW, P])
                    v.tensor_tensor(src_hots[s].rearrange("p (s c) -> p s c", s=WINDOW), places_low, low, ALU.is_equal).then_inc(src_hot, 1)
                    v.tensor_scalar(off, bucket[:, bass.ds(at, WINDOW)], bucket_no[:, bass.ds(b, 1)], FAR,
                                    ALU.not_equal, ALU.mult).then_inc(keyed, 1)
                    dve.wait_ge(keyed, b * 2 + 1)
                    dve.sem_inc(self.gate, 1)
                    v.tensor_tensor(edge_key[s], key[:, bass.ds(at, WINDOW)], off, ALU.add).then_inc(keyed, 1)
                    dve.wait_ge(keyed, b * 2 + 2)
                    for k in range(WINDOW):
                        before = k - HOTS if k >= HOTS else max(n for n in range(WINDOW) if n % HOTS == k) - WINDOW
                        if later(b) or before >= 0:
                            dve.wait_ge(summed, b * WINDOW + (before + 1))
                            dve.sem_inc(self.gate, 1)
                        v.tensor_scalar(pair_hots[k % HOTS], places, edge_key[s][:, k:k + 1], None, ALU.is_equal).then_inc(pair_hot, 1)
                        if k == WINDOW // 2:
                            combine(b, j, s)

                for s in range(2):
                    window(s, 0, s)
                with dve.Fori(1, TILES // 2) as j:
                    for s in range(2):
                        window(j * 2 + s, j, s)

            @block.tensor
            def _(pe):
                t = nc.tensor
                pe.wait_ge(row_ready, 1)
                t.matmul(self.ps[7][:, 0:PAIRS], self.ones[0:1, :], row, start=True, stop=True).then_inc(spread, 1)
                pe.wait_ge(first_ready, 1)
                t.matmul(self.ps[6][0:1, 0:P], first, self.ident[:, :], start=True, stop=True).then_inc(turned, 1)

                def bucket_sums(b, s):
                    pe.wait_ge(src_hot, b + 1)
                    for k in range(WINDOW):
                        pe.wait_ge(pair_hot, b * WINDOW + (k + 1))
                        pe.sem_inc(self.gate, 1)
                        for n, g in enumerate(last_order if k == WINDOW - 1 else range(BANKS)):
                            if k == 0 and g >= 3 and later(b):
                                pe.wait_ge(bank_out, b * BANKS + (g - 2 - BANKS))
                                pe.sem_inc(self.gate, 1)
                            elif k == 0 and g == 0 and not (isinstance(b, int) and b < 2):
                                pe.wait_ge(bank_out, b * BANKS - BANKS)
                                pe.sem_inc(self.gate, 1)
                            last = t.matmul(banks[s][g][:, :], src_hots[s][:, k * P:(k + 1) * P], pair_hots[k % HOTS][:, g * 512:(g + 1) * 512],
                                            start=(k == 0), stop=(k == WINDOW - 1))
                            if k == WINDOW - 1 and n < BANKS - 1:
                                last.then_inc(bank_full, 1)
                        last.then_inc(summed, 1)

                for s in range(2):
                    bucket_sums(s, s)
                with pe.Fori(1, TILES // 2) as j:
                    for s in range(2):
                        bucket_sums(j * 2 + s, s)

            @block.scalar
            def _(act):
                with act.Fori(0, TILES // 2) as j:
                    for s in range(2):
                        b = j * 2 + s
                        for n, g in enumerate(last_order):
                            if n < BANKS - 1:
                                act.wait_ge(bank_full, b * (BANKS - 1) + (n + 1))
                            else:
                                act.wait_ge(summed, b * WINDOW + WINDOW)
                            act.sem_inc(self.gate, 1)
                            nc.scalar.activation(self.counts[:, bass.ds(b * NPAD + g * 512, 512)], banks[s][g][:, :], ACT.Copy).then_inc(bank_out, 1)

    def degrees(self):
        nc = self.nc
        most = [self.scratch[0:1, k:k + 1] for k in range(2)]
        with self.stage_block() as (block, sem):
            link, degree, rooted, copied, ranked, high_ready = sem("link", "degree", "rooted", "copied", "ranked", "high_ready")

            @block.vector
            def _(dve):
                v = nc.vector
                step = Chain(dve, link)
                counts = self.acc[:, :].rearrange("p (t w) -> p t w", w=ACCW)[:, :, D:ACCW]
                self.inverse_root(dve, step, self.dinv, counts, 1.0, degree, rooted)
                step(v.tensor_copy(self.r3[:, :].rearrange("p (t w) -> p t w", w=1), counts))
                v.tensor_reduce(self.column[:, 0:1], self.r3[:, :], AX.X, ALU.max).then_inc(copied, 1)
                dve.wait_ge(ranked, 1)
                step(v.tensor_reduce(most[0], self.ps[0][0:1, 0:TILES], AX.X, ALU.max))
                step(v.tensor_reduce(most[1], self.ps[1][0:1, 0:P], AX.X, ALU.max))
                step(v.tensor_single_scalar(most[0], most[0], float(WINEDGES), ALU.is_gt))
                step(v.tensor_single_scalar(most[1], most[1], float(FULLCOUNT), ALU.is_gt))
                step(v.tensor_tensor(most[0], most[0], most[1], ALU.max))
                step(v.tensor_copy(self.uncounted[:, :], most[0]))
                self.low_weights(dve, v, high_ready)

            @block.tensor
            def _(pe):
                pe.wait_ge(copied, 1)
                nc.tensor.matmul(self.ps[0][0:1, 0:TILES], self.ones[:, 0:1], self.r3[:, :], start=True, stop=True)
                nc.tensor.matmul(self.ps[1][0:1, 0:P], self.column[:, 0:1], self.ident[:, :], start=True, stop=True).then_inc(ranked, 1)

            @block.scalar
            def _(act):
                self.high_weights(act, high_ready)
                self.root(act, degree, rooted)

    def high(self, slot, n=WE):
        return self.big[:, slot * 2 * WE:slot * 2 * WE + n].bitcast(F32R)

    def low(self, slot):
        return self.big[:, slot * 2 * WE + WE:(slot + 1) * 2 * WE]

    def fetch_expert(self, eng, m, e, loaded):
        a, pre, to = self.a, f"L{m}_ffn_", self.low(e % RING)
        self.pace()
        eng.dma_start(to[:, 0:W1E].rearrange("p (k h) -> p k h", k=KD), a[pre + "W1t"][e].rearrange("(k p) h -> p k h", p=P)).then_inc(loaded, 16)
        self.pace()
        eng.dma_start(to[:, W1E:WE].rearrange("p (c d) -> p c d", c=HC), a[pre + "W2t"][e].rearrange("(c p) d -> p c d", p=P)).then_inc(loaded, 16)

    def first_experts(self, m):
        def fetch(eng, _=None):
            for e in range(RING):
                self.fetch_expert(eng, m, e, self.experts_loaded)
            return 0
        return fetch

    def load_experts(self, m):
        with self.stage_block() as (block, _):
            @block.scalar
            def _(act):
                self.first_experts(m)(act)

    def route(self, m):
        nc, n = self.nc, TILES * E
        sc = self.scratch
        names = ("eq", "oh1", "oh2", "m2nd", "both", "tot", "sa", "sb", "excl", "pos")
        eq, oh1, oh2, rest, both, tot, sa, sb_, excl, pos = (sc[:, (k + 1) * n:(k + 2) * n] for k in range(len(names)))
        L = sc[:, 0:n]
        at = (len(names) + 1) * n
        m1, m2, i1, i2, t1, t2 = (sc[:, at + k * TILES:at + (k + 1) * TILES] for k in range(6))
        at += 6 * TILES
        nt, ea, eb, ts, gb = (sc[:, at + k * E:at + (k + 1) * E] for k in range(5))
        at += 5 * E
        ni = sc[:, at:at + E].bitcast(I32)
        row = [sc[0:1, at + E + k * MTILES:at + E + (k + 1) * MTILES] for k in range(2)]
        g3 = lambda t: t.rearrange("p (t e) -> p t e", e=E)
        over = lambda t: t.rearrange("p (t o) -> p t o", o=1).broadcast_to([P, TILES, E])
        per = lambda t: t.rearrange("p (o e) -> p o e", o=1).broadcast_to([P, TILES, E])
        with self.stage_block() as (block, sem):
            link, loaded, to_exp, exp_done, masked, ranked = sem("link", "loaded", "to_exp", "exp_done", "masked", "ranked")

            @block.sync
            def _(sp):
                sp.dma_start(gb, self.spread(self.a[("L0_ffn_bg", "L1_ffn_br")[m]])).then_inc(loaded, 16)

            @block.scalar
            def _(act):
                act.wait_ge(to_exp, 1)
                if m == 0:
                    nc.scalar.activation(t1, t1, ACT.Exp).then_inc(exp_done, 1)
                else:
                    nc.scalar.activation(L, L, ACT.Exp).then_inc(exp_done, 1)

            @block.vector
            def _(dve):
                v = nc.vector
                step = Chain(dve, link)

                def best(of, value, place, onehot):
                    step(v.tensor_reduce(value, g3(of), AX.X, ALU.max))
                    step(v.tensor_tensor(g3(eq), g3(of), over(value), ALU.is_equal))
                    step(v.tensor_tensor(eq, eq, self.iota_e[:, :], ALU.mult))
                    step(v.tensor_reduce(place, g3(eq), AX.X, ALU.min))
                    step(v.tensor_tensor(g3(onehot), g3(self.iota_e[:, :]), over(place), ALU.is_equal))

                dve.wait_ge(loaded, 16)
                step(v.tensor_tensor(g3(L), g3(L), per(gb), ALU.add))
                if m == 1:
                    step(v.tensor_reduce(m1, g3(L), AX.X, ALU.max))
                    v.tensor_tensor(g3(L), g3(L), over(m1), ALU.subtract).then_inc(to_exp, 1)
                    dve.wait_ge(exp_done, 1)
                    step(v.tensor_reduce(t1, g3(L), AX.X, ALU.add))
                    step(v.reciprocal(t2, t1))
                    step(v.tensor_tensor(g3(L), g3(L), over(t2), ALU.mult))
                best(L, m1, i1, oh1)
                step(v.scalar_tensor_tensor(out=rest, in0=oh1, scalar=NEG, in1=L, op0=ALU.mult, op1=ALU.add))
                best(rest, m2, i2, oh2)
                v.tensor_tensor(both, oh1, oh2, ALU.add).then_inc(masked, 1)
                w1, w2 = self.wcomb[:, 0:TILES], self.wcomb[:, TILES:2 * TILES]
                if m == 0:
                    v.tensor_tensor(t1, m2, m1, ALU.subtract).then_inc(to_exp, 1)
                    dve.wait_ge(exp_done, 1)
                    step(v.tensor_single_scalar(t2, t1, 1.0, ALU.add))
                    step(v.reciprocal(w1, t2))
                    step(v.tensor_tensor(w2, w1, t1, ALU.mult))
                else:
                    step(v.tensor_tensor(t1, m1, m2, ALU.add))
                    step(v.reciprocal(t2, t1))
                    step(v.tensor_tensor(w1, m1, t2, ALU.mult))
                    step(v.tensor_tensor(w2, m2, t2, ALU.mult))
                dve.wait_ge(ranked, 1)
                step(v.tensor_copy(tot, self.ps[1][:, 0:n]))
                a, b, d = tot, sa, 1
                while d < TILES:
                    step(v.tensor_copy(b[:, 0:d * E], a[:, 0:d * E]))
                    step(v.tensor_tensor(b[:, d * E:n], a[:, d * E:n], a[:, 0:n - d * E], ALU.add))
                    a, b, d = b, (sb_ if b is sa else sa), 2 * d
                step(v.tensor_tensor(excl, a, tot, ALU.subtract))
                step(v.tensor_single_scalar(ni, a[:, n - E:n], float(P - 1), ALU.add))
                step(v.tensor_single_scalar(ni, ni, 7, ALU.arith_shift_right))
                step(v.tensor_copy(nt, ni))
                a, b, d = nt, ea, 1
                while d < E:
                    step(v.tensor_copy(b[:, 0:d], a[:, 0:d]))
                    step(v.tensor_tensor(b[:, d:E], a[:, d:E], a[:, 0:E - d], ALU.add))
                    a, b, d = b, (eb if b is ea else ea), 2 * d
                step(v.tensor_tensor(ts, a, nt, ALU.subtract))
                step(v.tensor_single_scalar(ts, ts, float(P), ALU.mult))
                step(v.tensor_tensor(pos, excl, self.ps[0][:, 0:n], ALU.add))
                step(v.tensor_tensor(g3(pos), g3(pos), per(ts), ALU.add))
                for k, oh in enumerate((oh1, oh2)):
                    step(v.tensor_tensor(eq, oh, pos, ALU.mult))
                    step(v.tensor_reduce(t1, g3(eq), AX.X, ALU.add))
                    step(v.tensor_copy(self.spos[:, k * TILES:(k + 1) * TILES], t1))
                step(v.tensor_scalar(row[0], self.iota[0:1, 0:MTILES], a[0:1, 0:1], None, ALU.is_ge))
                for e in range(1, E - 1):
                    step(v.scalar_tensor_tensor(out=row[e % 2], in0=self.iota[0:1, 0:MTILES], scalar=a[0:1, e:e + 1],
                                                in1=row[(e - 1) % 2], op0=ALU.is_ge, op1=ALU.add))
                step(v.tensor_copy(self.texp[:, 0:MTILES], row[(E - 2) % 2]))
                step(v.tensor_single_scalar(self.texp[:, MTILES:MTILES + E], a[0:1, 0:E], 1.0, ALU.add))

            @block.tensor
            def _(pe):
                pe.wait_ge(masked, 1)
                nc.tensor.matmul(self.ps[0][:, 0:n], self.tri[:, :], both, start=True, stop=True)
                nc.tensor.matmul(self.ps[1][:, 0:n], self.ones[:, :], both, start=True, stop=True).then_inc(ranked, 1)

    def dispatch(self, m):
        nc = self.nc
        with self.stage_block() as (block, sem):
            high_ready = sem("high_ready")

            @block.scalar
            def _(act):
                act.wait_ge(self.experts_loaded, 16 * 2 * RING * (m + 1))
                for e in range(RING):
                    nc.scalar.activation(self.high(e), self.low(e), ACT.Copy).then_inc(high_ready, 1)

            @block.vector
            def _(dve):
                for e in range(RING):
                    dve.wait_ge(high_ready, e + 1)
                    nc.vector.tensor_tensor(self.low(e).bitcast(F32R), self.low(e), self.high(e), ALU.subtract)

            sent = self.sent.sem
            self.sent.base += 16 * TOPK * TILES

            @block.gpsimd
            def _(pool):
                for k in range(TOPK):
                    for t in range(TILES):
                        c = k * TILES + t
                        nc.gpsimd.indirect_dma_start(self.xd, bass.IndirectOffsetOnAxis(ap=self.spos[:, c:c + 1], axis=0),
                                                     self.acc[:, t * ACCW:t * ACCW + D], None).then_inc(sent, 16)
                pool.wait_ge(sent, self.sent.base)

    def experts(self, m):
        nc, a = self.nc, self.a
        affine = m == 1
        func = (ACT.Relu, ACT.Gelu)[m]
        psH, psX, psG, psY = self.ps[0:2], self.ps[2], self.ps[3:5], self.ps[5:7]
        with ExitStack() as memory, self.stage_block() as (block, sem):
            halves = self.scoped(memory, "halves", SLOTCOLS)
            hT_high, hT_low = (halves[:, k * H:(k + 1) * H].bitcast(F32R) for k in range(2))
            xT_high, xT_low = (halves[:, 2 * H + k * D:2 * H + (k + 1) * D].bitcast(F32R) for k in range(2))
            whole = self.scoped(memory, "whole", SCRATCH)
            rows = [whole[:, s * D:(s + 1) * D] for s in range(4)]
            xin, yout = rows[0:2], rows[2:4]
            h = whole[:, 4 * D:4 * D + H]
            brow = [self.acc[:, s * (H + D):(s + 1) * (H + D)] for s in range(2)]
            hT, xT = self.acc[:, 2 * (H + D):2 * (H + D) + H], self.acc[:, 2 * (H + D) + H:2 * (H + D) + H + D]
            lng, lnb = (self.hn[0][:, k * E * KD:(k + 1) * E * KD] for k in range(2))
            x_in, hbias_in, ybias_in, y_ready, y_stored = (
                [sem(f"{k}{s}") for s in range(2)] for k in ("x_in", "hbias_in", "ybias_in", "y_ready", "y_stored"))
            x_turned, x_step, xT_ready, h_full, h_ready, h_turned, g_ready, hT_ready, y_full, ln_loaded, expert_ready, high_ready = sem(
                "x_turned", "x_step", "xT_ready", "h_full", "h_ready", "h_turned", "g_ready", "hT_ready", "y_full", "ln_loaded",
                "expert_ready", "high_ready")
            x_steps = 3 if affine else 1

            def expert(eng, i):
                return eng.value_load(self.texp[0:1, bass.ds(i, 1)], min_val=0, max_val=E - 1)

            def weights(slot, half, at, n):
                return self.big[:, bass.ds(slot * (2 * WE) + (half * WE + at), n)].bitcast(F32R)

            @block.sync
            def _(sp):
                if affine:
                    sp.dma_start(lng, a["L1_ffn_lngT"]).then_inc(ln_loaded, 16)
                    sp.dma_start(lnb, a["L1_ffn_lnbT"]).then_inc(ln_loaded, 16)

                def fetch_bias(i, s, at, n, loaded):
                    e = expert(sp, i)
                    sp.dma_start(brow[s][:, at:at + n], a[f"L{m}_ffn_b12"][bass.ds(e, 1), at:at + n].to_broadcast([P, n])).then_inc(loaded[s], 16)

                def fetch_hbias(i, s):
                    if later(i) and not (isinstance(i, int) and i < 2):
                        sp.wait_ge(h_ready, i - 1)
                        sp.sem_inc(self.gate, 1)
                    fetch_bias(i, s, 0, H, hbias_in)

                def fetch_ybias(i, s):
                    fetch_bias(i, s, H, D, ybias_in)

                def store_y(i, j, s):
                    sp.wait_ge(y_ready[s], j + 1)
                    sp.sem_inc(self.gate, 1)
                    sp.dma_start(self.yd[bass.ds(i * P, P), :], yout[s][:, 0:D]).then_inc(y_stored[s], 16)

                for s in range(2):
                    fetch_hbias(s, s)
                    fetch_ybias(s, s)
                with sp.Fori(0, MTILES // 2 - 1) as j:
                    for s in range(2):
                        i = j * 2 + s
                        fetch_hbias(i + 2, s)
                        store_y(i, j, s)
                        fetch_ybias(i + 2, s)
                for s in range(2):
                    store_y(MTILES - 2 + s, MTILES // 2 - 1, s)
                    sp.wait_ge(y_stored[s], MTILES // 2 * 16)

            @block.gpsimd
            def _(pool):
                pool.sem_inc(expert_ready, RING)
                for e in range(RING, E):
                    end = pool.value_load(self.texp[0:1, MTILES + e - RING:MTILES + e - RING + 1], min_val=1, max_val=MTILES + 1)
                    pool.wait_ge(y_full, end)
                    pool.sem_inc(self.gate, 1)
                    self.fetch_expert(pool, m, e, self.refilled.sem)
                    self.refilled.base += 32
                    pool.wait_ge(self.refilled.sem, self.refilled.base)
                    nc.gpsimd.tensor_copy(self.high(e % RING), self.low(e % RING)).then_inc(high_ready, 1)
                    pool.wait_ge(high_ready, e + 1 - RING)
                    nc.gpsimd.tensor_tensor(self.low(e % RING).bitcast(F32R), self.low(e % RING), self.high(e % RING),
                                            ALU.subtract).then_inc(expert_ready, 1)

            @block.tensor
            def _(pe):
                def turn_x(j, s):
                    pe.wait_ge(x_in[s], j * 16 + 16)
                    for k in range(KD):
                        last = nc.tensor.transpose(psX[:, k * P:(k + 1) * P], xin[s][:, k * P:(k + 1) * P], self.ident[:, :])
                    last.then_inc(x_turned, 1)

                def products(to, lhs, slot, at, n, first, last):
                    for left, right in ((0, 0), (0, 1), (1, 0)):
                        ins = nc.tensor.matmul(to, lhs[left], weights(slot, right, at, n), start=first and (left, right) == (0, 0),
                                               stop=last and left == 1)
                    return ins

                def up(i, e):
                    slot = e % RING
                    pe.wait_ge(expert_ready, e + 1)
                    pe.sem_inc(self.gate, 1)
                    pe.wait_ge(xT_ready, i + 1)
                    pe.sem_inc(self.gate, 1)
                    for b in range(HB):
                        for k in range(KD):
                            last = products(psH[b][:, :], [x[:, k * P:(k + 1) * P] for x in (xT_high, xT_low)], slot,
                                            k * H + b * 512, 512, k == 0, k == KD - 1)
                    last.then_inc(h_full, 1)

                def turn_h(i):
                    pe.wait_ge(h_ready, i + 1)
                    for c in range(HC):
                        last = nc.tensor.transpose(psG[c // 4][:, (c % 4) * P:(c % 4 + 1) * P], h[:, c * P:(c + 1) * P], self.ident[:, :])
                    last.then_inc(h_turned, 1)

                def down(i, s, e):
                    slot = e % RING
                    for c in range(HC):
                        if c % (HC // 2) == 0:
                            pe.wait_ge(hT_ready, i * 2 + (1 + c // (HC // 2)))
                            pe.sem_inc(self.gate, 1)
                        last = products(psY[s][:, 0:D], [x[:, c * P:(c + 1) * P] for x in (hT_high, hT_low)], slot,
                                        W1E + c * D, D, c == 0, c == HC - 1)
                    last.then_inc(y_full, 1)

                pe.sem_inc(y_full, 1)
                turn_x(0, 0)
                up(0, expert(pe, 0))
                turn_x(0, 1)
                turn_h(0)
                with pe.Fori(0, MTILES // 2 - 1) as j:
                    i = j * 2
                    e = expert(pe, i + 1)
                    up(i + 1, e)
                    turn_x(j + 1, 0)
                    down(i, 0, expert(pe, i))
                    e_next = expert(pe, i + 2)
                    turn_h(i + 1)
                    up(i + 2, e_next)
                    turn_x(j + 1, 1)
                    down(i + 1, 1, e)
                    turn_h(i + 2)
                up(MTILES - 1, expert(pe, MTILES - 1))
                down(MTILES - 2, 0, expert(pe, MTILES - 2))
                turn_h(MTILES - 1)
                down(MTILES - 1, 1, expert(pe, MTILES - 1))

            @block.vector
            def _(dve):
                def take_x(i):
                    e = expert(dve, i) if affine else None
                    dve.wait_ge(x_turned, i + 1)
                    if affine:
                        dve.sem_inc(self.gate, 1)
                    if affine:
                        for k in range(KD):
                            nc.vector.tensor_scalar(xT[:, k * P:(k + 1) * P], psX[:, k * P:(k + 1) * P], lng[:, bass.ds(e * KD + k, 1)],
                                                    lnb[:, bass.ds(e * KD + k, 1)], ALU.mult, ALU.add).then_inc(x_step, 1)
                        dve.wait_ge(x_step, i * 3 + 2)
                        dve.sem_inc(self.gate, 1)
                    whole = xT if affine else psX[:, 0:D]
                    nc.vector.tensor_copy(xT_high, whole).then_inc(x_step, 1)
                    dve.wait_ge(x_step, i * x_steps + x_steps)
                    nc.vector.tensor_tensor(xT_low, whole, xT_high, ALU.subtract).then_inc(xT_ready, 1)

                def take_low(i):
                    for b in range(2):
                        dve.wait_ge(g_ready, i * 2 + (b + 1))
                        nc.vector.tensor_tensor(hT_low[:, b * 512:(b + 1) * 512], hT[:, b * 512:(b + 1) * 512],
                                                hT_high[:, b * 512:(b + 1) * 512], ALU.subtract).then_inc(hT_ready, 1)

                def take_h(i, j, s):
                    dve.wait_ge(hbias_in[s], j * 16 + 16)
                    dve.sem_inc(self.gate, 1)
                    dve.wait_ge(h_full, i + 1)
                    for b in range(HB):
                        last = nc.vector.tensor_tensor(h[:, b * 512:(b + 1) * 512], psH[b][:, :], brow[s][:, b * 512:(b + 1) * 512], ALU.add)
                    last.then_inc(h_ready, 1)

                def take_y(i, j, s):
                    if later(j):
                        dve.wait_ge(y_stored[s], j * 16)
                        dve.sem_inc(self.gate, 1)
                    dve.wait_ge(ybias_in[s], j * 16 + 16)
                    dve.sem_inc(self.gate, 1)
                    dve.wait_ge(y_full, i + 2)
                    nc.vector.tensor_tensor(yout[s][:, 0:D], psY[s][:, 0:D], brow[s][:, H:H + D], ALU.add).then_inc(y_ready[s], 1)

                def pair(j):
                    i = j * 2
                    take_h(i + 1, j, 1)
                    take_x(i + 2)
                    take_y(i, j, 0)
                    take_low(i + 1)
                    take_h(i + 2, j + 1, 0)
                    take_x(i + 3)
                    take_y(i + 1, j, 1)
                    take_low(i + 2)

                if affine:
                    dve.wait_ge(ln_loaded, 32)
                take_x(0)
                take_h(0, 0, 0)
                take_x(1)
                take_low(0)
                pair(0)
                with dve.Fori(1, MTILES // 2 - 1) as j:
                    pair(j)
                take_h(MTILES - 1, MTILES // 2 - 1, 1)
                take_y(MTILES - 2, MTILES // 2 - 1, 0)
                take_low(MTILES - 1)
                take_y(MTILES - 1, MTILES // 2 - 1, 1)

            @block.scalar
            def _(act):
                def take_g(i, first=False):
                    act.wait_ge(h_turned, i + 1)
                    for b in range(2):
                        if not first and b == 0:
                            act.sem_inc(self.gate, 1)
                            act.wait_ge(y_full, i + 1)
                        nc.scalar.activation(hT[:, b * 512:(b + 1) * 512], psG[b][:, :], func)
                        nc.scalar.activation(hT_high[:, b * 512:(b + 1) * 512], psG[b][:, :], func).then_inc(g_ready, 1)

                def fetch_x(i, s):
                    if later(i) and not (isinstance(i, int) and i < 2):
                        act.wait_ge(x_turned, i - 1)
                        act.sem_inc(self.gate, 1)
                    act.dma_start(xin[s][:, 0:D], self.xd[bass.ds(i * P, P), :]).then_inc(x_in[s], 16)

                for i in range(3):
                    fetch_x(i, i % 2)
                take_g(0, True)
                fetch_x(3, 1)
                take_g(1)
                with act.Fori(1, MTILES // 2 - 1) as j:
                    for s in range(2):
                        i = j * 2 + s
                        fetch_x(i + 2, s)
                        take_g(i)
                for s in range(2):
                    take_g(MTILES - 2 + s)

    def combine_and_store(self):
        nc = self.nc
        with self.stage_block() as (block, sem):
            added, stored = sem("added", "stored")
            fetched, before = [g.sem for g in self.gathered], [g.base for g in self.gathered]
            for g in self.gathered:
                g.base += 16 * TOPK * TILES // GSLOTS

            @block.gpsimd
            def _(pool):
                for n in range(TOPK * TILES):
                    s, c = n % GSLOTS, n % TOPK * TILES + n // TOPK
                    if n >= GSLOTS:
                        pool.wait_ge(added, n - GSLOTS + 1)
                    nc.gpsimd.indirect_dma_start(self.rowbuf[s][:, 0:D], None, self.yd,
                                                 bass.IndirectOffsetOnAxis(ap=self.spos[:, c:c + 1], axis=0)).then_inc(fetched[s], 16)

            @block.vector
            def _(dve):
                for n in range(TOPK * TILES):
                    s, t, c = n % GSLOTS, n // TOPK, n % TOPK * TILES + n // TOPK
                    dve.wait_ge(fetched[s], before[s] + 16 * (n // GSLOTS + 1))
                    if n % TOPK:
                        dve.wait_ge(added, n)
                    x = self.x[:, t * D:(t + 1) * D]
                    nc.vector.scalar_tensor_tensor(out=x, in0=self.rowbuf[s][:, 0:D], scalar=self.wcomb[:, c:c + 1], in1=x,
                                                   op0=ALU.mult, op1=ALU.add).then_inc(added, 1)

            @block.sync
            def _(sp):
                ends = list(range(0, TILES - 1, 4)) + [TILES - 1]
                for t0, t1 in zip(ends, ends[1:]):
                    sp.wait_ge(added, TOPK * t1)
                    sp.dma_start(self.out[t0 * P:t1 * P, :].rearrange("(t p) d -> p t d", p=P),
                                 self.x[:, t0 * D:t1 * D].rearrange("p (t d) -> p t d", d=D)).then_inc(stored, 16)
                sp.wait_ge(added, TOPK * TILES)
                sp.dma_start(self.out[(TILES - 1) * P:NODES, :], self.x[0:LAST, (TILES - 1) * D:TILES * D]).then_inc(stored, 16)
                sp.wait_ge(stored, 16 * len(ends))


def kernel(**inputs):
    import numpy as np
    import concourse.bacc as bacc
    from concourse.bass_utils import run_bass_kernel_spmd

    given = {k: np.asarray(v) for k, v in inputs.items()}
    arrays = {k: given[k] for k in (
        "x", "src", "dst", "edge_type_8", "L0_gnn_W1", "L0_gnn_self_w1", "L0_gnn_b1", "L0_gnn_W2", "L0_gnn_self_w2",
        "L0_gnn_b2", "L0_ffn_bg", "L1_gnn_W1", "L1_gnn_b1", "L1_gnn_W2", "L1_gnn_b2", "L1_gnn_W3", "L1_gnn_b3",
        "L1_gnn_Wp", "L1_gnn_bp", "L1_ffn_Wr", "L1_ffn_br")}
    arrays["L0_ffn_WgT"] = given["L0_ffn_Wg"].T
    arrays["L0_ffn_W1t"] = given["L0_ffn_W1"].transpose(0, 2, 1)
    arrays["L0_ffn_W2t"] = given["L0_ffn_W2"].transpose(0, 2, 1)
    arrays["L1_ffn_W1t"] = given["L1_ffn_W1"]
    arrays["L1_ffn_W2t"] = given["L1_ffn_W2"]
    for m in range(2):
        arrays[f"L{m}_ffn_b12"] = np.concatenate([given[f"L{m}_ffn_b1"], given[f"L{m}_ffn_b2"]], axis=1)
    for k, name in (("g", "L1_ffn_ln_g"), ("b", "L1_ffn_ln_b")):
        arrays[f"L1_ffn_ln{k}T"] = given[name].reshape(E, KD, P).transpose(2, 0, 1).reshape(P, E * KD)
    arrays = {k: np.ascontiguousarray(v) for k, v in arrays.items()}
    nc = bacc.Bacc("TRN2", target_bir_lowering=False, num_devices=1)
    a = {k: nc.dram_tensor(f"in_{k}", v.shape, mybir.dt.from_np(v.dtype), kind="ExternalInput").ap() for k, v in arrays.items()}
    out = nc.dram_tensor("out", (NODES, D), F32, kind="ExternalOutput").ap()
    build(nc, a, out)
    r = run_bass_kernel_spmd(nc, [{f"in_{k}": v for k, v in arrays.items()}], core_ids=[0])
    return r.results[0]["out"]
```
